# Optimizing a Trainium2 kernel written in Bass

```python
import numpy as np
import jax
import jax.numpy as jnp

def _softmax(x, axis=-1):
    return jax.nn.softmax(x, axis=axis)

def _gelu(x):
    return jax.nn.gelu(x, approximate=True)

def _silu(x):
    return jax.nn.silu(x)

def _sigmoid(x):
    return jax.nn.sigmoid(x)

def _layernorm(x, axis=-1, eps=1e-05):
    m = jnp.mean(x, axis=axis, keepdims=True)
    v = jnp.var(x, axis=axis, keepdims=True)
    return (x - m) / jnp.sqrt(v + eps)

def _scatter_add(tgt, idx, src, axis=0):
    return tgt.at[idx].add(src)

def _segment_sum(src, seg, n):
    return jax.ops.segment_sum(src, seg, n)
kernel_name = 'mk_decoder_postln_d2_seqx_r8_72f971'

def setup_inputs(seed: int=0):
    np.random.seed(seed)
    _w = jnp.asarray

    def _rec_inputs():
        import jax
        import jax.numpy as jnp
        _rk = jax.random.key(seed)
        x = -0.0002928 + 1 * jax.random.normal(jax.random.fold_in(_rk, 1), (8, 256, 128), jnp.float32)
        _lenS = 256 - jax.random.randint(jax.random.fold_in(_rk, 7), (8,), 0, max(1, 256 // 4) + 1, jnp.int32)
        _lenS2 = 256 - jax.random.randint(jax.random.fold_in(_rk, 8), (8,), 0, max(1, 256 // 4) + 1, jnp.int32)
        _ctx_1024P = jax.random.normal(jax.random.fold_in(_rk, 11), (8, 16, 128), jnp.float32)
        _ctx_1024c = jax.random.dirichlet(jax.random.fold_in(_rk, 511), 0.3 * jnp.ones((16,), jnp.float32), (8, 256))
        _ctx_1024t = jnp.einsum('bsk,bkd->bsd', _ctx_1024c, _ctx_1024P)
        _ctx_1024t = _ctx_1024t * jax.lax.rsqrt(jnp.mean(jnp.square(_ctx_1024t)) + 1e-12) * 0.953939
        ctx_1024 = -1.39393e-06 + 0.999914 * (_ctx_1024t + 0.3 * jax.random.normal(jax.random.fold_in(_rk, 611), (8, 256, 128), jnp.float32))
        return (x, ctx_1024)
    x, ctx_1024 = _rec_inputs()

    def _L0_attn_setup():
        import jax, jax.numpy as jnp
        import numpy as np
        NUM_HEADS = 16
        LORA_SCALE = 32.0 / 8.0
        ROPE_BASE = 10000.0

        def make_sincos(seq_len, dim):
            pos = jnp.arange(seq_len, dtype=jnp.float32)
            i = jnp.arange(0, dim, 2, dtype=jnp.float32) / dim
            theta = pos[:, None] / ROPE_BASE ** i[None, :]
            return (jnp.sin(theta), jnp.cos(theta))

        def apply_rope(x, sin, cos):
            x_even = x[..., 0::2]
            x_odd = x[..., 1::2]
            rot_even = x_even * cos - x_odd * sin
            rot_odd = x_even * sin + x_odd * cos
            return jnp.stack([rot_even, rot_odd], axis=-1).reshape(x.shape)
        key = jax.random.key(seed)
        ks = jax.random.split(key, 9)
        B, T, D, R = (4, 256, 128, 8)
        s = 1.0 / np.sqrt(D)
        return {'query': jax.random.normal(ks[0], (B, T, D), dtype=jnp.float32), 'wq': jax.random.normal(ks[1], (D, D), dtype=jnp.float32) * s, 'wk': jax.random.normal(ks[2], (D, D), dtype=jnp.float32) * s, 'wv': jax.random.normal(ks[3], (D, D), dtype=jnp.float32) * s, 'wo': jax.random.normal(ks[4], (D, D), dtype=jnp.float32) * s, 'Aq': jax.random.normal(ks[5], (D, R), dtype=jnp.float32) * s, 'Bq': jax.random.normal(ks[6], (R, D), dtype=jnp.float32) * 0.01, 'Av': jax.random.normal(ks[7], (D, R), dtype=jnp.float32) * s, 'Bv': jax.random.normal(ks[8], (R, D), dtype=jnp.float32) * 0.01}
    _L0_attn_all = _L0_attn_setup()
    _L0_attn_in = {k: v for k, v in _L0_attn_all.items() if k in ('wq', 'wk', 'wv', 'wo', 'Aq', 'Bq', 'Av', 'Bv')}
    del _L0_attn_all

    def _L0_xattn_setup():
        import jax, jax.numpy as jnp
        import numpy as np
        D_MODEL = 128
        N_HEADS = 16
        D_K = D_MODEL // N_HEADS

        def _mha(Q, K, V, W_Q, b_Q, W_K, b_K, W_V, b_V, W_O, b_O):
            B, S, _ = Q.shape

            def proj(x, W, b):
                y = jnp.einsum('bsd,de->bse', x, W) + b
                return y.reshape(B, S, N_HEADS, D_K).transpose(0, 2, 1, 3)
            q = proj(Q, W_Q, b_Q)
            k = proj(K, W_K, b_K)
            v = proj(V, W_V, b_V)
            scores = jnp.einsum('bhqd,bhkd->bhqk', q, k) / jnp.sqrt(jnp.float32(D_K))
            attn = jax.nn.softmax(scores, axis=-1)
            out = jnp.einsum('bhqk,bhkd->bhqd', attn, v)
            out = out.transpose(0, 2, 1, 3).reshape(B, S, D_MODEL)
            return jnp.einsum('bsd,de->bse', out, W_O) + b_O
        key = jax.random.key(seed)
        ks = jax.random.split(key, 11)
        B, S = (2, 256)
        scale = 1.0 / np.sqrt(D_MODEL)
        inp = {'Q': jax.random.normal(ks[0], (B, S, D_MODEL), jnp.float32), 'K': jax.random.normal(ks[1], (B, S, D_MODEL), jnp.float32), 'V': jax.random.normal(ks[2], (B, S, D_MODEL), jnp.float32), 'W_Q': jax.random.normal(ks[3], (D_MODEL, D_MODEL), jnp.float32) * scale, 'b_Q': jnp.zeros((D_MODEL,), jnp.float32), 'W_K': jax.random.normal(ks[4], (D_MODEL, D_MODEL), jnp.float32) * scale, 'b_K': jnp.zeros((D_MODEL,), jnp.float32), 'W_V': jax.random.normal(ks[5], (D_MODEL, D_MODEL), jnp.float32) * scale, 'b_V': jnp.zeros((D_MODEL,), jnp.float32), 'W_O': jax.random.normal(ks[6], (D_MODEL, D_MODEL), jnp.float32) * scale, 'b_O': jnp.zeros((D_MODEL,), jnp.float32)}
        return inp
    _L0_xattn_all = _L0_xattn_setup()
    _L0_xattn_in = {k: v for k, v in _L0_xattn_all.items() if k in ('W_Q', 'b_Q', 'W_K', 'b_K', 'W_V', 'b_V', 'W_O', 'b_O')}
    del _L0_xattn_all

    def _L0_ffn_setup():
        import jax, jax.numpy as jnp
        import numpy as np
        B, S, IN, OUT = (4, 1024, 128, 128)
        EPS = 1e-06

        def _xla_quantized_matmul(x2d, weight_q, weight_scale):
            amax = jnp.max(jnp.abs(x2d), axis=-1, keepdims=True)
            x_scale = jnp.maximum(amax, EPS) / 127.0
            x_q = jnp.clip(jnp.round(x2d / x_scale), -128, 127).astype(jnp.int8)
            acc = jax.lax.dot_general(x_q, weight_q, (((1,), (1,)), ((), ())), preferred_element_type=jnp.int32)
            return acc.astype(jnp.float32) * x_scale * weight_scale[None, :]
        key = jax.random.key(seed)
        k1, k2, k3, k4 = jax.random.split(key, 4)
        x = jax.random.normal(k1, (B, S, IN), dtype=jnp.float32)
        weight_q = jax.random.randint(k2, (OUT, IN), -128, 128, dtype=jnp.int32).astype(jnp.int8)
        weight_scale = jax.random.uniform(k3, (OUT,), dtype=jnp.float32, minval=0.001, maxval=0.01)
        bias = jax.random.normal(k4, (OUT,), dtype=jnp.float32) * 0.01
        return {'x': x, 'weight_q': weight_q, 'weight_scale': weight_scale, 'bias': bias}
    _L0_ffn_all = _L0_ffn_setup()
    _L0_ffn_in = {k: v for k, v in _L0_ffn_all.items() if k in ('weight_q', 'weight_scale', 'bias')}
    del _L0_ffn_all

    def _L1_attn_setup():
        import jax, jax.numpy as jnp
        import numpy as np
        NH, DK, DV, CHUNK = (4, 32, 32, 32)
        HID = 128
        FLOOR = 0.05
        EPS = 1e-05

        def _l2norm(x):
            return x * jax.lax.rsqrt(jnp.sum(x * x, -1, keepdims=True) + 1e-06)

        def _causal_dw_conv(x, w):
            K = w.shape[-1]
            y = jax.lax.conv_general_dilated(jnp.swapaxes(x, 1, 2), w[:, None, :], (1,), [(K - 1, 0)], dimension_numbers=('NCH', 'OIH', 'NCH'), feature_group_count=w.shape[0])
            return jnp.swapaxes(y, 1, 2)

        def _fir(x, w):
            B, L, H, D = x.shape
            return _causal_dw_conv(x.reshape(B, L, H * D), w.reshape(H * D, -1)).reshape(B, L, H, D)

        def _stats(x):
            mean = jnp.mean(x, -1, keepdims=True)
            var = jnp.var(x, -1, keepdims=True)
            am = jnp.mean(jnp.abs(x), -1, keepdims=True)
            l2 = jnp.linalg.norm(x, axis=-1, keepdims=True)
            return jnp.concatenate([mean, var, am, l2], -1)

        def _delta_rule(q, k, v, beta, c=CHUNK):
            b, h, L, dk = q.shape
            dv = v.shape[-1]
            q = _l2norm(q)
            k = _l2norm(k)
            v = v * beta[..., None]
            kb = k * beta[..., None]
            n = L // c
            rs = lambda t: t.reshape(b, h, n, c, -1)
            q, k, v, kb = (rs(q), rs(k), rs(v), rs(kb))
            strict_low = jnp.tril(jnp.ones((c, c), bool), -1)
            attn = -(kb @ jnp.swapaxes(k, -1, -2)) * strict_low
            col = jnp.arange(c)

            def row_body(i, a):
                upd = jnp.einsum('...k,...kj->...j', a[..., i, :], a)
                return a.at[..., i, :].add(jnp.where(col < i, upd, 0.0))
            attn_inv = jax.lax.fori_loop(1, c, row_body, attn) + jnp.eye(c, dtype=attn.dtype)
            u = attn_inv @ v
            w = attn_inv @ kb
            incl_low = jnp.tril(jnp.ones((c, c), bool))

            def step(S, xs):
                q_i, k_i, u_i, w_i = xs
                attn_loc = jnp.einsum('bhid,bhjd->bhij', q_i, k_i) * incl_low
                u_i = u_i - w_i @ S
                o_i = q_i @ S + attn_loc @ u_i
                return (S + jnp.swapaxes(k_i, -1, -2) @ u_i, o_i)
            mv = lambda t: jnp.moveaxis(t, 2, 0)
            S0 = jnp.zeros((b, h, dk, dv), q.dtype)
            S, o = jax.lax.scan(step, S0, (mv(q), mv(k), mv(u), mv(w)))
            return (jnp.moveaxis(o, 0, 2).reshape(b, h, L, dv), S)
        key = jax.random.key(seed)
        ks = jax.random.split(key, 16)
        B, L = (2, 512)
        s = 0.02
        hs = jax.random.normal(ks[0], (B, L, HID), jnp.float32)
        Wq = jax.random.normal(ks[1], (HID, NH * DK)) * s
        Wk = jax.random.normal(ks[2], (HID, NH * DK)) * s
        Wv = jax.random.normal(ks[3], (HID, NH * DV)) * s
        Wb = jax.random.normal(ks[4], (HID, NH)) * s
        conv_q_w = jax.random.normal(ks[5], (NH * DK, 4)) * 0.1
        conv_k_w = jax.random.normal(ks[6], (NH * DK, 4)) * 0.1
        conv_v_w = jax.random.normal(ks[7], (NH * DV, 4)) * 0.1
        fir_short_w = jnp.zeros((NH, DV, 5)).at[..., -1].set(1.0) + jax.random.normal(ks[8], (NH, DV, 5)) * 0.02
        fir_long_w = jnp.zeros((NH, DV, 64)).at[..., -1].set(1.0) + jax.random.normal(ks[9], (NH, DV, 64)) * 0.02
        gin, hg = (HID + 16, HID * 2 // 2)
        mlp_w1 = jax.random.normal(ks[10], (gin, hg)) * s
        mlp_b1 = jnp.zeros((hg,), jnp.float32)
        mlp_w2 = jax.random.normal(ks[11], (hg, 4)) * s
        mlp_b2 = jnp.array([-0.5, -0.5, 0.5, 1.5], jnp.float32)
        log_temp = jnp.zeros((NH, 1), jnp.float32)
        o_norm_w = jnp.ones((DV,), jnp.float32)
        Wo = jax.random.normal(ks[12], (NH * DV, HID)) * s
        return dict(hidden_states=hs, Wq=Wq, Wk=Wk, Wv=Wv, Wb=Wb, conv_q_w=conv_q_w, conv_k_w=conv_k_w, conv_v_w=conv_v_w, fir_short_w=fir_short_w, fir_long_w=fir_long_w, mlp_w1=mlp_w1, mlp_b1=mlp_b1, mlp_w2=mlp_w2, mlp_b2=mlp_b2, log_temp=log_temp, o_norm_w=o_norm_w, Wo=Wo)
    _L1_attn_all = _L1_attn_setup()
    _L1_attn_in = {k: v for k, v in _L1_attn_all.items() if k in ('Wq', 'Wk', 'Wv', 'Wb', 'conv_q_w', 'conv_k_w', 'conv_v_w', 'fir_short_w', 'fir_long_w', 'mlp_w1', 'mlp_b1', 'mlp_w2', 'mlp_b2', 'log_temp', 'o_norm_w', 'Wo')}
    del _L1_attn_all

    def _L1_xattn_setup():
        import jax, jax.numpy as jnp
        import numpy as np
        D_MODEL = 128
        H = 16
        D_K = D_MODEL // H
        CAUSAL = True
        NEG_INF = float('-inf')
        key = jax.random.key(seed)
        ks = jax.random.split(key, 11)
        B, S = (4, 256)
        scale = 1.0 / np.sqrt(D_MODEL)
        inp = {'query': jax.random.normal(ks[0], (B, S, D_MODEL), dtype=jnp.float32), 'value': jax.random.normal(ks[1], (B, S, D_MODEL), dtype=jnp.float32), 'key': jax.random.normal(ks[2], (B, S, D_MODEL), dtype=jnp.float32), 'Wq': jax.random.normal(ks[3], (D_MODEL, D_MODEL), dtype=jnp.float32) * scale, 'bq': jnp.zeros((D_MODEL,), dtype=jnp.float32), 'Wk': jax.random.normal(ks[4], (D_MODEL, D_MODEL), dtype=jnp.float32) * scale, 'bk': jnp.zeros((D_MODEL,), dtype=jnp.float32), 'Wv': jax.random.normal(ks[5], (D_MODEL, D_MODEL), dtype=jnp.float32) * scale, 'bv': jnp.zeros((D_MODEL,), dtype=jnp.float32), 'Wo': jax.random.normal(ks[6], (D_MODEL, D_MODEL), dtype=jnp.float32) * scale, 'bo': jnp.zeros((D_MODEL,), dtype=jnp.float32)}
        return inp
    _L1_xattn_all = _L1_xattn_setup()
    _L1_xattn_in = {k: v for k, v in _L1_xattn_all.items() if k in ('Wq', 'bq', 'Wk', 'bk', 'Wv', 'bv', 'Wo', 'bo')}
    del _L1_xattn_all

    def _L1_ffn_setup():
        import jax, jax.numpy as jnp
        import numpy as np
        D_MODEL, EXPERT_DIM, NUM_EXPERTS, TOP_K = (128, 256, 16, 2)
        SEQ_LEN, BATCH = (256, 2)
        key = jax.random.key(seed)
        ks = jax.random.split(key, 8)
        s_d = 1.0 / np.sqrt(D_MODEL)
        s_h = 1.0 / np.sqrt(EXPERT_DIM)
        return {'x': jax.random.normal(ks[0], (SEQ_LEN, BATCH, D_MODEL), jnp.float32), 'Wg': jax.random.uniform(ks[1], (D_MODEL, NUM_EXPERTS), jnp.float32, -s_d, s_d), 'bg': jax.random.uniform(ks[2], (NUM_EXPERTS,), jnp.float32, -s_d, s_d), 'bias': jnp.zeros((NUM_EXPERTS,), jnp.float32), 'W1': jax.random.uniform(ks[3], (NUM_EXPERTS, D_MODEL, EXPERT_DIM), jnp.float32, -s_d, s_d), 'b1': jax.random.uniform(ks[4], (NUM_EXPERTS, EXPERT_DIM), jnp.float32, -s_d, s_d), 'W2': jax.random.uniform(ks[5], (NUM_EXPERTS, EXPERT_DIM, D_MODEL), jnp.float32, -s_h, s_h), 'b2': jax.random.uniform(ks[6], (NUM_EXPERTS, D_MODEL), jnp.float32, -s_h, s_h)}
    _L1_ffn_all = _L1_ffn_setup()
    _L1_ffn_in = {k: v for k, v in _L1_ffn_all.items() if k in ('Wg', 'bg', 'bias', 'W1', 'b1', 'W2', 'b2')}
    del _L1_ffn_all
    return {'x': x, 'ctx_1024': ctx_1024, 'L0_attn_wq': _L0_attn_in['wq'], 'L0_attn_wk': _L0_attn_in['wk'], 'L0_attn_wv': _L0_attn_in['wv'], 'L0_attn_wo': _L0_attn_in['wo'], 'L0_attn_Aq': _L0_attn_in['Aq'], 'L0_attn_Bq': _L0_attn_in['Bq'], 'L0_attn_Av': _L0_attn_in['Av'], 'L0_attn_Bv': _L0_attn_in['Bv'], 'L0_xattn_W_Q': _L0_xattn_in['W_Q'], 'L0_xattn_b_Q': _L0_xattn_in['b_Q'], 'L0_xattn_W_K': _L0_xattn_in['W_K'], 'L0_xattn_b_K': _L0_xattn_in['b_K'], 'L0_xattn_W_V': _L0_xattn_in['W_V'], 'L0_xattn_b_V': _L0_xattn_in['b_V'], 'L0_xattn_W_O': _L0_xattn_in['W_O'], 'L0_xattn_b_O': _L0_xattn_in['b_O'], 'L0_ffn_weight_q': _L0_ffn_in['weight_q'], 'L0_ffn_weight_scale': _L0_ffn_in['weight_scale'], 'L0_ffn_bias': _L0_ffn_in['bias'], 'L1_attn_Wq': _L1_attn_in['Wq'], 'L1_attn_Wk': _L1_attn_in['Wk'], 'L1_attn_Wv': _L1_attn_in['Wv'], 'L1_attn_Wb': _L1_attn_in['Wb'], 'L1_attn_conv_q_w': _L1_attn_in['conv_q_w'], 'L1_attn_conv_k_w': _L1_attn_in['conv_k_w'], 'L1_attn_conv_v_w': _L1_attn_in['conv_v_w'], 'L1_attn_fir_short_w': _L1_attn_in['fir_short_w'], 'L1_attn_fir_long_w': _L1_attn_in['fir_long_w'], 'L1_attn_mlp_w1': _L1_attn_in['mlp_w1'], 'L1_attn_mlp_b1': _L1_attn_in['mlp_b1'], 'L1_attn_mlp_w2': _L1_attn_in['mlp_w2'], 'L1_attn_mlp_b2': _L1_attn_in['mlp_b2'], 'L1_attn_log_temp': _L1_attn_in['log_temp'], 'L1_attn_o_norm_w': _L1_attn_in['o_norm_w'], 'L1_attn_Wo': _L1_attn_in['Wo'], 'L1_xattn_Wq': _L1_xattn_in['Wq'], 'L1_xattn_bq': _L1_xattn_in['bq'], 'L1_xattn_Wk': _L1_xattn_in['Wk'], 'L1_xattn_bk': _L1_xattn_in['bk'], 'L1_xattn_Wv': _L1_xattn_in['Wv'], 'L1_xattn_bv': _L1_xattn_in['bv'], 'L1_xattn_Wo': _L1_xattn_in['Wo'], 'L1_xattn_bo': _L1_xattn_in['bo'], 'L1_ffn_Wg': _L1_ffn_in['Wg'], 'L1_ffn_bg': _L1_ffn_in['bg'], 'L1_ffn_bias': _L1_ffn_in['bias'], 'L1_ffn_W1': _L1_ffn_in['W1'], 'L1_ffn_b1': _L1_ffn_in['b1'], 'L1_ffn_W2': _L1_ffn_in['W2'], 'L1_ffn_b2': _L1_ffn_in['b2']}

def reference(x, ctx_1024, L0_attn_wq, L0_attn_wk, L0_attn_wv, L0_attn_wo, L0_attn_Aq, L0_attn_Bq, L0_attn_Av, L0_attn_Bv, L0_xattn_W_Q, L0_xattn_b_Q, L0_xattn_W_K, L0_xattn_b_K, L0_xattn_W_V, L0_xattn_b_V, L0_xattn_W_O, L0_xattn_b_O, L0_ffn_weight_q, L0_ffn_weight_scale, L0_ffn_bias, L1_attn_Wq, L1_attn_Wk, L1_attn_Wv, L1_attn_Wb, L1_attn_conv_q_w, L1_attn_conv_k_w, L1_attn_conv_v_w, L1_attn_fir_short_w, L1_attn_fir_long_w, L1_attn_mlp_w1, L1_attn_mlp_b1, L1_attn_mlp_w2, L1_attn_mlp_b2, L1_attn_log_temp, L1_attn_o_norm_w, L1_attn_Wo, L1_xattn_Wq, L1_xattn_bq, L1_xattn_Wk, L1_xattn_bk, L1_xattn_Wv, L1_xattn_bv, L1_xattn_Wo, L1_xattn_bo, L1_ffn_Wg, L1_ffn_bg, L1_ffn_bias, L1_ffn_W1, L1_ffn_b1, L1_ffn_W2, L1_ffn_b2):
    import jax
    import jax.numpy as jnp

    def _L0_attn_ref(query, wq, wk, wv, wo, Aq, Bq, Av, Bv):
        import jax, jax.numpy as jnp
        import numpy as np
        NUM_HEADS = 16
        LORA_SCALE = 32.0 / 8.0
        ROPE_BASE = 10000.0

        def make_sincos(seq_len, dim):
            pos = jnp.arange(seq_len, dtype=jnp.float32)
            i = jnp.arange(0, dim, 2, dtype=jnp.float32) / dim
            theta = pos[:, None] / ROPE_BASE ** i[None, :]
            return (jnp.sin(theta), jnp.cos(theta))

        def apply_rope(x, sin, cos):
            x_even = x[..., 0::2]
            x_odd = x[..., 1::2]
            rot_even = x_even * cos - x_odd * sin
            rot_odd = x_even * sin + x_odd * cos
            return jnp.stack([rot_even, rot_odd], axis=-1).reshape(x.shape)
        B, T, D = query.shape
        H = NUM_HEADS
        dh = D // H
        q = query @ wq + query @ Aq @ Bq * LORA_SCALE
        k = query @ wk
        v = query @ wv + query @ Av @ Bv * LORA_SCALE

        def split(x):
            return x.reshape(B, T, H, dh).transpose(0, 2, 1, 3)
        q, k, v = (split(q), split(k), split(v))
        sin, cos = make_sincos(T, dh)
        q = apply_rope(q, sin, cos)
        k = apply_rope(k, sin, cos)
        scores = jnp.einsum('bhqd,bhkd->bhqk', q, k) / jnp.sqrt(jnp.float32(dh))
        causal = jnp.triu(jnp.ones((T, T), dtype=bool), k=1)
        scores = jnp.where(causal[None, None], jnp.float32(-1000000000.0), scores)
        attn = jax.nn.softmax(scores, axis=-1)
        out = jnp.einsum('bhqk,bhkd->bhqd', attn, v)
        out = out.transpose(0, 2, 1, 3).reshape(B, T, D)
        return out @ wo

    def _L0_xattn_ref(Q, K, V, W_Q, b_Q, W_K, b_K, W_V, b_V, W_O, b_O):
        import jax, jax.numpy as jnp
        import numpy as np
        D_MODEL = 128
        N_HEADS = 16
        D_K = D_MODEL // N_HEADS

        def _mha(Q, K, V, W_Q, b_Q, W_K, b_K, W_V, b_V, W_O, b_O):
            B, S, _ = Q.shape

            def proj(x, W, b):
                y = jnp.einsum('bsd,de->bse', x, W) + b
                return y.reshape(B, S, N_HEADS, D_K).transpose(0, 2, 1, 3)
            q = proj(Q, W_Q, b_Q)
            k = proj(K, W_K, b_K)
            v = proj(V, W_V, b_V)
            scores = jnp.einsum('bhqd,bhkd->bhqk', q, k) / jnp.sqrt(jnp.float32(D_K))
            attn = jax.nn.softmax(scores, axis=-1)
            out = jnp.einsum('bhqk,bhkd->bhqd', attn, v)
            out = out.transpose(0, 2, 1, 3).reshape(B, S, D_MODEL)
            return jnp.einsum('bsd,de->bse', out, W_O) + b_O
        return _mha(Q, K, V, W_Q, b_Q, W_K, b_K, W_V, b_V, W_O, b_O)

    def _L0_ffn_ref(x, weight_q, weight_scale, bias):
        import jax, jax.numpy as jnp
        import numpy as np
        B, S, IN, OUT = (4, 1024, 128, 128)
        EPS = 1e-06

        def _xla_quantized_matmul(x2d, weight_q, weight_scale):
            amax = jnp.max(jnp.abs(x2d), axis=-1, keepdims=True)
            x_scale = jnp.maximum(amax, EPS) / 127.0
            x_q = jnp.clip(jnp.round(x2d / x_scale), -128, 127).astype(jnp.int8)
            acc = jax.lax.dot_general(x_q, weight_q, (((1,), (1,)), ((), ())), preferred_element_type=jnp.int32)
            return acc.astype(jnp.float32) * x_scale * weight_scale[None, :]
        orig_shape = x.shape
        x2d = x.reshape(-1, orig_shape[-1])
        out = _xla_quantized_matmul(x2d, weight_q, weight_scale)
        out = out.reshape(*orig_shape[:-1], out.shape[-1])
        out = out + bias
        return out

    def _L1_attn_ref(hidden_states, Wq, Wk, Wv, Wb, conv_q_w, conv_k_w, conv_v_w, fir_short_w, fir_long_w, mlp_w1, mlp_b1, mlp_w2, mlp_b2, log_temp, o_norm_w, Wo):
        import jax, jax.numpy as jnp
        import numpy as np
        NH, DK, DV, CHUNK = (4, 32, 32, 32)
        HID = 128
        FLOOR = 0.05
        EPS = 1e-05

        def _l2norm(x):
            return x * jax.lax.rsqrt(jnp.sum(x * x, -1, keepdims=True) + 1e-06)

        def _causal_dw_conv(x, w):
            K = w.shape[-1]
            y = jax.lax.conv_general_dilated(jnp.swapaxes(x, 1, 2), w[:, None, :], (1,), [(K - 1, 0)], dimension_numbers=('NCH', 'OIH', 'NCH'), feature_group_count=w.shape[0])
            return jnp.swapaxes(y, 1, 2)

        def _fir(x, w):
            B, L, H, D = x.shape
            return _causal_dw_conv(x.reshape(B, L, H * D), w.reshape(H * D, -1)).reshape(B, L, H, D)

        def _stats(x):
            mean = jnp.mean(x, -1, keepdims=True)
            var = jnp.var(x, -1, keepdims=True)
            am = jnp.mean(jnp.abs(x), -1, keepdims=True)
            l2 = jnp.linalg.norm(x, axis=-1, keepdims=True)
            return jnp.concatenate([mean, var, am, l2], -1)

        def _delta_rule(q, k, v, beta, c=CHUNK):
            b, h, L, dk = q.shape
            dv = v.shape[-1]
            q = _l2norm(q)
            k = _l2norm(k)
            v = v * beta[..., None]
            kb = k * beta[..., None]
            n = L // c
            rs = lambda t: t.reshape(b, h, n, c, -1)
            q, k, v, kb = (rs(q), rs(k), rs(v), rs(kb))
            strict_low = jnp.tril(jnp.ones((c, c), bool), -1)
            attn = -(kb @ jnp.swapaxes(k, -1, -2)) * strict_low
            col = jnp.arange(c)

            def row_body(i, a):
                upd = jnp.einsum('...k,...kj->...j', a[..., i, :], a)
                return a.at[..., i, :].add(jnp.where(col < i, upd, 0.0))
            attn_inv = jax.lax.fori_loop(1, c, row_body, attn) + jnp.eye(c, dtype=attn.dtype)
            u = attn_inv @ v
            w = attn_inv @ kb
            incl_low = jnp.tril(jnp.ones((c, c), bool))

            def step(S, xs):
                q_i, k_i, u_i, w_i = xs
                attn_loc = jnp.einsum('bhid,bhjd->bhij', q_i, k_i) * incl_low
                u_i = u_i - w_i @ S
                o_i = q_i @ S + attn_loc @ u_i
                return (S + jnp.swapaxes(k_i, -1, -2) @ u_i, o_i)
            mv = lambda t: jnp.moveaxis(t, 2, 0)
            S0 = jnp.zeros((b, h, dk, dv), q.dtype)
            S, o = jax.lax.scan(step, S0, (mv(q), mv(k), mv(u), mv(w)))
            return (jnp.moveaxis(o, 0, 2).reshape(b, h, L, dv), S)
        B, L, _ = hidden_states.shape
        q = jax.nn.silu(_causal_dw_conv(hidden_states @ Wq, conv_q_w)).reshape(B, L, NH, DK)
        k = jax.nn.silu(_causal_dw_conv(hidden_states @ Wk, conv_k_w)).reshape(B, L, NH, DK)
        v_direct = jax.nn.silu(_causal_dw_conv(hidden_states @ Wv, conv_v_w)).reshape(B, L, NH, DV)
        beta = jax.nn.sigmoid(hidden_states @ Wb)
        bhld = lambda t: jnp.transpose(t, (0, 2, 1, 3))
        delta_bh, _ = _delta_rule(bhld(q), bhld(k), bhld(v_direct), jnp.transpose(beta, (0, 2, 1)))
        delta_out = jnp.transpose(delta_bh, (0, 2, 1, 3))
        local_short = _fir(v_direct, fir_short_w)
        local_long = _fir(v_direct, fir_long_w)
        stats_vec = jnp.concatenate([_stats(local_short), _stats(local_long), _stats(delta_out), _stats(v_direct)], -1)
        hs_exp = jnp.broadcast_to(hidden_states[:, :, None, :], (B, L, NH, HID))
        gate_in = jnp.concatenate([hs_exp, stats_vec], -1)
        h1 = jax.nn.gelu(gate_in @ mlp_w1 + mlp_b1, approximate=False)
        logits = h1 @ mlp_w2 + mlp_b2
        probs = jax.nn.softmax(logits / jnp.exp(log_temp), -1)
        probs = FLOOR + (1.0 - 4.0 * FLOOR) * probs
        o = probs[..., 0:1] * local_short + probs[..., 1:2] * local_long + probs[..., 2:3] * delta_out + probs[..., 3:4] * v_direct
        o = o * jax.lax.rsqrt(jnp.mean(o * o, -1, keepdims=True) + EPS) * o_norm_w
        return o.reshape(B, L, NH * DV) @ Wo

    def _L1_xattn_ref(query, value, key, Wq, bq, Wk, bk, Wv, bv, Wo, bo):
        import jax, jax.numpy as jnp
        import numpy as np
        D_MODEL = 128
        H = 16
        D_K = D_MODEL // H
        CAUSAL = True
        NEG_INF = float('-inf')
        B, S, _ = query.shape

        def proj(x, W, b):
            return (x @ W + b).reshape(B, -1, H, D_K).transpose(0, 2, 1, 3)
        q = proj(query, Wq, bq)
        k = proj(key, Wk, bk)
        v = proj(value, Wv, bv)
        scores = jnp.einsum('bhqd,bhkd->bhqk', q, k) / np.sqrt(D_K)
        if CAUSAL:
            causal_mask = jnp.triu(jnp.ones((S, S), dtype=bool), k=1)
            scores = jnp.where(causal_mask, NEG_INF, scores)
        attn = jax.nn.softmax(scores, axis=-1)
        out = jnp.einsum('bhqk,bhkd->bhqd', attn, v)
        out = out.transpose(0, 2, 1, 3).reshape(B, S, D_MODEL)
        return out @ Wo + bo

    def _L1_ffn_ref(x, Wg, bg, bias, W1, b1, W2, b2):
        import jax, jax.numpy as jnp
        import numpy as np
        D_MODEL, EXPERT_DIM, NUM_EXPERTS, TOP_K = (128, 256, 16, 2)
        SEQ_LEN, BATCH = (256, 2)
        logits = jnp.einsum('sbd,de->sbe', x, Wg) + bg + bias
        vals, idx = jax.lax.top_k(logits, TOP_K)
        w = jax.nn.softmax(vals - jnp.max(vals, axis=-1, keepdims=True), axis=-1)
        cw = jnp.einsum('sbk,sbke->sbe', w, jax.nn.one_hot(idx, NUM_EXPERTS, dtype=x.dtype))
        h = jax.nn.relu(jnp.einsum('sbd,edh->esbh', x, W1) + b1[:, None, None, :])
        y = jnp.einsum('esbh,ehd->esbd', h, W2) + b2[:, None, None, :]
        out = jnp.einsum('esbd,sbe->sbd', y, cw)
        return out
    x = _layernorm(x + _L0_attn_ref(x, L0_attn_wq, L0_attn_wk, L0_attn_wv, L0_attn_wo, L0_attn_Aq, L0_attn_Bq, L0_attn_Av, L0_attn_Bv), axis=-1)
    x = _layernorm(x + _L0_xattn_ref(x, ctx_1024, ctx_1024, L0_xattn_W_Q, L0_xattn_b_Q, L0_xattn_W_K, L0_xattn_b_K, L0_xattn_W_V, L0_xattn_b_V, L0_xattn_W_O, L0_xattn_b_O), axis=-1)
    x = _layernorm(x + _L0_ffn_ref(x, L0_ffn_weight_q, L0_ffn_weight_scale, L0_ffn_bias), axis=-1)
    x = _layernorm(x + _L1_attn_ref(x, L1_attn_Wq, L1_attn_Wk, L1_attn_Wv, L1_attn_Wb, L1_attn_conv_q_w, L1_attn_conv_k_w, L1_attn_conv_v_w, L1_attn_fir_short_w, L1_attn_fir_long_w, L1_attn_mlp_w1, L1_attn_mlp_b1, L1_attn_mlp_w2, L1_attn_mlp_b2, L1_attn_log_temp, L1_attn_o_norm_w, L1_attn_Wo), axis=-1)
    x = _layernorm(x + _L1_xattn_ref(x, ctx_1024, ctx_1024, L1_xattn_Wq, L1_xattn_bq, L1_xattn_Wk, L1_xattn_bk, L1_xattn_Wv, L1_xattn_bv, L1_xattn_Wo, L1_xattn_bo), axis=-1)
    x = _layernorm(x + _L1_ffn_ref(x, L1_ffn_Wg, L1_ffn_bg, L1_ffn_bias, L1_ffn_W1, L1_ffn_b1, L1_ffn_W2, L1_ffn_b2), axis=-1)
    return x

_drawn_inputs = setup_inputs


def setup_inputs(seed=0):
    import zlib

    import numpy as np

    out = dict(_drawn_inputs(seed))
    spreads = {'L0_xattn_b_Q': (0.0, 0.1),
     'L0_xattn_b_K': (0.0, 2.0),
     'L0_xattn_b_V': (0.0, 0.1),
     'L0_xattn_b_O': (0.0, 0.1),
     'L1_attn_mlp_b1': (0.0, 0.8),
     'L1_attn_log_temp': (0.0, 2.0),
     'L1_attn_o_norm_w': (1.0, 0.2),
     'L1_xattn_bq': (0.0, 0.1),
     'L1_xattn_bk': (0.0, 2.0),
     'L1_xattn_bv': (0.0, 0.1),
     'L1_xattn_bo': (0.0, 0.1),
     'L1_ffn_bias': (0.0, 0.1)}
    factors = {'L0_ffn_bias': 6.966,
     'L1_attn_Wb': 6.6,
     'L1_attn_mlp_w1': 8.0,
     'L1_attn_mlp_w2': 8.0,
     'L1_ffn_b1': 3.854,
     'L1_attn_fir_long_w': 2.871}
    for name, (base, spread) in spreads.items():
        noise = np.random.default_rng([zlib.crc32(name.encode()), seed]).standard_normal(out[name].shape)
        drawn = base * np.exp(spread * noise) if base else spread * noise
        out[name] = jnp.asarray(drawn.astype(out[name].dtype))
    for name, factor in factors.items():
        out[name] = (out[name] * factor).astype(out[name].dtype)
    return out
```

```python
from contextlib import ExitStack

import concourse.bass as bass
import numpy as np
from concourse import mybir

F32 = mybir.dt.float32
BF16 = mybir.dt.bfloat16
I32 = mybir.dt.int32
ACT = mybir.ActivationFunctionType
ALU = mybir.AluOpType
AX = mybir.AxisListType

P = 128
B, S = 8, 256
GB = 2
G = B // GB
T = GB * S
NT = T // P
H, DH = 16, 8
HP, HG = 2, 8
SLOTS = 6
VW = DH + 1
SCALE = 1.0 / float(np.sqrt(DH))
LN_EPS = 1e-5
LORA_SCALE = 4.0
MASKED = -1e30

COLS = [
    ("ident", P), ("rope_c", S), ("rope_s", S), 
    ("L0_q", P), ("L0_qs", P), ("L0_k", P), ("L0_ks", P), ("L0_v", P), ("L0_o", P),
    ("X0_q", P), ("X0_k", P), ("X0_v", P), ("X0_o", P), ("X0_bq", 1), ("X0_bk", 1),
    ("X1_q", P), ("X1_k", P), ("X1_v", P), ("X1_o", P), ("X1_bq", 1), ("X1_bk", 1),
    ("mask_qk", P), ("mask_kq", P), ("sel", HG * P),
    ("ffn_ws", P), ("ffn_b", P),
]
AT = {}
_n = 0
for _name, _w in COLS:
    AT[_name] = (_n, _n + _w)
    _n += _w
NCOLS = _n
ROWS = [("X0_bv", P), ("X0_bo", P), ("X1_bv", P), ("X1_bo", P), ("ones", P)]
RAT = {}
_n = 0
for _name, _w in ROWS:
    RAT[_name] = (_n, _n + _w)
    _n += _w
NROWS = _n
DCOLS_ = [("Wb", 4), ("ident32", 32), ("mask2", 2 * P), ("off", P), ("heads", P), ("short", 5 * P)] + [
    (f"level{l}", P) for l in range(5)]
DAT = {}
_n = 0
for _name, _w in DCOLS_:
    DAT[_name] = (_n, _n + _w)
    _n += _w
DCOLS = _n
FLOOR = 0.05
MCOLS_ = [("mlp_w1", P), ("mlp_w1s", P), ("mlp_w2", 4), ("mlp_b1", 1), ("b2", 16), ("log_temp", 16), ("onorm", P), ("Wo", P),
          ("Wg", 16), ("bg", 16), ("bias", 16), ("iota", 16), ("eb1", 32), ("eb2", P), ("W1", 16 * 2 * P), ("W2", 16 * 2 * P)]
MAT = {}
_n = 0
for _name, _w in MCOLS_:
    MAT[_name] = (_n, _n + _w)
    _n += _w
MCOLS = _n
NLORA = 5 * P

PER = {}
STEPS, STAGE, BEFORE = {}, {}, {}


class Turn:

    def __init__(self, eng, loop, start=0):
        self.eng, self.start, self.done = eng, start, {}
        self.tmp = [eng.alloc_register(f"wait_{loop}_{k}") for k in range(4)]
        self.n = 0
        for per in sorted(set(PER.values())):
            self.done[per] = eng.alloc_register(f"done_{loop}_{per}")
            eng.reg_mov(self.done[per], start * per)

    def value(self, per, n):
        self.n += 1
        r = self.tmp[self.n % len(self.tmp)]
        self.eng.reg_add(r, self.done[per], n)
        return r

    def next(self):
        for per, r in self.done.items():
            self.eng.reg_add(r, r, per)


def decoder(nc, A, out):
    ctx = ExitStack()
    with ctx:
        def sb(name, shape, dt=F32, life=None):
            return (life or ctx).enter_context(nc.sbuf_tensor(name, shape, dt))

        sems = {}

        def sem(name):
            name = STEPS[name][0] if name in STEPS else name
            if name not in sems:
                sems[name] = ctx.enter_context(nc.semaphore("s_" + name.replace(".", "_")))
            return sems[name]

        def at(name, i, n):
            if name not in STEPS:
                return sem(name), i.value(PER[name], n)
            kind, earlier = STEPS[name]
            return sem(name), i.value(PER[kind], n + earlier + BEFORE.get(kind, 0))

        def stage(kind, prefix, counts):
            for signal, n in counts.items():
                shared = f"{kind}.{signal}"
                STEPS[f"{prefix}.{signal}"] = (shared, PER.get(shared, 0))
                STAGE[f"{prefix}.{signal}"] = n
                PER[shared] = PER.get(shared, 0) + n

        bkA = ctx.enter_context(nc.psum_tensor("bkA", [P, 2, 512], F32))
        bkB = ctx.enter_context(nc.psum_tensor("bkB", [P, 2, 2, 512], F32))
        bkC = ctx.enter_context(nc.psum_tensor("bkC", [P, 512], F32))
        bkD = ctx.enter_context(nc.psum_tensor("bkD", [P, 512], F32))
        bkD16 = bkD[:, :].bitcast(BF16)

        W = sb("W", [P, NCOLS])
        rows = sb("rows", [1, NROWS])
        lora = sb("lora", [8, NLORA])
        ident16 = sb("ident16", [P, P], BF16)
        mask16 = sb("mask16", [P, 2, 2, P], BF16)
        sel16 = sb("sel16", [P, HG, P], BF16)
        ffn_wi = sb("ffn_wi", [P, P], I32)
        ffn_w16 = sb("ffn_w16", [P, P], BF16)

        def w(name):
            return W[:, AT[name][0]:AT[name][1]]

        def row(name):
            return rows[0:1, RAT[name][0]:RAT[name][1]]

        ident = w("ident")

        xg = sb("xg", [P, NT, P])
        cg = sb("cg", [P, NT, P])
        xT = sb("xT", [P, T])
        cT = sb("cT", [P, T])
        y = sb("y", [P, NT, P])

        qf = sb("qf", [P, 2, T])
        rt = sb("rt", [P, 2, T])
        part = sb("part", [P, 2, 3, T], BF16)
        resid = sb("resid", [P, 2, T])
        stk = sb("stk", [P, 2, HG, T], BF16)
        vaug = sb("vaug", [P, NT, H, VW])
        mx = sb("mx", [P, GB, 2, HP, HG])
        mr = sb("mr", [P, 2, 2, HP, HG])
        mx16 = sb("mx16", [P, 2, HP, 64], BF16)
        nmT = sb("nmT", [P, 2, P], BF16)
        pT = sb("pT", [P, 2, 2 * 2 * S])
        rec = sb("rec", [P, 2, H])
        o_tm = sb("o_tm", [P, NT, H, DH])
        oT = sb("oT", [P, T])

        eps_ln = sb("eps_ln", [P, 1])
        bst = sb("bst", [P, NT, 6])
        bsum, bdif, bsq, bd2, mean, var = (sb(n, [P, NT]) for n in ("bsum", "bdif", "bsq", "bd2", "mean", "var"))
        lnv = sb("lnv", [P, NT])
        r0 = sb("r0", [P, NT])
        ra = sb("ra", [P, NT])
        rb = sb("rb", [P, NT])
        rstd = sb("rstd", [P, NT])

        am = sb("am", [P, NT])
        rxs = sb("rxs", [P, NT])
        xs = sb("xs", [P, NT])
        xq = sb("xq", [P, NT, P])
        xq16 = sb("xq16", [P, NT, P], BF16)
        xqT = sb("xqT", [P, T], BF16)
        fo = sb("fo", [P, NT, P])

        scratch = nc.dram_tensor("stack_scratch", [2, 3 * P, T], BF16, kind="Internal").ap()
        x3_d, v_d, dl_d, sh_d = (nc.dram_tensor(n, [B * S, P], F32, kind="Internal").ap().rearrange("(n p) c -> p n c", p=P)
                                 for n in ("x3_scratch", "v_scratch", "delta_scratch", "short_scratch"))

        PER.update({"xg": 16, "cg": 16, "xgT_ps": 1, "xgT": 1, "cgT": 1, "free": 64})

        def attention_counts(p, rope):
            stage("A", p, {
                "proj": 3 + 2 * rope, "rot": 6 if rope else 2, "p1": 2, "res": 2,
                "p2": 2, "p3": 2, "scr0": 16, "scr1": 16, "stk": 18 * 16, "v": 1,
                "s1": 4 * H // 2, "max": 4 * H // 2, "mparts": 2 * 5, "nmT_ps": 2,
                "nmT": 2, "s2": H, "exp": H, "pv": H,
                "rec": 2, "o": 2, "oT_ps": 1, "oT": 1, "oproj": 1, "y": 1})

        def norm_counts(p, transposed):
            stage("N", p, {"bst": NT, "mv": 6, "lnv": 1, "r0": 1, "newton": 4, "x": NT})
            if transposed:
                stage("N", p, {"xT_ps": 1, "xT": 1})

        def attention_pe(pe, p, i, q_ready, kv_ready, kvT, rope, causal, bias):
            pe.wait_ge(*q_ready)
            nc.tensor.matmul(bkA[:, 0, :], w(f"{p}_q"), xT[:, :], start=True, stop=True).then_inc(sem(f"{p}.proj"), 1)
            if rope:
                nc.tensor.matmul(bkA[:, 1, :], w(f"{p}_qs"), xT[:, :], start=True, stop=True).then_inc(sem(f"{p}.proj"), 1)
            if kv_ready:
                pe.wait_ge(*kv_ready)
            nc.tensor.matmul(bkB[:, 0, 0, :], w(f"{p}_k"), kvT[:, :], start=True, stop=True).then_inc(sem(f"{p}.proj"), 1)
            if rope:
                nc.tensor.matmul(bkB[:, 0, 1, :], w(f"{p}_ks"), kvT[:, :], start=True, stop=True).then_inc(sem(f"{p}.proj"), 1)
            for t in range(NT):
                o = bkB[:, 1, 0, t * P:(t + 1) * P]
                if bias:
                    nc.tensor.matmul(o, row("ones"), row(f"{p}_bv"), start=True, stop=False)
                mm = nc.tensor.matmul(o, kvT[:, t * P:(t + 1) * P], w(f"{p}_v"), start=not bias, stop=True)
            mm.then_inc(sem(f"{p}.proj"), 1)
            pe.wait_ge(*at(f"{p}.stk", i, STAGE[f"{p}.stk"]))
            pe.wait_ge(*at(f"{p}.rot", i, STAGE[f"{p}.rot"]))

            def score_rows(b, j, n):
                hp, g = j % 2, j // 2 * 2
                for qt in range(2):
                    kw = P if causal and qt == 0 else S
                    u = 2 * n + qt
                    if u >= 2:
                        pe.wait_ge(*at(f"{p}.max", i, u - 1))
                    o = bkA[:, u % 2, 0:2 * kw].rearrange("q (h k) -> q h k", h=2)
                    for hh in range(2):
                        r = slice(64 * hp, 64 * hp + SLOTS * DH)
                        c0 = b * S + qt * P
                        mm = nc.tensor.matmul(o[:, hh, :], stk[r, 0, g + hh, c0:c0 + P],
                                              stk[r, 1, g + hh, b * S:b * S + kw],
                                              start=hh == 0, stop=not causal and hh == 1, skip_group_check=True)
                    if causal:
                        mm = nc.tensor.matmul(o[:, :, kw - P:kw], ident16[:, :], mask16[:, 0, :, :],
                                              start=False, stop=True, skip_group_check=True)
                    mm.then_inc(sem(f"{p}.s1"), 1)

            def max_rows(b):
                pe.wait_ge(*at(f"{p}.mparts", i, 5 * (b + 1)))
                for qt in range(2):
                    mm = nc.tensor.transpose(bkD16[:, qt * P:(qt + 1) * P],
                                             mx16[:, qt, :, :].rearrange("q a c -> q (a c)"), ident16[:, :])
                mm.then_inc(sem(f"{p}.nmT_ps"), 1)

            def score_cols(b, j, n):
                hp, g = j % 2, j // 2 * 2
                if n >= 2:
                    pe.wait_ge(*at(f"{p}.exp", i, n - 1))
                for kt in range(2):
                    q0 = P if causal and kt else 0
                    for hh in range(2):
                        o = bkB[:, n % 2, kt, hh * (S - q0):(hh + 1) * (S - q0)]
                        r = slice(64 * hp, 64 * hp + 3 * HG)
                        nc.tensor.matmul(o, sel16[r, g + hh, :],
                                         nmT[r, :, :].rearrange("c t q -> c (t q)")[:, q0:S],
                                         start=hh == 0, stop=False, skip_group_check=True)
                        r = slice(64 * hp, 64 * hp + SLOTS * DH)
                        mm = nc.tensor.matmul(o, stk[r, 1, g + hh, b * S + kt * P:b * S + (kt + 1) * P],
                                              stk[r, 0, g + hh, b * S + q0:(b + 1) * S],
                                              start=False, stop=not causal and hh == 1, skip_group_check=True)
                    if causal:
                        o = bkB[:, n % 2, kt, 0:2 * (S - q0)].rearrange("k (h q) -> k h q", h=2)[:, :, 0:P]
                        mm = nc.tensor.matmul(o, ident16[:, :], mask16[:, 1, :, :], start=False, stop=True, skip_group_check=True)
                mm.then_inc(sem(f"{p}.s2"), 1)

            def weigh_values(b, j, n):
                hp, g = j % 2, j // 2 * 2
                pe.wait_ge(*at(f"{p}.exp", i, n + 1))
                if n == 0:
                    pe.wait_ge(*at(f"{p}.v", i, 1))
                if j == 0 and b:
                    pe.wait_ge(*at(f"{p}.o", i, b))
                acc = bkC[:, 0:2 * H * VW].rearrange("q (t h v) -> q t h v", t=2, h=H)
                for hh in range(2):
                    h = hp * HG + g + hh
                    for qt in range(2):
                        kts = [0] if causal and qt == 0 else [0, 1]
                        for kt in kts:
                            q0 = P if causal and kt else 0
                            c = kt * 512 + hh * (S - q0) + qt * P - q0
                            mm = nc.tensor.matmul(acc[:, qt, h, :], pT[:, n % 2, c:c + P],
                                                  vaug[:, 2 * b + kt, h, :], start=kt == 0, stop=kt == kts[-1],
                                                  skip_group_check=True)
                mm.then_inc(sem(f"{p}.pv"), 1)

            pairs = H // 2
            for j in range(pairs):
                score_rows(0, j, j)
            for b in range(GB):
                max_rows(b)
                pe.wait_ge(*at(f"{p}.nmT", i, b + 1))
                if b == 0:
                    pe.wait_ge(*at(f"{p}.v", i, 1))
                for j in range(pairs):
                    n = b * pairs + j
                    score_cols(b, j, n)
                    if b + 1 < GB:
                        score_rows(b + 1, j, n + pairs)
                    if n:
                        weigh_values((n - 1) // pairs, (n - 1) % pairs, n - 1)
            weigh_values(GB - 1, pairs - 1, GB * pairs - 1)

            pe.wait_ge(*at(f"{p}.o", i, GB))
            for t in range(NT):
                mm = nc.tensor.transpose(bkD[:, t * P:(t + 1) * P], o_tm[:, t, :, :].rearrange("q h d -> q (h d)"), ident)
            mm.then_inc(sem(f"{p}.oT_ps"), 1)
            pe.wait_ge(*at(f"{p}.oT", i, 1))
            for t in range(NT):
                o = bkA[:, 0, t * P:(t + 1) * P]
                if bias:
                    nc.tensor.matmul(o, row("ones"), row(f"{p}_bo"), start=True, stop=False)
                mm = nc.tensor.matmul(o, oT[:, t * P:(t + 1) * P], w(f"{p}_o"), start=not bias, stop=True)
            mm.then_inc(sem(f"{p}.oproj"), 1)

        def attention_dve(dve, p, i, rope, causal, bias):
            def rc(name):
                return w(name).rearrange("p (o s) -> p o s", o=1).to_broadcast([P, GB, S])
            for n in range(2):
                bank = bkA if n == 0 else bkB[:, 0]
                if rope:
                    v3 = lambda a: a.rearrange("p (b s) -> p b s", b=GB)
                    dve.wait_ge(*at(f"{p}.proj", i, 2 * n + 1))
                    nc.vector.tensor_tensor(v3(rt[:, 0, :]), v3(bank[:, 0, :]), rc("rope_c"), ALU.mult).then_inc(sem(f"{p}.rot"), 1)
                    dve.wait_ge(*at(f"{p}.proj", i, 2 * n + 2))
                    nc.vector.tensor_tensor(v3(rt[:, 1, :]), v3(bank[:, 1, :]), rc("rope_s"), ALU.mult).then_inc(sem(f"{p}.rot"), 1)
                    dve.wait_ge(*at(f"{p}.rot", i, 3 * n + 2))
                    nc.vector.tensor_tensor(qf[:, n, :], rt[:, 0, :], rt[:, 1, :], ALU.add).then_inc(sem(f"{p}.rot"), 1)
                    dve.wait_ge(*at(f"{p}.rot", i, 3 * n + 3))
                else:
                    dve.wait_ge(*at(f"{p}.proj", i, n + 1))
                    b = w(f"{p}_bq" if n == 0 else f"{p}_bk")
                    nc.vector.tensor_scalar(qf[:, n, :], bank[:, 0, :], b, None, ALU.add).then_inc(sem(f"{p}.rot"), 1)
            def maxima(b, j, n):
                hp, g = j % 2, j // 2 * 2
                for qt in range(2):
                    u = 2 * n + qt
                    kw = P if causal and qt == 0 else S
                    dve.wait_ge(*at(f"{p}.s1", i, u + 1))
                    nc.vector.tensor_reduce(mx[:, b, qt, hp, g:g + 2],
                                            bkA[:, u % 2, 0:2 * kw].rearrange("q (h k) -> q h k", h=2),
                                            AX.X, ALU.max).then_inc(sem(f"{p}.max"), 1)

            def max_parts(b):
                s, m = sem(f"{p}.mparts"), mx[:, b, :, :, :]
                dve.wait_ge(*at(f"{p}.max", i, 16 * (b + 1)))
                if b:
                    dve.wait_ge(*at(f"{p}.nmT_ps", i, b))
                nc.vector.tensor_copy(mx16[:, :, :, 0:8], m).then_inc(s, 1)
                dve.wait_ge(*at(f"{p}.mparts", i, 5 * b + 1))
                nc.vector.tensor_tensor(mr[:, 0], m, mx16[:, :, :, 0:8], ALU.subtract).then_inc(s, 1)
                dve.wait_ge(*at(f"{p}.mparts", i, 5 * b + 2))
                nc.vector.tensor_copy(mx16[:, :, :, 8:16], mr[:, 0]).then_inc(s, 1)
                dve.wait_ge(*at(f"{p}.mparts", i, 5 * b + 3))
                nc.vector.tensor_tensor(mr[:, 1], mr[:, 0], mx16[:, :, :, 8:16], ALU.subtract).then_inc(s, 1)
                dve.wait_ge(*at(f"{p}.mparts", i, 5 * b + 4))
                nc.vector.tensor_copy(mx16[:, :, :, 16:24], mr[:, 1]).then_inc(s, 1)

            def normalise(b):
                acc = bkC[:, 0:2 * H * VW].rearrange("q (t h v) -> q t h v", t=2, h=H)
                dve.wait_ge(*at(f"{p}.pv", i, 8 * (b + 1)))
                nc.vector.reciprocal(rec[:, :, :], acc[:, :, :, DH]).then_inc(sem(f"{p}.rec"), 1)
                dve.wait_ge(*at(f"{p}.rec", i, b + 1))
                nc.vector.tensor_tensor(o_tm[:, 2 * b:2 * b + 2, :, :], acc[:, :, :, 0:DH],
                                        rec[:, :, :].rearrange("q t (h o) -> q t h o", o=1).to_broadcast([P, 2, H, DH]),
                                        ALU.mult).then_inc(sem(f"{p}.o"), 1)
            pairs = H // 2
            for j in range(pairs):
                maxima(0, j, j)
            max_parts(0)
            for j in range(pairs):
                maxima(1, j, j + pairs)
            max_parts(1)
            normalise(0)
            normalise(1)
            dve.wait_ge(*at(f"{p}.oproj", i, 1))
            nc.vector.tensor_tensor(y[:, :, :], bkA[:, 0, :].rearrange("q (t c) -> q t c", t=NT), xg[:, :, :],
                                    ALU.add).then_inc(sem(f"{p}.y"), 1)

        def attention_act(act, p, i, rope, causal):
            s1, s2 = sem(f"{p}.p1"), sem(f"{p}.p2")
            for n in range(2):
                act.wait_ge(*at(f"{p}.rot", i, (3 if rope else 1) * (n + 1)))
                nc.scalar.copy(part[:, n, 0, :], qf[:, n, :]).then_inc(s1, 1)
            act.wait_ge(*at(f"{p}.proj", i, STAGE[f"{p}.proj"]))
            nc.scalar.copy(vaug[:, :, :, 0:DH],
                           bkB[:, 1, 0, :].rearrange("k (t h d) -> k t h d", t=NT, h=H)).then_inc(sem(f"{p}.v"), 1)
            for n in range(2):
                act.wait_ge(*at(f"{p}.res", i, n + 1))
                nc.scalar.copy(part[:, n, 1, :], resid[:, n, :]).then_inc(s2, 1)
            pairs = H // 2
            for b in range(GB):
                act.wait_ge(*at(f"{p}.nmT_ps", i, b + 1))
                if b:
                    act.wait_ge(*at(f"{p}.s2", i, b * pairs))
                nc.scalar.mul(nmT[:, :, :].rearrange("c t q -> c (t q)"), bkD16[:, 0:S], -1.0).then_inc(sem(f"{p}.nmT"), 1)
                for j in range(pairs):
                    n = b * pairs + j
                    act.wait_ge(*at(f"{p}.s2", i, n + 1))
                    if n >= 2:
                        act.wait_ge(*at(f"{p}.pv", i, n - 1))
                    wd = 3 * S if causal else 4 * S
                    nc.scalar.activation(pT[:, n % 2, 0:wd], bkB[:, n % 2, :, :].rearrange("k t c -> k (t c)")[:, 0:wd],
                                         ACT.Exp, scale=SCALE).then_inc(sem(f"{p}.exp"), 1)
            act.wait_ge(*at(f"{p}.oT_ps", i, 1))
            nc.scalar.copy(oT[:, :], bkD[:, :]).then_inc(sem(f"{p}.oT"), 1)

        def attention_pool(pool, p, i, rope, causal):
            for n in range(2):
                pool.wait_ge(*at(f"{p}.p1", i, n + 1))
                nc.gpsimd.tensor_tensor(resid[:, n, :], qf[:, n, :], part[:, n, 0, :], ALU.subtract).then_inc(sem(f"{p}.res"), 1)
            for n in range(2):
                pool.wait_ge(*at(f"{p}.p2", i, n + 1))
                pool.wait_ge(*at(f"{p}.res", i, n + 1))
                nc.gpsimd.tensor_tensor(part[:, n, 2, :], resid[:, n, :], part[:, n, 1, :], ALU.subtract).then_inc(sem(f"{p}.p3"), 1)

        def attention_sp(sp, p, i):
            for n in range(2):
                p3, p2 = at(f"{p}.p3", i, n + 1), at(f"{p}.p2", i, n + 1)
                sp.wait_ge(*p3)
                sp.wait_ge(*p2)
                sp.dma_start(scratch[n].rearrange("(j p) t -> p j t", j=3), part[:, n, :, :]).then_inc(sem(f"{p}.scr{n}"), 16)
            for n in range(2):
                sp.wait_ge(*at(f"{p}.scr{n}", i, 16))
                src = scratch[n].rearrange("(e a g) t -> a e g t", a=HP, g=HG)
                runs = [(0, 1, 0), (1, 1, 0), (2, 1, 0), (3, 1, 1), (4, 1, 1), (5, 1, 2)] if n == 0 else [(0, 3, 0), (3, 2, 0), (5, 1, 0)]
                for a in range(HP):
                    for s0, k, j in runs:
                        d0 = 64 * a + DH * s0
                        sp.dma_start(stk[d0:d0 + DH * k, n, :, :], src[a, DH * j:DH * (j + k), :, :]).then_inc(sem(f"{p}.stk"), 16)

        def norm_dve(dve, p, i, y_ready):
            dve.wait_ge(*y_ready)
            for t in range(NT):
                nc.vector.bn_stats(bst[:, t, :], y[:, t, :]).then_inc(sem(f"{p}.bst"), 1)
            dve.wait_ge(*at(f"{p}.bst", i, NT))
            s = sem(f"{p}.mv")
            nc.vector.tensor_tensor(bsum[:, :], bst[:, :, 1], bst[:, :, 4], ALU.add).then_inc(s, 1)
            nc.vector.tensor_tensor(bdif[:, :], bst[:, :, 1], bst[:, :, 4], ALU.subtract).then_inc(s, 1)
            nc.vector.tensor_tensor(bsq[:, :], bst[:, :, 2], bst[:, :, 5], ALU.add).then_inc(s, 1)
            dve.wait_ge(*at(f"{p}.mv", i, 3))
            nc.vector.scalar_tensor_tensor(out=bd2[:, :], in0=bdif[:, :], scalar=0.25, in1=bdif[:, :], op0=ALU.mult, op1=ALU.mult).then_inc(s, 1)
            nc.vector.tensor_scalar(mean[:, :], bsum[:, :], 0.5, None, ALU.mult).then_inc(s, 1)
            dve.wait_ge(*at(f"{p}.mv", i, 5))
            nc.vector.scalar_tensor_tensor(out=var[:, :], in0=bsq[:, :], scalar=1.0 / P, in1=bd2[:, :], op0=ALU.mult, op1=ALU.add).then_inc(s, 1)
            dve.wait_ge(*at(f"{p}.r0", i, 1))
            s = sem(f"{p}.newton")
            nc.vector.scalar_tensor_tensor(out=ra[:, :], in0=var[:, :], scalar=LN_EPS, in1=r0[:, :], op0=ALU.add, op1=ALU.mult).then_inc(s, 1)
            dve.wait_ge(*at(f"{p}.newton", i, 1))
            nc.vector.tensor_tensor(rb[:, :], ra[:, :], r0[:, :], ALU.mult).then_inc(s, 1)
            dve.wait_ge(*at(f"{p}.newton", i, 2))
            nc.vector.tensor_scalar(ra[:, :], rb[:, :], -0.5, 1.5, ALU.mult, ALU.add).then_inc(s, 1)
            dve.wait_ge(*at(f"{p}.newton", i, 3))
            nc.vector.tensor_tensor(rstd[:, :], ra[:, :], r0[:, :], ALU.mult).then_inc(s, 1)
            dve.wait_ge(*at(f"{p}.newton", i, 4))
            for t in range(NT):
                nc.vector.tensor_scalar(xg[:, t, :], y[:, t, :], mean[:, t:t + 1], rstd[:, t:t + 1], ALU.subtract, ALU.mult).then_inc(sem(f"{p}.x"), 1)

        def norm_act(act, p, i, dst):
            act.wait_ge(*at(f"{p}.mv", i, 6))
            nc.scalar.activation(lnv[:, :], var[:, :], ACT.Ln, bias=eps_ln[:, :]).then_inc(sem(f"{p}.lnv"), 1)
            act.wait_ge(*at(f"{p}.lnv", i, 1))
            nc.scalar.activation(r0[:, :], lnv[:, :], ACT.Exp, scale=-0.5).then_inc(sem(f"{p}.r0"), 1)
            if dst is not None:
                act.wait_ge(*at(f"{p}.xT_ps", i, 1))
                nc.scalar.copy(dst, bkA[:, 1, :].rearrange("c (b s) -> c b s", b=GB)).then_inc(sem(f"{p}.xT"), 1)

        def norm_pe(pe, p, i):
            for t in range(NT):
                pe.wait_ge(*at(f"{p}.x", i, t + 1))
                mm = nc.tensor.transpose(bkA[:, 1, t * P:(t + 1) * P], xg[:, t, :], ident)
            mm.then_inc(sem(f"{p}.xT_ps"), 1)

        MAGIC = 1.5 * 2.0 ** 23
        PER.update({"F.am": 1, "F.xs": 1, "F.rxs": 1, "F.div": NT, "F.clip": 1, "F.xq": 1, "F.xqT_ps": 1, "F.xqT": 1,
                    "F.acc": 1, "F.fo": NT, "F.xb": 1, "F.y": 1})

        def ffn_dve(dve, i):
            dve.wait_ge(*at("n1.x", i, NT))
            nc.vector.tensor_reduce(am[:, :], xg[:, :, :], AX.X, ALU.max, apply_absolute_value=True).then_inc(sem("F.am"), 1)
            dve.wait_ge(*at("F.am", i, 1))
            nc.vector.tensor_scalar(xs[:, :], am[:, :], 1e-6, 1.0 / 127.0, ALU.max, ALU.mult).then_inc(sem("F.xs"), 1)
            dve.wait_ge(*at("F.xs", i, 1))
            nc.vector.reciprocal(rxs[:, :], xs[:, :]).then_inc(sem("F.rxs"), 1)
            dve.wait_ge(*at("F.rxs", i, 1))
            for t in range(NT):
                nc.vector.tensor_scalar(xq[:, t, :], xg[:, t, :], rxs[:, t:t + 1], MAGIC, ALU.mult, ALU.add).then_inc(sem("F.div"), 1)
            dve.wait_ge(*at("F.div", i, NT))
            nc.vector.tensor_scalar(xq[:, :, :], xq[:, :, :], MAGIC + 127.0, MAGIC - 128.0, ALU.min, ALU.max).then_inc(sem("F.clip"), 1)
            dve.wait_ge(*at("F.clip", i, 1))
            nc.vector.tensor_scalar(xq16[:, :, :], xq[:, :, :], MAGIC, None, ALU.subtract).then_inc(sem("F.xq"), 1)
            dve.wait_ge(*at("F.acc", i, 1))
            for t in range(NT):
                nc.vector.scalar_tensor_tensor(out=fo[:, t, :], in0=bkA[:, 0, t * P:(t + 1) * P], scalar=xs[:, t:t + 1],
                                               in1=w("ffn_ws"), op0=ALU.mult, op1=ALU.mult).then_inc(sem("F.fo"), 1)
            dve.wait_ge(*at("F.xb", i, 1))
            dve.wait_ge(*at("F.fo", i, NT))
            nc.vector.tensor_tensor(y[:, :, :], fo[:, :, :], xq[:, :, :], ALU.add).then_inc(sem("F.y"), 1)

        def ffn_pool(pool, i):
            pool.wait_ge(*at("n1.x", i, NT))
            pool.wait_ge(*at("F.xq", i, 1))
            nc.gpsimd.tensor_tensor(xq[:, :, :], xg[:, :, :],
                                    w("ffn_b").rearrange("p (o c) -> p o c", o=1).to_broadcast([P, NT, P]),
                                    ALU.add).then_inc(sem("F.xb"), 1)

        def ffn_pe(pe, i):
            pe.wait_ge(*at("F.xq", i, 1))
            for t in range(NT):
                mm = nc.tensor.transpose(bkD16[:, t * P:(t + 1) * P], xq16[:, t, :], ident16[:, :])
            mm.then_inc(sem("F.xqT_ps"), 1)
            pe.wait_ge(*at("F.xqT", i, 1))
            for t in range(NT):
                mm = nc.tensor.matmul(bkA[:, 0, t * P:(t + 1) * P], xqT[:, t * P:(t + 1) * P], ffn_w16[:, :], start=True, stop=True)
            mm.then_inc(sem("F.acc"), 1)

        def ffn_act(act, i):
            act.wait_ge(*at("F.xqT_ps", i, 1))
            nc.scalar.copy(xqT[:, :], bkD16[:, 0:T]).then_inc(sem("F.xqT"), 1)

        TAPS, SHORT, LONG = 4, 5, 64
        NH, DV, BLK = 4, 32, 32
        LEVELS = 5
        NU = P // BLK
        first = ExitStack()
        xTp = sb("xTp", [P, GB, TAPS - 1 + S], life=first)
        conv_bc = sb("conv_bc", [P, TAPS, 3 * P], life=first)
        Wqkv = sb("Wqkv", [P, 3 * P], life=first)
        DW = sb("DW", [P, DCOLS], life=first)
        qkv = sb("qkv", [P, NT, 3 * P], life=first)
        sq = sb("sq", [P, NT, 2 * NH, DV], life=first)
        ez, eb, beta = (sb(n, [P, NT * NH], life=first) for n in ("ez", "eb", "beta"))
        ss, lss, rs0, rsa, rsb, rn = (sb(n, [P, NT * 2 * NH], life=first) for n in ("ss", "lss", "rs0", "rsa", "rsb", "rn"))
        qkn = sb("qkn", [P, NT, 2 * NH, DV], life=first)
        vb = sb("vb", [P, NT, NH, DV], life=first)
        kb = sb("kb", [P, NT, NH, DV], life=first)
        kT = sb("kT", [P, NT, 3 * P], life=first)
        MT = sb("MT", [P, NT, NH, 2 * P], life=first)
        Cm = sb("Cm", [P, 2, NT * NH, P], life=first)
        LT = sb("LT", [P, NT * NH, P], life=first)
        TTf = sb("TTf", [P, NT * NH, P], life=first)
        Tc, TcT, Xs = (sb(n, [P, NT * NH, BLK], life=first) for n in ("Tc", "TcT", "Xs"))
        rr = sb("rr", [P, GB, NH, DV], life=first)
        uu = sb("uu", [P, GB, NH, DV], life=first)
        wv = sb("wv", [P, GB, NH, DV], life=first)
        Sbd = sb("Sbd", [P, GB, P], life=first)
        vTp = sb("vTp", [P, GB, SHORT - 1 + S], life=first)
        d_tm = sb("d_tm", [P, GB, 2, P], life=first)
        sh_tm = sb("sh_tm", [P, NT, P], life=first)
        eps_l2 = sb("eps_l2", [P, 1], life=first)

        PER.update({"D.z": 1, "D.qkv": 1, "D.ez": 1, "D.silu": 1, "D.beta": 2, "D.sq": 1, "D.ss": 1, "D.lss": 1,
                    "D.rs0": 1, "D.newton": 4, "D.qkn": 1, "D.vkb": 2, "D.tr": NT, "D.trc": NT,
                    "D.gram": NT, "D.msk": NT, "D.cm": LEVELS, "D.lt": 1, "D.mmX": LEVELS, "D.tc": LEVELS,
                    "D.tcT": LEVELS, "D.expA": 2 * LEVELS, "D.expD": 2 * LEVELS, "D.xs": LEVELS - 1,
                    "D.mmY": LEVELS - 1, "D.ks": 1, "D.r": 1, "D.u": 2 * NU, "D.uc": 2 * NU, "D.lu": 2 * (NU - 1),
                    "D.w": 2 * (NU - 1), "D.S": 1, "D.Sbd": 1, "D.o": 2, "D.oc": 2, "D.vT": 1, "D.vTc": 1,
                    "D.sh": 1, "D.shc": 1})

        def dw(name):
            return DW[:, DAT[name][0]:DAT[name][1]]

        def delta_pe(pe, i):
            pe.wait_ge(*at("n2.xT", i, 1))
            for t in range(NT):
                c = TAPS - 1 + (t % 2) * P
                mm = nc.tensor.matmul(bkD[:, t * NH:(t + 1) * NH], xTp[:, t // 2, c:c + P], dw("Wb"), start=True, stop=True)
            mm.then_inc(sem("D.z"), 1)
            for t in range(NT):
                for j in range(TAPS):
                    c = j + (t % 2) * P
                    mm = nc.tensor.matmul(bkB[:, t // 2, t % 2, 0:3 * P], xTp[:, t // 2, c:c + P], conv_bc[:, j, :],
                                          start=j == 0, stop=j == TAPS - 1)
            mm.then_inc(sem("D.qkv"), 1)
            pe.wait_ge(*at("D.silu", i, 1))
            for t in range(NT):
                mm = nc.tensor.transpose(bkC[:, t * P:(t + 1) * P], qkv[:, t, 2 * P:3 * P], ident)
            mm.then_inc(sem("D.vT"), 1)
            pe.wait_ge(*at("D.qkn", i, 1))
            pe.wait_ge(*at("D.vkb", i, 2))
            for t in range(NT):
                if t >= 2:
                    pe.wait_ge(*at("D.trc", i, t - 1))
                for n, a in enumerate((qkn[:, t, NH:2 * NH, :], kb[:, t, :, :], qkn[:, t, 0:NH, :])):
                    mm = nc.tensor.transpose(bkA[:, t % 2, n * P:(n + 1) * P], a.rearrange("q h d -> q (h d)"), ident)
                mm.then_inc(sem("D.tr"), 1)
            for t in range(NT):
                pe.wait_ge(*at("D.trc", i, t + 1))
                if t:
                    pe.wait_ge(*at("D.msk", i, t))
                for h in range(NH):
                    r = slice(DV * h, DV * (h + 1))
                    mm = nc.tensor.matmul(bkB[:, h // 2, h % 2, 0:2 * P], kT[r, t, 0:P], kT[r, t, P:3 * P], start=True, stop=True)
                mm.then_inc(sem("D.gram"), 1)
            pe.wait_ge(*at("D.vTc", i, 1))
            for t in range(NT):
                for j in range(SHORT):
                    c = j + (t % 2) * P
                    mm = nc.tensor.matmul(bkA[:, 1, t * P:(t + 1) * P], vTp[:, t // 2, c:c + P], dw("short")[:, j * P:(j + 1) * P],
                                          start=j == 0, stop=j == SHORT - 1)
            mm.then_inc(sem("D.sh"), 1)
            for l in range(LEVELS):
                pe.wait_ge(*at("D.cm", i, l + 1))
                if l:
                    pe.wait_ge(*at("D.tc", i, l))
                for m in range(NT * NH):
                    rhs = dw("ident32") if l == 0 else Tc[:, m, :]
                    mm = nc.tensor.matmul(bkC[:, m * BLK:(m + 1) * BLK], Cm[:, l % 2, m, :], rhs, start=True, stop=True)
                mm.then_inc(sem("D.mmX"), 1)
                if l:
                    pe.wait_ge(*at("D.xs", i, l))
                    pe.wait_ge(*at("D.expA", i, 2 * l))
                    pe.wait_ge(*at("D.expD", i, 2 * l))
                    for m in range(NT * NH):
                        mm = nc.tensor.matmul(bkD[:, m * BLK:(m + 1) * BLK], TTf[:, m, :], Xs[:, m, :], start=True, stop=True)
                    mm.then_inc(sem("D.mmY"), 1)
            pe.wait_ge(*at("D.expA", i, 2 * LEVELS))
            pe.wait_ge(*at("D.expD", i, 2 * LEVELS))
            pe.wait_ge(*at("D.lt", i, 1))
            for s in range(2):
                if s:
                    pe.wait_ge(*at("D.Sbd", i, 1))
                    for b in range(GB):
                        mm = nc.tensor.matmul(bkD[:, b * P:(b + 1) * P], kT[:, 2 * b + 1, P:2 * P], Sbd[:, b, :], start=True, stop=True)
                    mm.then_inc(sem("D.ks"), 1)
                    pe.wait_ge(*at("D.r", i, 1))
                for n in range(NU):
                    if n:
                        pe.wait_ge(*at("D.uc", i, NU * s + n))
                        for b in range(GB):
                            for h in range(NH):
                                mm = nc.tensor.matmul(bkD[:, b * P + h * DV:b * P + (h + 1) * DV], LT[:, (2 * b + s) * NH + h, :],
                                                      uu[:, b, h, :], start=True, stop=True)
                        mm.then_inc(sem("D.lu"), 1)
                        pe.wait_ge(*at("D.w", i, (NU - 1) * s + n))
                    for b in range(GB):
                        for h in range(NH):
                            rhs = wv[:, b, h, :] if n else rr[:, b, h, :] if s else vb[:, 2 * b, h, :]
                            mm = nc.tensor.matmul(bkC[:, b * P + h * DV:b * P + (h + 1) * DV], TTf[:, (2 * b + s) * NH + h, :],
                                                  rhs, start=True, stop=True)
                    mm.then_inc(sem("D.u"), 1)
                pe.wait_ge(*at("D.uc", i, NU * (s + 1)))
                if s == 0:
                    for b in range(GB):
                        mm = nc.tensor.matmul(bkD[:, b * P:(b + 1) * P], qkn[:, 2 * b, NH:2 * NH, :].rearrange("q h d -> q (h d)"),
                                              uu[:, b, :, :].rearrange("q h d -> q (h d)"), start=True, stop=True)
                    mm.then_inc(sem("D.S"), 1)
                else:
                    pe.wait_ge(*at("D.oc", i, 1))
                for b in range(GB):
                    t = 2 * b + s
                    if s:
                        nc.tensor.matmul(bkA[:, 0, b * P:(b + 1) * P], kT[:, t, 2 * P:3 * P], Sbd[:, b, :],
                                         start=True, stop=False, skip_group_check=True)
                    for h in range(NH):
                        mm = nc.tensor.matmul(bkA[:, 0, b * P + h * DV:b * P + (h + 1) * DV], MT[:, t, h, P:2 * P], uu[:, b, h, :],
                                              start=s == 0, stop=True, skip_group_check=True)
                mm.then_inc(sem("D.o"), 1)

        def delta_sp(sp, k, i):
            tiles = bass.ds(k * NT, NT)
            for src, dst, ready in ((qkv[:, :, 2 * P:3 * P], v_d, at("D.silu", i, 1)), (xg[:, :, :], x3_d, at("n2.x", i, NT)),
                                    (sh_tm[:, :, :], sh_d, at("D.shc", i, 1)),
                                    (d_tm[:, :, :, :].rearrange("p b s c -> p (b s) c"), dl_d, at("D.oc", i, 2))):
                sp.wait_ge(*ready)
                sp.dma_start(dst[:, tiles, :], src).then_inc(sem("free"), 16)

        def delta_act(act, i):
            act.wait_ge(*at("D.z", i, 1))
            nc.scalar.activation(ez[:, :], bkD[:, 0:NT * NH], ACT.Exp, scale=-1.0).then_inc(sem("D.ez"), 1)
            act.wait_ge(*at("D.qkv", i, 1))
            nc.scalar.activation(qkv[:, :, :].rearrange("p (a b) c -> p a b c", a=2), bkB[:, :, :, 0:3 * P], ACT.Silu).then_inc(sem("D.silu"), 1)
            act.wait_ge(*at("D.vT", i, 1))
            nc.scalar.copy(vTp[:, :, SHORT - 1:], bkC[:, :].rearrange("c (b s) -> c b s", b=GB)).then_inc(sem("D.vTc"), 1)
            act.wait_ge(*at("D.ss", i, 1))
            nc.scalar.activation(lss[:, :], ss[:, :], ACT.Ln, bias=eps_l2[:, :]).then_inc(sem("D.lss"), 1)
            act.wait_ge(*at("D.lss", i, 1))
            nc.scalar.activation(rs0[:, :], lss[:, :], ACT.Exp, scale=-0.5).then_inc(sem("D.rs0"), 1)
            for t in range(NT):
                act.wait_ge(*at("D.tr", i, t + 1))
                nc.scalar.copy(kT[:, t, :], bkA[:, t % 2, 0:3 * P]).then_inc(sem("D.trc"), 1)
            for l in range(LEVELS):
                if l:
                    act.wait_ge(*at("D.mmX", i, l + 1))
                    nc.scalar.copy(Xs[:, :, :], bkC[:, :].rearrange("p (m c) -> p m c", c=BLK)).then_inc(sem("D.xs"), 1)
                act.wait_ge(*at("D.tcT", i, l + 1))
                for k in (0, 1):
                    r = slice(BLK * k, BLK * (k + 1))
                    nc.scalar.copy(TTf[r, :, r], TcT[r, :, :]).then_inc(sem("D.expA"), 1)
            for n in range(2 * NU):
                act.wait_ge(*at("D.u", i, n + 1))
                if n == NU:
                    act.wait_ge(*at("D.o", i, 1))
                nc.scalar.copy(uu[:, :, :, :], bkC[:, 0:GB * P].rearrange("p (b h d) -> p b h d", b=GB, h=NH)).then_inc(sem("D.uc"), 1)

        def delta_pool(pool, k, i):
            pool.wait_ge(*at("D.silu", i, 1))
            qk = qkv[:, :, 0:2 * P].rearrange("p t (h d) -> p t h d", d=DV)
            nc.gpsimd.tensor_tensor(sq[:, :, :, :], qk, qk, ALU.mult).then_inc(sem("D.sq"), 1)
            bb = beta[:, :].rearrange("p (t h o) -> p t h o", h=NH, o=1).to_broadcast([P, NT, NH, DV])
            pool.wait_ge(*at("D.beta", i, 2))
            nc.gpsimd.tensor_tensor(vb[:, :, :, :], qkv[:, :, 2 * P:3 * P].rearrange("p t (h d) -> p t h d", d=DV), bb, ALU.mult).then_inc(sem("D.vkb"), 1)
            pool.wait_ge(*at("D.qkn", i, 1))
            nc.gpsimd.tensor_tensor(kb[:, :, :, :], qkn[:, :, NH:2 * NH, :], bb, ALU.mult).then_inc(sem("D.vkb"), 1)
            A = MT[:, :, :, 0:P].rearrange("p t h c -> p (t h) c")

            def masked(out, name, done):
                nc.gpsimd.tensor_tensor(out, A, dw(name).rearrange("p (o c) -> p o c", o=1).to_broadcast([P, NT * NH, P]),
                                        ALU.mult).then_inc(done, 1)
            pool.wait_ge(*at("D.msk", i, NT))
            for l in range(LEVELS):
                if l >= 2:
                    pool.wait_ge(*at("D.mmX", i, l - 1))
                masked(Cm[:, l % 2, :, :], f"level{l}", sem("D.cm"))
            masked(LT[:, :, :], "off", sem("D.lt"))

        def delta_dve(dve, k, i):
            dve.wait_ge(*at("D.ez", i, 1))
            nc.vector.tensor_scalar(eb[:, :], ez[:, :], 1.0, None, ALU.add).then_inc(sem("D.beta"), 1)
            dve.wait_ge(*at("D.beta", i, 1))
            nc.vector.reciprocal(beta[:, :], eb[:, :]).then_inc(sem("D.beta"), 1)
            dve.wait_ge(*at("D.sq", i, 1))
            nc.vector.tensor_reduce(ss[:, :].rearrange("p (t h) -> p t h", t=NT), sq[:, :, :, :], AX.X, ALU.add).then_inc(sem("D.ss"), 1)
            dve.wait_ge(*at("D.rs0", i, 1))
            s = sem("D.newton")
            nc.vector.scalar_tensor_tensor(out=rsa[:, :], in0=ss[:, :], scalar=1e-6, in1=rs0[:, :], op0=ALU.add, op1=ALU.mult).then_inc(s, 1)
            dve.wait_ge(*at("D.newton", i, 1))
            nc.vector.tensor_tensor(rsb[:, :], rsa[:, :], rs0[:, :], ALU.mult).then_inc(s, 1)
            dve.wait_ge(*at("D.newton", i, 2))
            nc.vector.tensor_scalar(rsa[:, :], rsb[:, :], -0.5, 1.5, ALU.mult, ALU.add).then_inc(s, 1)
            dve.wait_ge(*at("D.newton", i, 3))
            nc.vector.tensor_tensor(rn[:, :], rsa[:, :], rs0[:, :], ALU.mult).then_inc(s, 1)
            dve.wait_ge(*at("D.newton", i, 4))
            nc.vector.tensor_tensor(qkn[:, :, :, :], qkv[:, :, 0:2 * P].rearrange("p t (h d) -> p t h d", d=DV),
                                    rn[:, :].rearrange("p (t h o) -> p t h o", t=NT, o=1).to_broadcast([P, NT, 2 * NH, DV]),
                                    ALU.mult).then_inc(sem("D.qkn"), 1)
            for t in range(NT):
                dve.wait_ge(*at("D.gram", i, t + 1))
                nc.vector.tensor_tensor(MT[:, t, :, :], bkB[:, :, :, 0:2 * P].rearrange("p a b c -> p (a b) c"),
                                        dw("mask2").rearrange("p (o c) -> p o c", o=1).to_broadcast([P, NH, 2 * P]),
                                        ALU.mult).then_inc(sem("D.msk"), 1)
            dve.wait_ge(*at("D.sh", i, 1))
            nc.vector.tensor_copy(sh_tm[:, :, :], bkA[:, 1, :].rearrange("p (t c) -> p t c", t=NT)).then_inc(sem("D.shc"), 1)
            for l in range(LEVELS):
                if l == 0:
                    dve.wait_ge(*at("D.mmX", i, 1))
                    prev, new = dw("ident32").rearrange("p (o c) -> p o c", o=1).to_broadcast([P, NT * NH, BLK]), bkC
                else:
                    dve.wait_ge(*at("D.mmY", i, l))
                    prev, new = Tc[:, :, :], bkD
                nc.vector.tensor_tensor(Tc[:, :, :], prev, new[:, :].rearrange("p (m c) -> p m c", c=BLK), ALU.subtract).then_inc(sem("D.tc"), 1)
                dve.wait_ge(*at("D.tc", i, l + 1))
                if l:
                    dve.wait_ge(*at("D.expA", i, 2 * l))
                nc.vector.transpose(TcT[:, :, :].rearrange("p m c -> p (m c)"), Tc[:, :, :].rearrange("p m c -> p (m c)")).then_inc(sem("D.tcT"), 1)
                dve.wait_ge(*at("D.tcT", i, l + 1))
                for n in (2, 3):
                    r = slice(BLK * n, BLK * (n + 1))
                    nc.vector.tensor_copy(TTf[r, :, r], TcT[r, :, :]).then_inc(sem("D.expD"), 1)
            ps = lambda bank: bank[:, 0:GB * P].rearrange("p (b h d) -> p b h d", b=GB, h=NH)
            rows4 = lambda a, s: a.rearrange("p (b s) h d -> p s b h d", s=2)[:, s]
            for s in range(2):
                if s:
                    dve.wait_ge(*at("D.ks", i, 1))
                    nc.vector.tensor_tensor(rr[:, :, :, :], rows4(vb[:, :, :, :], 1), ps(bkD), ALU.subtract).then_inc(sem("D.r"), 1)
                for n in range(1, NU):
                    dve.wait_ge(*at("D.lu", i, (NU - 1) * s + n))
                    if s:
                        dve.wait_ge(*at("D.r", i, 1))
                    nc.vector.tensor_tensor(wv[:, :, :, :], rr[:, :, :, :] if s else rows4(vb[:, :, :, :], 0), ps(bkD), ALU.subtract).then_inc(sem("D.w"), 1)
                if s == 0:
                    dve.wait_ge(*at("D.S", i, 1))
                    nc.vector.tensor_tensor(Sbd[:, :, :], bkD[:, 0:GB * P].rearrange("p (b c) -> p b c", b=GB),
                                            dw("heads").rearrange("p (o c) -> p o c", o=1).to_broadcast([P, GB, P]),
                                            ALU.mult).then_inc(sem("D.Sbd"), 1)
                dve.wait_ge(*at("D.o", i, s + 1))
                nc.vector.tensor_copy(d_tm[:, :, s, :], bkA[:, 0, 0:GB * P].rearrange("p (b c) -> p b c", b=GB)).then_inc(sem("D.oc"), 1)

        attention_counts("L0", True)
        attention_counts("X0", False)
        for n, transposed in (("n0", True), ("n1", False), ("n2", True)):
            norm_counts(n, transposed)
        s_w, s_rows, s_lora, s_x, s_c, s_wi = (sem(n) for n in ("load_w", "load_rows", "load_lora", "load_x", "load_c", "load_wi"))
        s_const, s_lora_mm, s_lora_w, s_memset = (sem(n) for n in ("const", "lora_mm", "lora_w", "memset"))
        block = first.enter_context(nc.Block())
        x_view = A["x"].rearrange("(n p) c -> p n c", p=P)
        c_view = A["ctx"].rearrange("(n p) c -> p n c", p=P)
        out_view = out.rearrange("(n p) c -> p n c", p=P)

        @block.sync
        def _(sp):
            for n in range(4):
                sp.dma_start(DW[32 * n:32 * n + 32, :], A["DW"][32 * n:32 * n + 32, :]).then_inc(sem("free"), 16)
            sp.dma_start(lora[:, :], A["lora"]).then_inc(s_lora, 16)
            sp.dma_start(rows[:, :], A["rows"]).then_inc(s_rows, 16)
            sp.dma_start(W[:, :], A["W"]).then_inc(s_w, 16)
            sp.dma_start(conv_bc[:, :, :], A["conv"]).then_inc(sem("load_DW"), 16)
            sp.dma_start(Wqkv[:, :], A["Wqkv"]).then_inc(sem("load_DW"), 16)
            sp.dma_start(ffn_wi[:, :], A["ffn_w"]).then_inc(s_wi, 16)
            i = Turn(sp, "first")
            with sp.Fori(0, G) as k:
                sp.wait_ge(*at("free", i, 64))
                sp.dma_start(xg[:, :, :], x_view[:, bass.ds(k * NT, NT), :]).then_inc(sem("xg"), 16)
                sp.dma_start(cg[:, :, :], c_view[:, bass.ds(k * NT, NT), :]).then_inc(sem("cg"), 16)
                attention_sp(sp, "L0", i)
                attention_sp(sp, "X0", i)
                delta_sp(sp, k, i)
                i.next()
            sp.wait_ge(sem("free"), 64 * (G + 1))

        @block.gpsimd
        def _(pool):
            nc.gpsimd.memset(vaug[:, :, :, :], 1.0).then_inc(s_memset, 1)
            nc.gpsimd.memset(mx16[:, :, :, :], 0.0).then_inc(s_memset, 1)
            nc.gpsimd.memset(eps_ln[:, :], LN_EPS).then_inc(s_memset, 1)
            nc.gpsimd.memset(xTp[:, :, :], 0.0).then_inc(s_memset, 1)
            nc.gpsimd.memset(vTp[:, :, :], 0.0).then_inc(s_memset, 1)
            nc.gpsimd.memset(TTf[:, :, :], 0.0).then_inc(s_memset, 1)
            nc.gpsimd.memset(eps_l2[:, :], 1e-6).then_inc(s_memset, 1)
            pool.wait_ge(sem("free"), 64)
            i = Turn(pool, "first")
            with pool.Fori(0, G) as k:
                attention_pool(pool, "L0", i, True, True)
                attention_pool(pool, "X0", i, False, False)
                ffn_pool(pool, i)
                delta_pool(pool, k, i)
                i.next()

        @block.vector
        def _(dve):
            dve.wait_ge(s_w, 16)
            nc.vector.tensor_copy(ident16[:, :], ident).then_inc(s_const, 1)
            for n, name in enumerate(("mask_qk", "mask_kq")):
                nc.vector.tensor_copy(mask16[:, n, :, :], w(name).rearrange("p (o c) -> p o c", o=1).to_broadcast([P, 2, P])).then_inc(s_const, 1)
            nc.vector.tensor_copy(sel16[:, :, :], w("sel").rearrange("p (g k) -> p g k", g=HG)).then_inc(s_const, 1)
            dve.wait_ge(s_wi, 16)
            nc.vector.tensor_copy(ffn_w16[:, :], ffn_wi[:, :]).then_inc(s_const, 1)
            dve.wait_ge(s_lora_mm, 1)
            for n, name in enumerate(("L0_q", "L0_qs", "L0_v")):
                nc.vector.scalar_tensor_tensor(out=w(name), in0=bkA[:, 0, n * P:(n + 1) * P], scalar=LORA_SCALE,
                                               in1=w(name), op0=ALU.mult, op1=ALU.add).then_inc(s_lora_w, 1)
            dve.wait_ge(sem("load_DW"), 32)
            for j in range(TAPS):
                nc.vector.tensor_tensor(conv_bc[:, j, :], conv_bc[:, j, :], Wqkv[:, :], ALU.mult).then_inc(s_const, 1)
            dve.wait_ge(s_memset, 7)
            dve.wait_ge(sem("free"), 64)
            i = Turn(dve, "first")
            with dve.Fori(0, G) as k:
                attention_dve(dve, "L0", i, True, True, False)
                norm_dve(dve, "n0", i, at("L0.y", i, 1))
                attention_dve(dve, "X0", i, False, False, True)
                norm_dve(dve, "n1", i, at("X0.y", i, 1))
                ffn_dve(dve, i)
                norm_dve(dve, "n2", i, at("F.y", i, 1))
                delta_dve(dve, k, i)
                i.next()

        @block.scalar
        def _(act):
            act.wait_ge(s_memset, 7)
            i = Turn(act, "first")
            with act.Fori(0, G) as k:
                act.wait_ge(*at("xgT_ps", i, 1))
                nc.scalar.copy(xT[:, :], bkA[:, 0, :]).then_inc(sem("xgT"), 1)
                nc.scalar.copy(cT[:, :], bkA[:, 1, :]).then_inc(sem("cgT"), 1)
                attention_act(act, "L0", i, True, True)
                norm_act(act, "n0", i, xT[:, :].rearrange("c (b s) -> c b s", b=GB))
                attention_act(act, "X0", i, False, False)
                norm_act(act, "n1", i, None)
                ffn_act(act, i)
                norm_act(act, "n2", i, xTp[:, :, TAPS - 1:])
                delta_act(act, i)
                i.next()

        @block.tensor
        def _(pe):
            pe.wait_ge(s_lora, 16)
            for n, a in enumerate((0, 0, 1)):
                mm = nc.tensor.matmul(bkA[:, 0, n * P:(n + 1) * P], lora[:, a * P:(a + 1) * P],
                                      lora[:, (2 + n) * P:(3 + n) * P], start=True, stop=True)
            mm.then_inc(s_lora_mm, 1)
            pe.wait_ge(s_lora_w, 3)
            pe.wait_ge(s_rows, 16)
            pe.wait_ge(s_memset, 7)
            pe.wait_ge(sem("free"), 64)
            pe.wait_ge(s_const, 5 + TAPS)
            i = Turn(pe, "first")
            with pe.Fori(0, G) as k:
                pe.wait_ge(*at("xg", i, 16))
                pe.wait_ge(*at("cg", i, 16))
                for t in range(NT):
                    nc.tensor.transpose(bkA[:, 0, t * P:(t + 1) * P], xg[:, t, :], ident)
                for t in range(NT):
                    mm = nc.tensor.transpose(bkA[:, 1, t * P:(t + 1) * P], cg[:, t, :], ident)
                mm.then_inc(sem("xgT_ps"), 1)
                attention_pe(pe, "L0", i, at("cgT", i, 1), None, xT, True, True, False)
                norm_pe(pe, "n0", i)
                attention_pe(pe, "X0", i, at("n0.xT", i, 1), None, cT, False, False, True)
                ffn_pe(pe, i)
                norm_pe(pe, "n2", i)
                delta_pe(pe, i)
                i.next()
        first.close()

        FC = 16
        TW = P + LONG
        filt = ExitStack()
        Tz = sb("Tz", [P, 2, FC, TW], life=filt)
        V2 = sb("V2", [P, G * NT, P], life=filt)
        Vc = sb("Vc", [P, 2, G * NT, FC], life=filt)
        LL = sb("LL", [P, G * NT, P], life=filt)
        ll_d = nc.dram_tensor("long_scratch", [B * S, P], F32, kind="Internal").ap().rearrange("(n p) c -> p n c", p=P)
        BEFORE.update({n: G * PER[n] for n, _ in STEPS.values()})
        PER.clear()
        PER.update({"L.tz0": 16, "L.tz1": 16, "L.vc": 2, "L.fir": 2, "L.ll": 2})
        taps = A["taps"].rearrange("i (c j) -> i c j", j=TW)
        CHUNKS = P // FC
        block = filt.enter_context(nc.Block())

        @block.sync
        def _(sp):
            sp.dma_start(V2[:, :, :], v_d).then_inc(sem("load_v2"), 16)
            for n in range(2):
                sp.dma_start(Tz[:, n, :, :], taps[:, n * FC:(n + 1) * FC, :]).then_inc(sem(f"L.tz{n}"), 16)
            i = Turn(sp, "fir")
            with sp.Fori(0, CHUNKS // 2 - 1) as k:
                for n in range(2):
                    sp.wait_ge(*at("L.fir", i, n + 1))
                    sp.dma_start(Tz[:, n, :, :], taps[:, bass.ds(k * 2 * FC + (n + 2) * FC, FC), :]).then_inc(sem(f"L.tz{n}"), 16)
                i.next()
            sp.wait_ge(sem("L.ll"), CHUNKS)
            sp.dma_start(ll_d, LL[:, :, :]).then_inc(sem("free2"), 16)
            sp.wait_ge(sem("free2"), 16)

        @block.tensor
        def _(pe):
            i = Turn(pe, "fir")
            with pe.Fori(0, CHUNKS // 2) as k:
                for n in range(2):
                    pe.wait_ge(*at(f"L.tz{n}", i, 16))
                    pe.wait_ge(*at("L.vc", i, n + 1))
                    for c in range(FC):
                        o = bkA[:, n, c * G * NT:(c + 1) * G * NT]
                        v = Vc[:, n, :, c]
                        nc.tensor.matmul(o, Tz[:, n, c, 0:P], v, start=True, stop=False, skip_group_check=True)
                        mm = nc.tensor.matmul(o[0:LONG].rearrange("q (b s) -> q b s", s=2)[:, :, 1], Tz[:, n, c, P:TW],
                                              v.rearrange("q (b s) -> q b s", s=2)[:, :, 0], start=False, stop=True, skip_group_check=True)
                    mm.then_inc(sem("L.fir"), 1)
                i.next()

        @block.vector
        def _(dve):
            dve.wait_ge(sem("load_v2"), 16)
            i = Turn(dve, "fir")
            def gather(k, n):
                nc.vector.tensor_scalar(Vc[:, n, :, :], V2[:, :, bass.ds(k * 2 * FC + n * FC, FC)], 1.0, None, ALU.mult).then_inc(sem("L.vc"), 1)
            for n in range(2):
                gather(0, n)

            def results(k, n):
                dve.wait_ge(*at("L.fir", i, n + 1))
                nc.vector.tensor_scalar(LL[:, :, bass.ds(k * 2 * FC + n * FC, FC)],
                                        bkA[:, n, 0:FC * G * NT].rearrange("p (c t) -> p t c", c=FC), 1.0, None, ALU.mult).then_inc(sem("L.ll"), 1)
            with dve.Fori(0, CHUNKS // 2 - 1) as k:
                for n in range(2):
                    results(k, n)
                    dve.wait_ge(*at("L.ll", i, n + 1))
                    gather(k + 1, n)
                i.next()
            for n in range(2):
                results(CHUNKS // 2 - 1, n)

        filt.close()

        PER.clear()
        NE, HID = 16, 2
        for p in ("G", "O"):
            stage("N", p, {"lnv": 1, "r0": 1, "newton": 4})
        stage("A", "O", {"oT_ps": 1, "oT": 1, "oproj": 1, "y": 1})
        attention_counts("X1", False)
        for n, transposed in (("n3", True), ("n4", True), ("n5", False)):
            norm_counts(n, transposed)
        PER.update({"free2": 16, "x2": 16, "c2": 16, "src": 64, "x2T_ps": 1, "x2T": 1, "c2T": 1,
                    "G.sum": 1, "G.abs": 1, "G.mean": 1, "G.xc": 1, "G.xsq": 1, "G.ssq": 1, "G.st": 3, "G.q": 3, 
                    "G.l2": 1, "G.stT_ps": 1, "G.stT": 1, "G.h1": NH, "G.gelu": NH, "G.lg": 1,
                    "G.soft": 8, "G.pexp": 1, "G.mixD": 2, "G.mixP": 2, "G.sum2": 2, "G.o": 1, "G.osq": 1, "G.oss": 2, 
                    "G.on": 2, 
                    "M.lg": 1, "M.rt": 21, "M.ed": 1, "M.cwT_ps": 1, "M.cwT": 1, "M.b2": 1, "M.y0": 1,
                    "M.up": 2 * NE, "M.rA": NE, "M.rD": NE, "M.dn": NE, "M.mul": NE, "M.acc": NE})
        second = ExitStack()
        s2 = lambda name, shape, dt=F32: sb(name, shape, dt, life=second)
        MW = s2("MW", [P, MCOLS])
        X4 = s2("X4", [P, NT, 4, P])
        xc = s2("xc", [P, NT, 4, P])
        NS = NT * 4 * NH
        gs1, gsa, gmean, gss, gq, gqs, gqm, gln, gr0, gra, grb, gr = (s2(n, [P, NS]) for n in (
            "gs1", "gsa", "gmean", "gss", "gq", "gqs", "gqm", "gln", "gr0", "gra", "grb", "gr"))
        st = s2("st", [P, NT, NH, 32])
        stT = s2("stT", [P, T])
        h1T = s2("h1T", [P, NH, T])
        inv_temp = s2("inv_temp", [P, NH * 4])
        la, lb, lc, le, pr = (s2(n, [P, NT * NH, 4]) for n in ("la", "lb", "lc", "le", "pr"))
        lm, lsum, lrec = (s2(n, [P, NT * NH]) for n in ("lm", "lsum", "lrec"))
        xm = s2("xm", [P, NT, 4, P])
        x2s = s2("x2s", [P, NT, 2, P])
        og = s2("og", [P, NT, P])
        osq = s2("osq", [P, NT, P])
        oss, ovv, oln, or0, ora, orb, orr = (s2(n, [P, NT * NH]) for n in ("oss", "ovv", "oln", "or0", "ora", "orb", "orr"))
        on1 = s2("on1", [P, NT, P])
        on2 = s2("on2", [P, NT, P])
        rt0, rlg, rlc, oh1, oh2, ow1, ow2, cw = (s2(n, [P, NT, NE]) for n in ("rt0", "rlg", "rlc", "oh1", "oh2", "ow1", "ow2", "cw"))
        rmx = s2("rmx", [P, NT, 8])
        rix = s2("rix", [P, NT, 8], mybir.dt.uint32)
        rif = s2("rif", [P, NT, 2])
        rd, red, rsu, rw1, rw2 = (s2(n, [P, NT]) for n in ("rd", "red", "rsu", "rw1", "rw2"))
        cwT = s2("cwT", [NE, T])
        hT = s2("hT", [P, 2, HID, T])
        tmp = s2("tmp", [P, 2, NT, P])
        block = second.enter_context(nc.Block())

        def mw(name):
            return MW[:, MAT[name][0]:MAT[name][1]]

        heads = lambda a: a.rearrange("p t (h d) -> p (t h) d", d=DV)
        col = lambda a: a.rearrange("p (m o) -> p m o", o=1)

        def stat(n):
            return st[:, :, :, :].rearrange("p t h (s k) -> p t s h k", k=4)[:, :, 0:4, :, n]

        def tsh(a):
            return a[:, :].rearrange("p (t s h) -> p t s h", t=NT, s=4)

        def newton(dve, name, i, var, eps, r0_, a_, b_, out_):
            s = sem(name)
            nc.vector.scalar_tensor_tensor(out=a_[:, :], in0=var[:, :], scalar=eps, in1=r0_[:, :], op0=ALU.add, op1=ALU.mult).then_inc(s, 1)
            dve.wait_ge(*at(name, i, 1))
            nc.vector.tensor_tensor(b_[:, :], a_[:, :], r0_[:, :], ALU.mult).then_inc(s, 1)
            dve.wait_ge(*at(name, i, 2))
            nc.vector.tensor_scalar(a_[:, :], b_[:, :], -0.5, 1.5, ALU.mult, ALU.add).then_inc(s, 1)
            dve.wait_ge(*at(name, i, 3))
            nc.vector.tensor_tensor(out_[:, :], a_[:, :], r0_[:, :], ALU.mult).then_inc(s, 1)
            dve.wait_ge(*at(name, i, 4))

        def gate_dve(dve, i):
            x4 = X4[:, :, :, :].rearrange("p t s (h d) -> p (t s h) d", d=DV)
            dve.wait_ge(*at("src", i, 64))
            nc.vector.tensor_reduce(gs1[:, :], x4, AX.X, ALU.add).then_inc(sem("G.sum"), 1)
            dve.wait_ge(*at("G.sum", i, 1))
            nc.vector.tensor_scalar(gmean[:, :], gs1[:, :], 1.0 / DV, None, ALU.mult).then_inc(sem("G.mean"), 1)
            nc.vector.tensor_reduce(gsa[:, :], x4, AX.X, ALU.add, apply_absolute_value=True).then_inc(sem("G.abs"), 1)
            nc.vector.tensor_scalar(stat(0), tsh(gs1), 1.0 / DV, None, ALU.mult).then_inc(sem("G.st"), 1)
            dve.wait_ge(*at("G.mean", i, 1))
            nc.vector.tensor_tensor(gq[:, :], gs1[:, :], gmean[:, :], ALU.mult).then_inc(sem("G.q"), 1)
            dve.wait_ge(*at("G.abs", i, 1))
            nc.vector.tensor_scalar(stat(2), tsh(gsa), 1.0 / DV, None, ALU.mult).then_inc(sem("G.st"), 1)
            dve.wait_ge(*at("G.xsq", i, 1))
            nc.vector.tensor_reduce(gss[:, :], xc[:, :, :, :].rearrange("p t s (h d) -> p (t s h) d", d=DV), AX.X, ALU.add).then_inc(sem("G.ssq"), 1)
            dve.wait_ge(*at("G.ssq", i, 1))
            dve.wait_ge(*at("G.q", i, 1))
            nc.vector.tensor_scalar(stat(1), tsh(gss), 1.0 / DV, None, ALU.mult).then_inc(sem("G.st"), 1)
            nc.vector.tensor_tensor(gqs[:, :], gss[:, :], gq[:, :], ALU.add).then_inc(sem("G.q"), 1)
            dve.wait_ge(*at("G.q", i, 2))
            nc.vector.tensor_scalar(gqm[:, :], gqs[:, :], 1e-18, None, ALU.max).then_inc(sem("G.q"), 1)
            dve.wait_ge(*at("G.r0", i, 1))
            dve.wait_ge(*at("G.q", i, 3))
            newton(dve, "G.newton", i, gqm, 0.0, gr0, gra, grb, gr)
            nc.vector.tensor_tensor(stat(3), tsh(gqs), tsh(gr), ALU.mult).then_inc(sem("G.l2"), 1)
            s = sem("G.soft")
            dve.wait_ge(*at("G.lg", i, 1))
            hb = lambda a: a.rearrange("p (o h s) -> p o (h s)", o=1, s=4).to_broadcast([P, NT, NH * 4])
            f3 = lambda a: a[:, :, :].rearrange("p (t h) s -> p t (h s)", t=NT)
            nc.vector.tensor_tensor(f3(la), bkC[:, 0:NS].rearrange("p (t m) -> p t m", t=NT), hb(mw("b2")), ALU.add).then_inc(s, 1)
            dve.wait_ge(*at("G.soft", i, 1))
            nc.vector.tensor_tensor(f3(lb), f3(la), hb(inv_temp[:, :]), ALU.mult).then_inc(s, 1)
            dve.wait_ge(*at("G.soft", i, 2))
            nc.vector.tensor_reduce(lm[:, :], lb[:, :, :], AX.X, ALU.max).then_inc(s, 1)
            dve.wait_ge(*at("G.soft", i, 3))
            nc.vector.tensor_tensor(lc[:, :, :], lb[:, :, :], col(lm[:, :]).to_broadcast([P, NT * NH, 4]), ALU.subtract).then_inc(s, 1)
            dve.wait_ge(*at("G.pexp", i, 1))
            nc.vector.tensor_reduce(lsum[:, :], le[:, :, :], AX.X, ALU.add).then_inc(s, 1)
            dve.wait_ge(*at("G.soft", i, 5))
            nc.vector.reciprocal(lrec[:, :], lsum[:, :]).then_inc(s, 1)
            dve.wait_ge(*at("G.soft", i, 6))
            nc.vector.tensor_tensor(la[:, :, :], le[:, :, :], col(lrec[:, :]).to_broadcast([P, NT * NH, 4]), ALU.mult).then_inc(s, 1)
            dve.wait_ge(*at("G.soft", i, 7))
            nc.vector.tensor_scalar(pr[:, :, :], la[:, :, :], 1.0 - 4 * FLOOR, FLOOR, ALU.mult, ALU.add).then_inc(s, 1)
            dve.wait_ge(*at("G.soft", i, 8))
            for t in (0, 1):
                mix(nc.vector, t).then_inc(sem("G.mixD"), 1)
            dve.wait_ge(*at("G.sum2", i, 2))
            nc.vector.tensor_tensor(og[:, :, :], x2s[:, :, 0, :], x2s[:, :, 1, :], ALU.add).then_inc(sem("G.o"), 1)
            dve.wait_ge(*at("G.osq", i, 1))
            nc.vector.tensor_reduce(oss[:, :], heads(osq[:, :, :]), AX.X, ALU.add).then_inc(sem("G.oss"), 1)
            dve.wait_ge(*at("G.oss", i, 1))
            nc.vector.tensor_scalar(ovv[:, :], oss[:, :], 1.0 / DV, LN_EPS, ALU.mult, ALU.add).then_inc(sem("G.oss"), 1)
            dve.wait_ge(*at("O.r0", i, 1))
            dve.wait_ge(*at("G.oss", i, 2))
            newton(dve, "O.newton", i, ovv, 0.0, or0, ora, orb, orr)
            nc.vector.tensor_tensor(heads(on1[:, :, :]), heads(og[:, :, :]), col(orr[:, :]).to_broadcast([P, NT * NH, DV]), ALU.mult).then_inc(sem("G.on"), 1)
            dve.wait_ge(*at("G.on", i, 1))
            nc.vector.tensor_tensor(on2[:, :, :], on1[:, :, :], mw("onorm").rearrange("p (o c) -> p o c", o=1).to_broadcast([P, NT, P]), ALU.mult).then_inc(sem("G.on"), 1)
            dve.wait_ge(*at("O.oproj", i, 1))
            nc.vector.tensor_tensor(y[:, :, :], bkA[:, 0, :].rearrange("q (t c) -> q t c", t=NT), xg[:, :, :], ALU.add).then_inc(sem("O.y"), 1)

        def mix(eng, t):
            p = pr[:, t * NH:(t + 1) * NH, :].rearrange("p h (s o) -> p s h o", o=1).to_broadcast([P, 4, NH, DV])
            return eng.tensor_tensor(xm[:, t, :, :].rearrange("p s (h d) -> p s h d", d=DV),
                                     X4[:, t, :, :].rearrange("p s (h d) -> p s h d", d=DV), p, ALU.mult)

        def gate_pool(pool, i):
            x4 = lambda a: a[:, :, :, :].rearrange("p t s (h d) -> p (t s h) d", d=DV)
            pool.wait_ge(*at("G.mean", i, 1))
            nc.gpsimd.tensor_tensor(x4(xc), x4(X4), col(gmean[:, :]).to_broadcast([P, NS, DV]), ALU.subtract).then_inc(sem("G.xc"), 1)
            pool.wait_ge(*at("G.soft", i, 8))
            for t in (2, 3):
                mix(nc.gpsimd, t).then_inc(sem("G.mixP"), 1)
            pool.wait_ge(*at("G.mixP", i, 2))
            nc.gpsimd.tensor_tensor(x2s[:, 2:4, :, :], xm[:, 2:4, 0:2, :], xm[:, 2:4, 2:4, :], ALU.add).then_inc(sem("G.sum2"), 1)
            pool.wait_ge(*at("G.mixD", i, 2))
            nc.gpsimd.tensor_tensor(x2s[:, 0:2, :, :], xm[:, 0:2, 0:2, :], xm[:, 0:2, 2:4, :], ALU.add).then_inc(sem("G.sum2"), 1)
            pool.wait_ge(*at("G.o", i, 1))
            nc.gpsimd.tensor_tensor(osq[:, :, :], og[:, :, :], og[:, :, :], ALU.mult).then_inc(sem("G.osq"), 1)

        def gate_act(act, i):
            act.wait_ge(*at("G.xc", i, 1))
            nc.scalar.activation(xc[:, :, :, :], xc[:, :, :, :], ACT.Square).then_inc(sem("G.xsq"), 1)
            act.wait_ge(*at("G.q", i, 3))
            nc.scalar.activation(gln[:, :], gqm[:, :], ACT.Ln).then_inc(sem("G.lnv"), 1)
            act.wait_ge(*at("G.lnv", i, 1))
            nc.scalar.activation(gr0[:, :], gln[:, :], ACT.Exp, scale=-0.5).then_inc(sem("G.r0"), 1)
            act.wait_ge(*at("G.stT_ps", i, 1))
            nc.scalar.copy(stT[:, :], bkC[:, :]).then_inc(sem("G.stT"), 1)
            for h in range(NH):
                act.wait_ge(*at("G.h1", i, h + 1))
                nc.scalar.activation(h1T[:, h, :], bkB[:, h // 2, h % 2, :], ACT.Gelu, bias=mw("mlp_b1")).then_inc(sem("G.gelu"), 1)
            act.wait_ge(*at("G.soft", i, 4))
            nc.scalar.activation(le[:, :, :], lc[:, :, :], ACT.Exp).then_inc(sem("G.pexp"), 1)
            act.wait_ge(*at("G.oss", i, 2))
            nc.scalar.activation(oln[:, :], ovv[:, :], ACT.Ln).then_inc(sem("O.lnv"), 1)
            act.wait_ge(*at("O.lnv", i, 1))
            nc.scalar.activation(or0[:, :], oln[:, :], ACT.Exp, scale=-0.5).then_inc(sem("O.r0"), 1)
            act.wait_ge(*at("O.oT_ps", i, 1))
            nc.scalar.copy(oT[:, :], bkD[:, :]).then_inc(sem("O.oT"), 1)

        def gate_pe(pe, i):
            pe.wait_ge(*at("G.l2", i, 1))
            pe.wait_ge(*at("G.st", i, 3))
            for t in range(NT):
                mm = nc.tensor.transpose(bkC[:, t * P:(t + 1) * P], st[:, t, :, :].rearrange("p h c -> p (h c)"), ident)
            mm.then_inc(sem("G.stT_ps"), 1)
            pe.wait_ge(*at("x2T", i, 1))
            pe.wait_ge(*at("G.stT", i, 1))
            for h in range(NH):
                o = bkB[:, h // 2, h % 2, :]
                nc.tensor.matmul(o, mw("mlp_w1"), xT[:, :], start=True, stop=False)
                r = slice(32 * h, 32 * h + 16)
                nc.tensor.matmul(o, MW[r, MAT["mlp_w1s"][0]:MAT["mlp_w1s"][1]], stT[r, :], start=False, stop=True).then_inc(sem("G.h1"), 1)
            for h in range(NH):
                pe.wait_ge(*at("G.gelu", i, h + 1))
                for t in range(NT):
                    m = (t * NH + h) * 4
                    mm = nc.tensor.matmul(bkC[:, m:m + 4], h1T[:, h, t * P:(t + 1) * P], mw("mlp_w2"), start=True, stop=True)
            mm.then_inc(sem("G.lg"), 1)
            pe.wait_ge(*at("G.on", i, 2))
            for t in range(NT):
                mm = nc.tensor.transpose(bkD[:, t * P:(t + 1) * P], on2[:, t, :], ident)
            mm.then_inc(sem("O.oT_ps"), 1)
            pe.wait_ge(*at("O.oT", i, 1))
            for t in range(NT):
                mm = nc.tensor.matmul(bkA[:, 0, t * P:(t + 1) * P], oT[:, t * P:(t + 1) * P], mw("Wo"), start=True, stop=True)
            mm.then_inc(sem("O.oproj"), 1)

        def experts_dve(dve, i):
            s = sem("M.rt")
            rb = lambda a: a.rearrange("p (o e) -> p o e", o=1).to_broadcast([P, NT, NE])
            tb = lambda a: a.rearrange("p (t o) -> p t o", o=1).to_broadcast([P, NT, NE])
            dve.wait_ge(*at("M.lg", i, 1))
            nc.vector.tensor_tensor(rt0[:, :, :], bkC[:, 0:NT * NE].rearrange("p (t e) -> p t e", t=NT), rb(mw("bg")), ALU.add).then_inc(s, 1)
            dve.wait_ge(*at("M.rt", i, 1))
            nc.vector.tensor_tensor(rlg[:, :, :], rt0[:, :, :], rb(mw("bias")), ALU.add).then_inc(s, 1)
            dve.wait_ge(*at("M.rt", i, 2))
            nc.vector.tensor_copy(rlc[:, :, :], rlg[:, :, :]).then_inc(s, 1)
            for t in range(NT):
                nc.vector.max(rmx[:, t, :], rlg[:, t, :]).then_inc(s, 1)
            dve.wait_ge(*at("M.rt", i, 3 + NT))
            nc.vector.tensor_tensor(rd[:, :], rmx[:, :, 1], rmx[:, :, 0], ALU.subtract).then_inc(s, 1)
            for t in range(NT):
                nc.vector.max_index(rix[:, t, :], rmx[:, t, :], rlc[:, t, :]).then_inc(s, 1)
            dve.wait_ge(*at("M.ed", i, 1))
            nc.vector.tensor_scalar(rsu[:, :], red[:, :], 1.0, None, ALU.add).then_inc(s, 1)
            dve.wait_ge(*at("M.rt", i, 5 + 2 * NT))
            nc.vector.reciprocal(rw1[:, :], rsu[:, :]).then_inc(s, 1)
            dve.wait_ge(*at("M.rt", i, 14))
            nc.vector.tensor_tensor(rw2[:, :], red[:, :], rw1[:, :], ALU.mult).then_inc(s, 1)
            nc.vector.tensor_copy(rif[:, :, :], rix[:, :, 0:2]).then_inc(s, 1)
            dve.wait_ge(*at("M.rt", i, 16))
            nc.vector.tensor_tensor(oh1[:, :, :], rb(mw("iota")), tb(rif[:, :, 0]), ALU.is_equal).then_inc(s, 1)
            nc.vector.tensor_tensor(oh2[:, :, :], rb(mw("iota")), tb(rif[:, :, 1]), ALU.is_equal).then_inc(s, 1)
            dve.wait_ge(*at("M.rt", i, 18))
            nc.vector.tensor_tensor(ow1[:, :, :], oh1[:, :, :], tb(rw1[:, :]), ALU.mult).then_inc(s, 1)
            nc.vector.tensor_tensor(ow2[:, :, :], oh2[:, :, :], tb(rw2[:, :]), ALU.mult).then_inc(s, 1)
            dve.wait_ge(*at("M.rt", i, 20))
            nc.vector.tensor_tensor(cw[:, :, :], ow1[:, :, :], ow2[:, :, :], ALU.add).then_inc(s, 1)
            dve.wait_ge(*at("M.b2", i, 1))
            nc.vector.tensor_tensor(y[:, :, :], bkC[:, :].rearrange("q (t c) -> q t c", t=NT), xg[:, :, :], ALU.add).then_inc(sem("M.y0"), 1)
            for e in range(NE + 1):
                if e < NE:
                    dve.wait_ge(*at("M.up", i, 2 * e + 2))
                    if e >= 2:
                        dve.wait_ge(*at("M.dn", i, e - 1))
                    nc.vector.tensor_scalar(hT[:, e % 2, 1, :], bkB[:, e % 2, 1, :], mw("eb1")[:, 2 * e + 1:2 * e + 2], 0.0, ALU.add, ALU.max).then_inc(sem("M.rD"), 1)
                if e:
                    u = e - 1
                    dve.wait_ge(*at("M.dn", i, u + 1))
                    if u >= 2:
                        dve.wait_ge(*at("M.acc", i, u - 1))
                    nc.vector.tensor_tensor(tmp[:, u % 2, :, :], bkA[:, u % 2, :].rearrange("q (t c) -> q t c", t=NT),
                                            cw[:, :, u:u + 1].to_broadcast([P, NT, P]), ALU.mult).then_inc(sem("M.mul"), 1)

        def experts_act(act, i):
            act.wait_ge(*at("M.rt", i, 4 + NT))
            nc.scalar.activation(red[:, :], rd[:, :], ACT.Exp).then_inc(sem("M.ed"), 1)
            act.wait_ge(*at("M.cwT_ps", i, 1))
            nc.scalar.copy(cwT[:, :], bkD[0:NE, :]).then_inc(sem("M.cwT"), 1)
            for e in range(NE):
                act.wait_ge(*at("M.up", i, 2 * e + 1))
                if e >= 2:
                    act.wait_ge(*at("M.dn", i, e - 1))
                nc.scalar.activation(hT[:, e % 2, 0, :], bkB[:, e % 2, 0, :], ACT.Relu, bias=mw("eb1")[:, 2 * e:2 * e + 1]).then_inc(sem("M.rA"), 1)

        def experts_pool(pool, i):
            pool.wait_ge(*at("M.y0", i, 1))
            for e in range(NE):
                pool.wait_ge(*at("M.mul", i, e + 1))
                if e:
                    pool.wait_ge(*at("M.acc", i, e))
                nc.gpsimd.tensor_tensor(y[:, :, :], y[:, :, :], tmp[:, e % 2, :, :], ALU.add).then_inc(sem("M.acc"), 1)

        def experts_pe(pe, i):
            pe.wait_ge(*at("n4.xT", i, 1))
            for t in range(NT):
                mm = nc.tensor.matmul(bkC[:, t * NE:(t + 1) * NE], xT[:, t * P:(t + 1) * P], mw("Wg"), start=True, stop=True)
            mm.then_inc(sem("M.lg"), 1)

            def up(e):
                for f in range(HID):
                    if e >= 2:
                        pe.wait_ge(*at("M.rD" if f else "M.rA", i, e - 1))
                    c = MAT["W1"][0] + (e * HID + f) * P
                    nc.tensor.matmul(bkB[:, e % 2, f, :], MW[:, c:c + P], xT[:, :], start=True, stop=True).then_inc(sem("M.up"), 1)

            def down(e):
                pe.wait_ge(*at("M.rA", i, e + 1))
                pe.wait_ge(*at("M.rD", i, e + 1))
                if e >= 2:
                    pe.wait_ge(*at("M.mul", i, e - 1))
                for t in range(NT):
                    for f in range(HID):
                        c = MAT["W2"][0] + (e * HID + f) * P
                        mm = nc.tensor.matmul(bkA[:, e % 2, t * P:(t + 1) * P], hT[:, e % 2, f, t * P:(t + 1) * P], MW[:, c:c + P],
                                              start=f == 0, stop=f == HID - 1)
                mm.then_inc(sem("M.dn"), 1)
            up(0)
            up(1)
            pe.wait_ge(*at("M.rt", i, 21))
            for t in range(NT):
                mm = nc.tensor.transpose(bkD[0:NE, t * P:(t + 1) * P], cw[:, t, :], ident)
            mm.then_inc(sem("M.cwT_ps"), 1)
            pe.wait_ge(*at("M.cwT", i, 1))
            for t in range(NT):
                mm = nc.tensor.matmul(bkC[:, t * P:(t + 1) * P], cwT[0:NE, t * P:(t + 1) * P], MW[0:NE, MAT["eb2"][0]:MAT["eb2"][1]], start=True, stop=True)
            mm.then_inc(sem("M.b2"), 1)
            for e in range(NE):
                down(e)
                if e + 2 < NE:
                    up(e + 2)

        @block.sync
        def _(sp):
            for n in range(4):
                r = slice(32 * n, 32 * n + 32)
                sp.dma_start(MW[r, :], A["MW"][r, :]).then_inc(sem("load_MW"), 16)
            i = Turn(sp, "second")
            with sp.Fori(0, G) as k:
                tiles = bass.ds(k * NT, NT)
                sp.wait_ge(*at("free2", i, 16))
                sp.dma_start(xg[:, :, :], x3_d[:, tiles, :]).then_inc(sem("x2"), 16)
                for n, src in enumerate((sh_d, ll_d, dl_d, v_d)):
                    sp.dma_start(X4[:, :, n, :], src[:, tiles, :]).then_inc(sem("src"), 16)
                sp.dma_start(cg[:, :, :], c_view[:, tiles, :]).then_inc(sem("c2"), 16)
                attention_sp(sp, "X1", i)
                sp.wait_ge(*at("n5.x", i, NT))
                sp.dma_start(out_view[:, tiles, :], xg[:, :, :]).then_inc(sem("free2"), 16)
                i.next()
            sp.wait_ge(sem("free2"), 16 * (G + 1))

        @block.gpsimd
        def _(pool):
            nc.gpsimd.memset(st[:, :, :, :], 0.0).then_inc(sem("st_zero"), 1)
            i = Turn(pool, "second")
            with pool.Fori(0, G) as k:
                gate_pool(pool, i)
                attention_pool(pool, "X1", i, False, True)
                experts_pool(pool, i)
                i.next()

        @block.vector
        def _(dve):
            dve.wait_ge(sem("load_MW"), 64)
            dve.wait_ge(sem("st_zero"), 1)
            dve.wait_ge(sem("inv_temp"), 1)
            i = Turn(dve, "second")
            with dve.Fori(0, G) as k:
                gate_dve(dve, i)
                norm_dve(dve, "n3", i, at("O.y", i, 1))
                attention_dve(dve, "X1", i, False, True, True)
                norm_dve(dve, "n4", i, at("X1.y", i, 1))
                experts_dve(dve, i)
                norm_dve(dve, "n5", i, at("M.acc", i, NE))
                i.next()

        @block.scalar
        def _(act):
            act.wait_ge(sem("load_MW"), 64)
            nc.scalar.activation(inv_temp[:, :], mw("log_temp"), ACT.Exp, scale=-1.0).then_inc(sem("inv_temp"), 1)
            i = Turn(act, "second")
            with act.Fori(0, G) as k:
                act.wait_ge(*at("x2T_ps", i, 1))
                nc.scalar.copy(xT[:, :], bkA[:, 0, :]).then_inc(sem("x2T"), 1)
                nc.scalar.copy(cT[:, :], bkA[:, 1, :]).then_inc(sem("c2T"), 1)
                gate_act(act, i)
                norm_act(act, "n3", i, xT[:, :].rearrange("c (b s) -> c b s", b=GB))
                attention_act(act, "X1", i, False, True)
                norm_act(act, "n4", i, xT[:, :].rearrange("c (b s) -> c b s", b=GB))
                experts_act(act, i)
                norm_act(act, "n5", i, None)
                i.next()

        @block.tensor
        def _(pe):
            pe.wait_ge(sem("load_MW"), 64)
            pe.wait_ge(sem("st_zero"), 1)
            i = Turn(pe, "second")
            with pe.Fori(0, G) as k:
                pe.wait_ge(*at("x2", i, 16))
                pe.wait_ge(*at("c2", i, 16))
                for t in range(NT):
                    nc.tensor.transpose(bkA[:, 0, t * P:(t + 1) * P], xg[:, t, :], ident)
                for t in range(NT):
                    mm = nc.tensor.transpose(bkA[:, 1, t * P:(t + 1) * P], cg[:, t, :], ident)
                mm.then_inc(sem("x2T_ps"), 1)
                gate_pe(pe, i)
                norm_pe(pe, "n3", i)
                attention_pe(pe, "X1", i, at("n3.xT", i, 1), at("c2T", i, 1), cT, False, True, True)
                norm_pe(pe, "n4", i)
                experts_pe(pe, i)
                i.next()

        second.close()


def _layout(inputs):
    f = lambda n: np.asarray(inputs[n], dtype=None)
    dh = np.array([h * DH + d for d in range(DH) for h in range(H)])
    dh_swap = np.array([h * DH + (d ^ 1) for d in range(DH) for h in range(H)])
    W = np.zeros((P, NCOLS), np.float32)

    def put(name, a):
        W[:, AT[name][0]:AT[name][1]] = a

    put("ident", np.eye(P, dtype=np.float32))
    theta = (np.arange(S, dtype=np.float32)[:, None]
             / np.float32(10000.0) ** (np.arange(0, DH, 2, dtype=np.float32) / np.float32(DH))[None, :]).astype(np.float32)
    sin, cos = np.sin(theta), np.cos(theta)
    for d in range(DH):
        r = slice(d * H, (d + 1) * H)
        W[r, AT["rope_c"][0]:AT["rope_c"][1]] = cos[:, d // 2]
        W[r, AT["rope_s"][0]:AT["rope_s"][1]] = sin[:, d // 2] if d % 2 else -sin[:, d // 2]
    put("mask_qk", np.triu(np.full((P, P), MASKED, np.float32), 1))
    put("mask_kq", np.tril(np.full((P, P), MASKED, np.float32), -1))
    sel = np.zeros((P, HG, P), np.float32)
    for a in range(HP):
        for j in range(3):
            for g in range(HG):
                sel[64 * a + HG * j + g, g, :] = 1.0
    put("sel", sel.reshape(P, -1))
    put("L0_q", f("L0_attn_wq")[:, dh]); put("L0_qs", f("L0_attn_wq")[:, dh_swap])
    put("L0_k", f("L0_attn_wk")[:, dh]); put("L0_ks", f("L0_attn_wk")[:, dh_swap])
    put("L0_v", f("L0_attn_wv")); put("L0_o", f("L0_attn_wo"))
    for n, names in (("X0", ("W_Q", "W_K", "W_V", "W_O", "b_Q", "b_K")), ("X1", ("Wq", "Wk", "Wv", "Wo", "bq", "bk"))):
        m = ("L0" if n == "X0" else "L1") + "_xattn_"
        put(n + "_q", f(m + names[0])[:, dh]); put(n + "_k", f(m + names[1])[:, dh])
        put(n + "_v", f(m + names[2])); put(n + "_o", f(m + names[3]))
        put(n + "_bq", f(m + names[4])[dh][:, None]); put(n + "_bk", f(m + names[5])[dh][:, None])
    put("ffn_ws", np.broadcast_to(f("L0_ffn_weight_scale"), (P, P))); put("ffn_b", np.broadcast_to(f("L0_ffn_bias"), (P, P)))
    rows = np.zeros((1, NROWS), np.float32)
    for n, m in (("X0_bv", "L0_xattn_b_V"), ("X0_bo", "L0_xattn_b_O"), ("X1_bv", "L1_xattn_bv"), ("X1_bo", "L1_xattn_bo")):
        rows[0, RAT[n][0]:RAT[n][1]] = f(m)
    rows[0, RAT["ones"][0]:RAT["ones"][1]] = 1.0
    lora = np.concatenate([f("L0_attn_Aq").T, f("L0_attn_Av").T, f("L0_attn_Bq")[:, dh], f("L0_attn_Bq")[:, dh_swap],
                           f("L0_attn_Bv")], axis=1)
    return {"x": f("x").reshape(B * S, P), "ctx": f("ctx_1024").reshape(B * S, P), "W": W, "rows": rows,
            "lora": np.ascontiguousarray(lora), "ffn_w": np.ascontiguousarray(f("L0_ffn_weight_q").T.astype(np.int32)), **_layout2(inputs)}


def _layout2(inputs):
    f = lambda n: np.asarray(inputs[n])
    D = np.zeros((P, DCOLS), np.float32)

    def put(name, a):
        D[:, DAT[name][0]:DAT[name][1]] = a

    j, i = np.arange(P)[:, None], np.arange(P)[None, :]
    put("Wb", f("L1_attn_Wb"))
    put("ident32", (j % 32 == np.arange(32)[None, :]).astype(np.float32))
    put("mask2", np.concatenate([(i > j), (i >= j)], axis=1).astype(np.float32))
    put("off", ((i > j) & (i // 32 != j // 32)).astype(np.float32))
    put("heads", (i // 32 == j // 32).astype(np.float32))
    for l in range(5):
        n = 2 << l
        put(f"level{l}", ((i > j) & (i // n == j // n) & (i // (n // 2) != j // (n // 2))).astype(np.float32))
    short = np.zeros((P, 5, P), np.float32)
    for k in range(5):
        short[np.arange(P), k, np.arange(P)] = f("L1_attn_fir_short_w").reshape(P, 5)[:, k]
    put("short", short.reshape(P, -1))
    conv = np.concatenate([f("L1_attn_conv_q_w"), f("L1_attn_conv_k_w"), f("L1_attn_conv_v_w")]).T
    M = np.zeros((P, MCOLS), np.float32)

    def putm(name, a, r=slice(None)):
        M[r, MAT[name][0]:MAT[name][1]] = a

    w1 = f("L1_attn_mlp_w1")
    putm("mlp_w1", w1[:P])
    for h in range(4):
        putm("mlp_w1s", w1[P:], slice(32 * h, 32 * h + 16))
    putm("mlp_w2", f("L1_attn_mlp_w2"))
    putm("mlp_b1", f("L1_attn_mlp_b1")[:, None])
    putm("b2", np.tile(f("L1_attn_mlp_b2"), 4))
    putm("log_temp", np.repeat(f("L1_attn_log_temp").reshape(4), 4))
    putm("onorm", np.tile(f("L1_attn_o_norm_w"), 4))
    putm("Wo", f("L1_attn_Wo"))
    putm("Wg", f("L1_ffn_Wg")); putm("bg", f("L1_ffn_bg")); putm("bias", f("L1_ffn_bias"))
    putm("iota", np.arange(16, dtype=np.float32))
    putm("eb1", f("L1_ffn_b1").reshape(32, P).T)
    putm("eb2", f("L1_ffn_b2"), slice(0, 16))
    putm("W1", f("L1_ffn_W1").transpose(1, 0, 2).reshape(P, -1))
    putm("W2", f("L1_ffn_W2").reshape(16, 2, P, P).transpose(2, 0, 1, 3).reshape(P, -1))
    taps = np.zeros((P, P, P + 64), np.float32)
    for r in range(P):
        taps[r, :, r:r + 64] = f("L1_attn_fir_long_w").reshape(P, 64)[:, ::-1]
    return {"MW": M, "taps": taps.reshape(P, -1), "DW": D, "conv": np.ascontiguousarray(np.broadcast_to(conv[None], (P, 4, 3 * P))),
            "Wqkv": np.concatenate([f("L1_attn_Wq"), f("L1_attn_Wk"), f("L1_attn_Wv")], axis=1)}


def kernel(**inputs):
    import numpy as _np
    import concourse.bacc as _bacc
    from concourse import mybir as _mybir
    from concourse.bass_utils import run_bass_kernel_spmd as _run

    nc = _bacc.Bacc("TRN2", target_bir_lowering=False, num_devices=1)
    arrays = _layout(inputs)
    A = {n: nc.dram_tensor("in_" + n, a.shape, _mybir.dt.from_np(a.dtype), kind="ExternalInput").ap()
         for n, a in arrays.items()}
    out = nc.dram_tensor("out_x", (B * S, P), _mybir.dt.float32, kind="ExternalOutput").ap()
    decoder(nc, A, out)
    r = _run(nc, [{"in_" + n: a for n, a in arrays.items()}], core_ids=[0])
    return r.results[0]["out_x"].reshape(B, S, P)
```

```python
from contextlib import ExitStack

import concourse.bass as bass
import numpy as np
from concourse import mybir

F32 = mybir.dt.float32
BF16 = mybir.dt.bfloat16
I32 = mybir.dt.int32
ACT = mybir.ActivationFunctionType
ALU = mybir.AluOpType
AX = mybir.AxisListType

P = 128
B, S = 8, 256
GB = 2
G = B // GB
T = GB * S
NT = T // P
H, DH = 16, 8
HP, HG = 2, 8
SLOTS = 6
UNITS = 2 * GB
SCALE = 1.0 / float(np.sqrt(DH))
LN_EPS = 1e-5
LORA_SCALE = 4.0
MASKED = -1e30

COLS = [
    ("ident", P), ("rope_c", S), ("rope_s", S), 
    ("L0_q", P), ("L0_qs", P), ("L0_k", P), ("L0_ks", P), ("L0_v", P), ("L0_o", P),
    ("X0_q", P), ("X0_k", P), ("X0_v", P), ("X0_o", P), ("X0_bq", 1), ("X0_bk", 1),
    ("X1_q", P), ("X1_k", P), ("X1_v", P), ("X1_o", P), ("X1_bq", 1), ("X1_bk", 1),
    ("mask_qk", P), ("mask_kq", P), ("sel", HG * P),
    ("ffn_ws", P), ("ffn_b", P),
]
AT = {}
_n = 0
for _name, _w in COLS:
    AT[_name] = (_n, _n + _w)
    _n += _w
NCOLS = _n
ROWS = [("X0_bv", P), ("X0_bo", P), ("X1_bv", P), ("X1_bo", P), ("ones", P)]
RAT = {}
_n = 0
for _name, _w in ROWS:
    RAT[_name] = (_n, _n + _w)
    _n += _w
NROWS = _n
DCOLS_ = [("Wb", 4), ("ident32", 32), ("mask2", 2 * P), ("off", P), ("heads", P), ("short", 5 * P)] + [
    (f"level{l}", P) for l in range(5)]
DAT = {}
_n = 0
for _name, _w in DCOLS_:
    DAT[_name] = (_n, _n + _w)
    _n += _w
DCOLS = _n
FLOOR = 0.05
MCOLS_ = [("mlp_w1", P), ("mlp_w1s", P), ("mlp_w2", 4), ("mlp_b1", 1), ("b2", 16), ("log_temp", 16), ("onorm", P), ("Wo", P),
          ("Wg", 16), ("bg", 16), ("bias", 16), ("iota", 16), ("pick", 16), ("eb1", 32), ("eb2", P), ("W1", 16 * 2 * P), ("W2", 16 * 2 * P)]
MAT = {}
_n = 0
for _name, _w in MCOLS_:
    MAT[_name] = (_n, _n + _w)
    _n += _w
MCOLS = _n
NLORA = 5 * P

PER = {}
STEPS, STAGE, BEFORE = {}, {}, {}


class Turn:

    def __init__(self, eng, loop, start=0):
        self.eng, self.start, self.done = eng, start, {}
        self.tmp = [eng.alloc_register(f"wait_{loop}_{k}") for k in range(4)]
        self.n = 0
        for per in sorted(set(PER.values())):
            self.done[per] = eng.alloc_register(f"done_{loop}_{per}")
            eng.reg_mov(self.done[per], start * per)

    def value(self, per, n):
        self.n += 1
        r = self.tmp[self.n % len(self.tmp)]
        self.eng.reg_add(r, self.done[per], n)
        return r

    def next(self):
        for per, r in self.done.items():
            self.eng.reg_add(r, r, per)


def decoder(nc, A, out):
    ctx = ExitStack()
    with ctx:
        def sb(name, shape, dt=F32, life=None):
            return (life or ctx).enter_context(nc.sbuf_tensor(name, shape, dt))

        sems = {}

        def sem(name):
            name = STEPS[name][0] if name in STEPS else name
            if name not in sems:
                sems[name] = ctx.enter_context(nc.semaphore("s_" + name.replace(".", "_")))
            return sems[name]

        def at(name, i, n, later=0):
            if name not in STEPS:
                return sem(name), i.value(PER[name], n + later * PER[name])
            kind, earlier = STEPS[name]
            return sem(name), i.value(PER[kind], n + earlier + later * PER[kind] + BEFORE.get(kind, 0))

        def stage(kind, prefix, counts):
            for signal, n in counts.items():
                shared = f"{kind}.{signal}"
                STEPS[f"{prefix}.{signal}"] = (shared, PER.get(shared, 0))
                STAGE[f"{prefix}.{signal}"] = n
                PER[shared] = PER.get(shared, 0) + n

        bkA = ctx.enter_context(nc.psum_tensor("bkA", [P, 2, 512], F32))
        bkB = ctx.enter_context(nc.psum_tensor("bkB", [P, 2, 2, 512], F32))
        bkC = ctx.enter_context(nc.psum_tensor("bkC", [P, 512], F32))
        bkD = ctx.enter_context(nc.psum_tensor("bkD", [P, 512], F32))
        bkD16 = bkD[:, :].bitcast(BF16)
        bkA16 = bkA[:, 0, :].bitcast(BF16)
        rows_bank = lambda b, j, qt: bkB[:, 0, qt, :] if b == 0 and j % 2 else bkA[:, qt, :]
        unit_bank = lambda m: (bkC, bkD)[m % 2]

        W = sb("W", [P, NCOLS])
        rows = sb("rows", [1, NROWS])
        lora = sb("lora", [8, NLORA])
        ident16 = sb("ident16", [P, P], BF16)
        mask16 = sb("mask16", [P, 2, 2, P], BF16)
        sel16 = sb("sel16", [P, HG, P], BF16)
        ffn_wi = sb("ffn_wi", [P, P], I32)
        ffn_w16 = sb("ffn_w16", [P, P], BF16)

        def w(name):
            return W[:, AT[name][0]:AT[name][1]]

        def row(name):
            return rows[0:1, RAT[name][0]:RAT[name][1]]

        ident = w("ident")

        xg = sb("xg", [P, NT, P])
        xn = sb("xn", [P, NT, P])
        cg = sb("cg", [P, NT, P])
        xT = sb("xT", [P, T])
        cT = sb("cT", [P, T])
        y = sb("y", [P, NT, P])

        qf = sb("qf", [P, 2, T])
        rt = sb("rt", [P, 2, T])
        part = sb("part", [P, 2, 3, T], BF16)
        resid = sb("resid", [P, 2, T])
        stk = sb("stk", [P, 2, HG, T], BF16)
        vaug = sb("vaug", [P, NT, H, 32])
        oe = sb("oe", [P, 2, 512])
        mx = sb("mx", [P, GB, 2, HP, HG])
        mr = sb("mr", [P, 2, 2, HP, HG])
        mx16 = sb("mx16", [P, 2, HP, 64], BF16)
        nmT = sb("nmT", [P, 2, P], BF16)
        pT = sb("pT", [P, 2, 2 * 2 * S])
        rec = sb("rec", [P, 2, 2, 2, 4])
        o_tm = sb("o_tm", [P, NT, H, DH])
        oT = sb("oT", [P, T])

        eps_ln = sb("eps_ln", [P, 1])
        bst = sb("bst", [P, NT, 6])
        bsum, bdif, bsq, bd2, mean, var = (sb(n, [P, NT]) for n in ("bsum", "bdif", "bsq", "bd2", "mean", "var"))
        root = sb("root", [P, NT])
        r0 = sb("r0", [P, NT])
        ra = sb("ra", [P, NT])
        rb = sb("rb", [P, NT])
        rstd = sb("rstd", [P, NT])

        am = sb("am", [P, NT])
        rxs = sb("rxs", [P, NT])
        xs = sb("xs", [P, NT])
        xq = sb("xq", [P, NT, P])
        xq16 = sb("xq16", [P, NT, P], BF16)
        xqT = sb("xqT", [P, T], BF16)
        fo = rt[:, 0, :].rearrange("p (t c) -> p t c", t=NT)

        scratch = nc.dram_tensor("stack_scratch", [2, 3 * P, T], BF16, kind="Internal").ap()
        x3_d, v_d, dl_d, sh_d = (nc.dram_tensor(n, [B * S, P], F32, kind="Internal").ap().rearrange("(n p) c -> p n c", p=P)
                                 for n in ("x3_scratch", "v_scratch", "delta_scratch", "short_scratch"))

        PER.update({"free": 64})

        def attention_counts(p, rope):
            if not rope:
                stage("A", p, {"proj": 2, "rot": 2, "parts": 4, "rest": 2, "qrest": 2, "scr0": 16, "scr1": 16, "stk": 18 * 16})
            stage("A", p, {
                "vproj": 1, "v": 1,
                "s1": 4 * H // 2, "max": 4 * H // 2, "mparts": 2 * 5, "nmT_ps": 2,
                "nmT": 2, "s2": H, "exp": H, "pv": H,
                "ov": UNITS, "ot": UNITS, "rec": UNITS, "o": UNITS, "oT_ps": 1, "oT": 1, "oproj": 1, "y": 1})

        def norm_counts(p, transposed):
            stage("N", p, {"bst": NT, "mv": 6, "root": 1, "r0": 1, "newton": 4, "x": NT})
            if transposed:
                stage("N", p, {"xT_ps": 1, "xT": 1})

        def attention_pe(pe, p, i, q_ready, kvT, rope, causal, bias, keys_of=None):
            if rope:
                pe.wait_ge(*at("P.xT", i, 1))
            else:
                pe.wait_ge(*q_ready)
                nc.tensor.matmul(bkA[:, 0, :], w(f"{p}_q"), xT[:, :], start=True, stop=True).then_inc(sem(f"{p}.proj"), 1)
            for t in range(NT):
                o = bkB[:, 1, 0, t * P:(t + 1) * P]
                if bias:
                    nc.tensor.matmul(o, row("ones"), row(f"{p}_bv"), start=True, stop=False)
                mm = nc.tensor.matmul(o, kvT[:, t * P:(t + 1) * P], w(f"{p}_v"), start=not bias, stop=True)
            mm.then_inc(sem(f"{p}.vproj"), 1)
            if rope:
                pe.wait_ge(*at("P.stk", i, PER["P.stk"]))
            else:
                pe.wait_ge(*at(f"{p}.stk", i, STAGE[f"{p}.stk"]))
                pe.wait_ge(*at(f"{p}.rot", i, 2))
            if keys_of:
                keys_pe(pe, keys_of, i)

            def score_rows(b, j, n):
                hp, g = j % 2, j // 2 * 2
                for qt in range(2):
                    kw = P if causal and qt == 0 else S
                    free = 2 * (n - (1 if b else 2)) + qt + 1
                    if free > 0:
                        pe.wait_ge(*at(f"{p}.max", i, free))
                    o = rows_bank(b, j, qt)[:, 0:2 * kw].rearrange("q (h k) -> q h k", h=2)
                    for hh in range(2):
                        r = slice(64 * hp, 64 * hp + SLOTS * DH)
                        c0 = b * S + qt * P
                        mm = nc.tensor.matmul(o[:, hh, :], stk[r, 0, g + hh, c0:c0 + P],
                                              stk[r, 1, g + hh, b * S:b * S + kw],
                                              start=hh == 0, stop=not causal and hh == 1, skip_group_check=True)
                    if causal:
                        mm = nc.tensor.matmul(o[:, :, kw - P:kw], ident16[:, :], mask16[:, 0, :, :],
                                              start=False, stop=True, skip_group_check=True)
                    mm.then_inc(sem(f"{p}.s1"), 1)

            def max_rows(b):
                pe.wait_ge(*at(f"{p}.mparts", i, 5 * (b + 1)))
                for qt in range(2):
                    mm = nc.tensor.transpose(bkA16[:, qt * P:(qt + 1) * P],
                                             mx16[:, qt, :, :].rearrange("q a c -> q (a c)"), ident16[:, :])
                mm.then_inc(sem(f"{p}.nmT_ps"), 1)

            def score_cols(b, j, n):
                hp, g = j % 2, j // 2 * 2
                if n >= 2:
                    pe.wait_ge(*at(f"{p}.exp", i, n - 1))
                for kt in range(2):
                    q0 = P if causal and kt else 0
                    for hh in range(2):
                        o = bkB[:, n % 2, kt, hh * (S - q0):(hh + 1) * (S - q0)]
                        r = slice(64 * hp, 64 * hp + 3 * HG)
                        nc.tensor.matmul(o, sel16[r, g + hh, :],
                                         nmT[r, :, :].rearrange("c t q -> c (t q)")[:, q0:S],
                                         start=hh == 0, stop=False, skip_group_check=True)
                        r = slice(64 * hp, 64 * hp + SLOTS * DH)
                        mm = nc.tensor.matmul(o, stk[r, 1, g + hh, b * S + kt * P:b * S + (kt + 1) * P],
                                              stk[r, 0, g + hh, b * S + q0:(b + 1) * S],
                                              start=False, stop=not causal and hh == 1, skip_group_check=True)
                    if causal:
                        o = bkB[:, n % 2, kt, 0:2 * (S - q0)].rearrange("k (h q) -> k h q", h=2)[:, :, 0:P]
                        mm = nc.tensor.matmul(o, ident16[:, :], mask16[:, 1, :, :], start=False, stop=True, skip_group_check=True)
                mm.then_inc(sem(f"{p}.s2"), 1)

            def weigh_values(b, j, n):
                hp, g, m = j % 2, j // 2 * 2, n // 4
                pe.wait_ge(*at(f"{p}.exp", i, n + 1))
                if n == 0:
                    pe.wait_ge(*at(f"{p}.v", i, 1))
                if n % 4 == 0 and m >= 2:
                    pe.wait_ge(*at(f"{p}.o", i, m - 1))
                for hh in range(2):
                    c = g % 4 + hh
                    for kt in range(2):
                        q0 = P if causal and kt else 0
                        at0 = kt * 512 + hh * (S - q0)
                        mm = nc.tensor.matmul(unit_bank(m)[32 * c:32 * c + 32, hp * S + q0:(hp + 1) * S],
                                              vaug[:, 2 * b + kt, hp * HG + g + hh, :], pT[:, n % 2, at0:at0 + S - q0],
                                              start=kt == 0, stop=kt == 1, skip_group_check=True)
                mm.then_inc(sem(f"{p}.pv"), 1)

            def unit_rows(m):
                pe.wait_ge(*at(f"{p}.ov", i, m + 1))
                for x in range(4):
                    mm = nc.tensor.transpose(unit_bank(m)[:, x * P:(x + 1) * P], oe[:, m % 2, x * P:(x + 1) * P], ident)
                mm.then_inc(sem(f"{p}.ot"), 1)

            pairs = H // 2
            for j in range(pairs):
                score_rows(0, j, j)
            if keys_of:
                pe.wait_ge(*at(f"{keys_of}.rot", i, 1))
            for b in range(GB):
                max_rows(b)
                pe.wait_ge(*at(f"{p}.nmT", i, b + 1))
                if b == 0:
                    pe.wait_ge(*at(f"{p}.v", i, 1))
                for j in range(pairs):
                    n = b * pairs + j
                    score_cols(b, j, n)
                    if b + 1 < GB:
                        score_rows(b + 1, j, n + pairs)
                    if j:
                        weigh_values(b, j - 1, n - 1)
                    if n > 4 and n % 4 == 1:
                        unit_rows(n // 4 - 1)
                weigh_values(b, pairs - 1, n)
            unit_rows(UNITS - 1)

            pe.wait_ge(*at(f"{p}.o", i, UNITS))
            for t in range(NT):
                mm = nc.tensor.transpose(bkD[:, t * P:(t + 1) * P], o_tm[:, t, :, :].rearrange("q h d -> q (h d)"), ident)
            mm.then_inc(sem(f"{p}.oT_ps"), 1)
            pe.wait_ge(*at(f"{p}.oT", i, 1))
            for t in range(NT):
                o = bkA[:, 0, t * P:(t + 1) * P]
                if bias:
                    nc.tensor.matmul(o, row("ones"), row(f"{p}_bo"), start=True, stop=False)
                mm = nc.tensor.matmul(o, oT[:, t * P:(t + 1) * P], w(f"{p}_o"), start=not bias, stop=True)
            mm.then_inc(sem(f"{p}.oproj"), 1)

        def attention_dve(dve, p, i, rope, causal, bias, keys_of=None):
            if not rope:
                dve.wait_ge(*at(f"{p}.proj", i, 2))
                nc.vector.tensor_scalar(qf[:, 0, :], bkA[:, 0, :], w(f"{p}_bq"), None, ALU.add).then_inc(sem(f"{p}.rot"), 1)
                dve.wait_ge(*at(f"{p}.parts", i, 3))
                nc.vector.tensor_tensor(resid[:, 0, :], qf[:, 0, :], part[:, 0, 0, :], ALU.subtract).then_inc(sem(f"{p}.qrest"), 1)
                dve.wait_ge(*at(f"{p}.parts", i, 4))
                nc.vector.tensor_tensor(part[:, 0, 2, :], resid[:, 0, :], part[:, 0, 1, :], ALU.subtract).then_inc(sem(f"{p}.qrest"), 1)
            if keys_of:
                keys_dve(dve, keys_of, i)

            def maxima(b, j, n):
                hp, g = j % 2, j // 2 * 2
                for qt in range(2):
                    u = 2 * n + qt
                    kw = P if causal and qt == 0 else S
                    dve.wait_ge(*at(f"{p}.s1", i, u + 1))
                    nc.vector.tensor_reduce(mx[:, b, qt, hp, g:g + 2],
                                            rows_bank(b, j, qt)[:, 0:2 * kw].rearrange("q (h k) -> q h k", h=2),
                                            AX.X, ALU.max).then_inc(sem(f"{p}.max"), 1)

            def max_parts(b):
                s, m = sem(f"{p}.mparts"), mx[:, b, :, :, :]
                dve.wait_ge(*at(f"{p}.max", i, 16 * (b + 1)))
                if b:
                    dve.wait_ge(*at(f"{p}.nmT_ps", i, b))
                nc.vector.tensor_copy(mx16[:, :, :, 0:8], m).then_inc(s, 1)
                dve.wait_ge(*at(f"{p}.mparts", i, 5 * b + 1))
                nc.vector.tensor_tensor(mr[:, 0], m, mx16[:, :, :, 0:8], ALU.subtract).then_inc(s, 1)
                dve.wait_ge(*at(f"{p}.mparts", i, 5 * b + 2))
                nc.vector.tensor_copy(mx16[:, :, :, 8:16], mr[:, 0]).then_inc(s, 1)
                dve.wait_ge(*at(f"{p}.mparts", i, 5 * b + 3))
                nc.vector.tensor_tensor(mr[:, 1], mr[:, 0], mx16[:, :, :, 8:16], ALU.subtract).then_inc(s, 1)
                dve.wait_ge(*at(f"{p}.mparts", i, 5 * b + 4))
                nc.vector.tensor_copy(mx16[:, :, :, 16:24], mr[:, 1]).then_inc(s, 1)

            def unit_out(m):
                dve.wait_ge(*at(f"{p}.pv", i, 4 * (m + 1)))
                if m >= 2:
                    dve.wait_ge(*at(f"{p}.ot", i, m - 1))
                nc.vector.tensor_copy(oe[:, m % 2, :], unit_bank(m)[:, :]).then_inc(sem(f"{p}.ov"), 1)

            def normalise(m):
                b, f = m // 2, m % 2
                acc = unit_bank(m)[:, :].rearrange("q (s t c v) -> q s t c v", s=2, t=2, v=32)
                dve.wait_ge(*at(f"{p}.ot", i, m + 1))
                nc.vector.reciprocal(rec[:, m % 2, :, :, :], acc[:, :, :, :, DH]).then_inc(sem(f"{p}.rec"), 1)
                dve.wait_ge(*at(f"{p}.rec", i, m + 1))
                for t in range(2):
                    o = nc.vector.tensor_tensor(o_tm[:, 2 * b + t, :, :].rearrange("q (s f c) d -> q f s c d", s=2, f=2)[:, f],
                                                acc[:, :, t, :, 0:DH],
                                                rec[:, m % 2, :, t, :].rearrange("q s (c o) -> q s c o", o=1).to_broadcast([P, 2, 4, DH]),
                                                ALU.mult)
                o.then_inc(sem(f"{p}.o"), 1)
            pairs = H // 2
            for j in range(pairs):
                maxima(0, j, j)
            max_parts(0)
            for j in range(pairs):
                maxima(1, j, j + pairs)
                if j == 4:
                    unit_out(0)
                if j == 5:
                    normalise(0)
            max_parts(1)
            for m in range(1, UNITS):
                unit_out(m)
                normalise(m)
            dve.wait_ge(*at(f"{p}.oproj", i, 1))
            nc.vector.tensor_tensor(y[:, :, :], bkA[:, 0, :].rearrange("q (t c) -> q t c", t=NT),
                                    (xn if rope else xg)[:, :, :], ALU.add).then_inc(sem(f"{p}.y"), 1)

        def attention_act(act, p, i, rope, causal, keys_of=None):
            if not rope:
                act.wait_ge(*at(f"{p}.rot", i, 2))
                nc.scalar.copy(part[:, 0, 0, :], qf[:, 0, :]).then_inc(sem(f"{p}.parts"), 1)
                act.wait_ge(*at(f"{p}.qrest", i, 1))
                nc.scalar.copy(part[:, 0, 1, :], resid[:, 0, :]).then_inc(sem(f"{p}.parts"), 1)
            act.wait_ge(*at(f"{p}.vproj", i, 1))
            nc.scalar.copy(vaug[:, :, :, 0:DH],
                           bkB[:, 1, 0, :].rearrange("k (t h d) -> k t h d", t=NT, h=H)).then_inc(sem(f"{p}.v"), 1)
            if keys_of:
                keys_act(act, keys_of, i, 0)
                keys_act(act, keys_of, i, 1)
            pairs = H // 2
            for b in range(GB):
                act.wait_ge(*at(f"{p}.nmT_ps", i, b + 1))
                if b:
                    act.wait_ge(*at(f"{p}.s2", i, b * pairs))
                nc.scalar.mul(nmT[:, :, :].rearrange("c t q -> c (t q)"), bkA16[:, 0:S], -1.0).then_inc(sem(f"{p}.nmT"), 1)
                for j in range(pairs):
                    n = b * pairs + j
                    act.wait_ge(*at(f"{p}.s2", i, n + 1))
                    if n >= 2:
                        act.wait_ge(*at(f"{p}.pv", i, n - 1))
                    wd = 3 * S if causal else 4 * S
                    nc.scalar.activation(pT[:, n % 2, 0:wd], bkB[:, n % 2, :, :].rearrange("k t c -> k (t c)")[:, 0:wd],
                                         ACT.Exp, scale=SCALE).then_inc(sem(f"{p}.exp"), 1)
            act.wait_ge(*at(f"{p}.oT_ps", i, 1))
            nc.scalar.copy(oT[:, :], bkD[:, :]).then_inc(sem(f"{p}.oT"), 1)

        def keys_pe(pe, p, i):
            nc.tensor.matmul(bkD[:, :], w(f"{p}_k"), cT[:, :], start=True, stop=True).then_inc(sem(f"{p}.proj"), 1)

        def keys_dve(dve, p, i, later=0):
            dve.wait_ge(*at(f"{p}.proj", i, 1, later))
            nc.vector.tensor_scalar(qf[:, 1, :], bkD[:, :], w(f"{p}_bk"), None, ALU.add).then_inc(sem(f"{p}.rot"), 1)

        def keys_act(act, p, i, part_n, later=0):
            act.wait_ge(*(at(f"{p}.rest", i, 1, later) if part_n else at(f"{p}.rot", i, 1, later)))
            nc.scalar.copy(part[:, 1, part_n, :], (resid if part_n else qf)[:, 1, :]).then_inc(sem(f"{p}.parts"), 1)

        def keys_pool(pool, p, i, later=0):
            pool.wait_ge(*at(f"{p}.parts", i, 1, later))
            nc.gpsimd.tensor_tensor(resid[:, 1, :], qf[:, 1, :], part[:, 1, 0, :], ALU.subtract).then_inc(sem(f"{p}.rest"), 1)
            pool.wait_ge(*at(f"{p}.parts", i, 2, later))
            nc.gpsimd.tensor_tensor(part[:, 1, 2, :], resid[:, 1, :], part[:, 1, 1, :], ALU.subtract).then_inc(sem(f"{p}.rest"), 1)

        def split_pool(pool, p, i, later):
            for n in range(2):
                pool.wait_ge(*at(f"{p}.parts", i, n + 1, later))
                nc.gpsimd.tensor_tensor(resid[:, n, :], qf[:, n, :], part[:, n, 0, :], ALU.subtract).then_inc(sem(f"{p}.rest"), 1)
            for n in range(2):
                pool.wait_ge(*at(f"{p}.parts", i, n + 3, later))
                pool.wait_ge(*at(f"{p}.rest", i, n + 1, later))
                nc.gpsimd.tensor_tensor(part[:, n, 2, :], resid[:, n, :], part[:, n, 1, :], ALU.subtract).then_inc(sem(f"{p}.rest"), 1)

        def scratch_sp(sp, p, i, n, rest, parts, later=0):
            queries = n == 0 and p != "P"
            rest, parts = at(f"{p}.{'qrest' if queries else 'rest'}", i, rest, later), at(f"{p}.parts", i, parts, later)
            sp.wait_ge(*rest)
            sp.wait_ge(*parts)
            sp.dma_start(scratch[n].rearrange("(j p) t -> p j t", j=3), part[:, n, :, :]).then_inc(sem(f"{p}.scr{n}"), 16)

        def stack_sp(sp, p, i, n, later=0, unused=None):
            waits = [at(f"{p}.scr{n}", i, 16, later)] + ([at(unused, i, H)] if unused else [])
            for wait in waits:
                sp.wait_ge(*wait)
            src = scratch[n].rearrange("(e a g) t -> a e g t", a=HP, g=HG)
            runs = [(0, 1, 0), (1, 1, 0), (2, 1, 0), (3, 1, 1), (4, 1, 1), (5, 1, 2)] if n == 1 else [(0, 3, 0), (3, 2, 0), (5, 1, 0)]
            for a in range(HP):
                for s0, k, j in runs:
                    d0 = 64 * a + DH * s0
                    sp.dma_start(stk[d0:d0 + DH * k, n, :, :], src[a, DH * j:DH * (j + k), :, :]).then_inc(sem(f"{p}.stk"), 16)

        def start_sp(sp, i, later):
            for n in range(2):
                scratch_sp(sp, "P", i, n, n + 3, n + 3, later)
            for n in range(2):
                stack_sp(sp, "P", i, n, later)

        PER.update({"P.in": 32, "P.T_ps": 1, "P.xT": 2, "P.proj": 4, "P.rot": 6, "P.parts": 4, "P.rest": 4,
                    "P.scr0": 16, "P.scr1": 16, "P.stk": 18 * 16})

        def start_in_pe(pe, i, later):
            pe.wait_ge(*at("P.in", i, 32, later))
            for t in range(NT):
                nc.tensor.transpose(bkC[:, t * P:(t + 1) * P], xn[:, t, :], ident)
            for t in range(NT):
                mm = nc.tensor.transpose(bkD[:, t * P:(t + 1) * P], cg[:, t, :], ident)
            mm.then_inc(sem("P.T_ps"), 1)

        def start_qk_pe(pe, i, later):
            pe.wait_ge(*at("P.xT", i, 2, later))
            for n, (name, bank) in enumerate((("L0_q", bkA[:, 0, :]), ("L0_qs", bkA[:, 1, :]), ("L0_k", bkC[:, :]), ("L0_ks", bkD[:, :]))):
                nc.tensor.matmul(bank, w(name), xT[:, :], start=True, stop=True).then_inc(sem("P.proj"), 1)

        def start_dve(dve, i, later):
            v3 = lambda a: a.rearrange("p (b s) -> p b s", b=GB)
            for n, banks in enumerate(((bkA[:, 0, :], bkA[:, 1, :]), (bkC[:, :], bkD[:, :]))):
                for x in range(2):
                    dve.wait_ge(*at("P.proj", i, 2 * n + x + 1, later))
                    nc.vector.tensor_tensor(v3(rt[:, x, :]), v3(banks[x]),
                                            w(("rope_c", "rope_s")[x]).rearrange("p (o s) -> p o s", o=1).to_broadcast([P, GB, S]),
                                            ALU.mult).then_inc(sem("P.rot"), 1)
                dve.wait_ge(*at("P.rot", i, 3 * n + 2, later))
                nc.vector.tensor_tensor(qf[:, n, :], rt[:, 0, :], rt[:, 1, :], ALU.add).then_inc(sem("P.rot"), 1)
                if n == 0:
                    dve.wait_ge(*at("P.rot", i, 3, later))

        def start_act(act, i, later):
            act.wait_ge(*at("P.T_ps", i, 1, later))
            nc.scalar.copy(xT[:, :], bkC[:, :]).then_inc(sem("P.xT"), 1)
            nc.scalar.copy(cT[:, :], bkD[:, :]).then_inc(sem("P.xT"), 1)
            for n in range(2):
                act.wait_ge(*at("P.rot", i, 3 * (n + 1), later))
                nc.scalar.copy(part[:, n, 0, :], qf[:, n, :]).then_inc(sem("P.parts"), 1)
            for n in range(2):
                act.wait_ge(*at("P.rest", i, n + 1, later))
                nc.scalar.copy(part[:, n, 1, :], resid[:, n, :]).then_inc(sem("P.parts"), 1)

        def norm_dve(dve, p, i, y_ready):
            dve.wait_ge(*y_ready)
            for t in range(NT):
                nc.vector.bn_stats(bst[:, t, :], y[:, t, :]).then_inc(sem(f"{p}.bst"), 1)
            dve.wait_ge(*at(f"{p}.bst", i, NT))
            s = sem(f"{p}.mv")
            nc.vector.tensor_tensor(bsum[:, :], bst[:, :, 1], bst[:, :, 4], ALU.add).then_inc(s, 1)
            nc.vector.tensor_tensor(bdif[:, :], bst[:, :, 1], bst[:, :, 4], ALU.subtract).then_inc(s, 1)
            nc.vector.tensor_tensor(bsq[:, :], bst[:, :, 2], bst[:, :, 5], ALU.add).then_inc(s, 1)
            dve.wait_ge(*at(f"{p}.mv", i, 3))
            nc.vector.scalar_tensor_tensor(out=bd2[:, :], in0=bdif[:, :], scalar=0.25, in1=bdif[:, :], op0=ALU.mult, op1=ALU.mult).then_inc(s, 1)
            nc.vector.tensor_scalar(mean[:, :], bsum[:, :], 0.5, None, ALU.mult).then_inc(s, 1)
            dve.wait_ge(*at(f"{p}.mv", i, 5))
            nc.vector.scalar_tensor_tensor(out=var[:, :], in0=bsq[:, :], scalar=1.0 / P, in1=bd2[:, :], op0=ALU.mult, op1=ALU.add).then_inc(s, 1)
            dve.wait_ge(*at(f"{p}.root", i, 1))
            nc.vector.reciprocal(r0[:, :], root[:, :]).then_inc(sem(f"{p}.r0"), 1)
            dve.wait_ge(*at(f"{p}.r0", i, 1))
            s = sem(f"{p}.newton")
            nc.vector.scalar_tensor_tensor(out=ra[:, :], in0=var[:, :], scalar=LN_EPS, in1=r0[:, :], op0=ALU.add, op1=ALU.mult).then_inc(s, 1)
            dve.wait_ge(*at(f"{p}.newton", i, 1))
            nc.vector.tensor_tensor(rb[:, :], ra[:, :], r0[:, :], ALU.mult).then_inc(s, 1)
            dve.wait_ge(*at(f"{p}.newton", i, 2))
            nc.vector.tensor_scalar(ra[:, :], rb[:, :], -0.5, 1.5, ALU.mult, ALU.add).then_inc(s, 1)
            dve.wait_ge(*at(f"{p}.newton", i, 3))
            nc.vector.tensor_tensor(rstd[:, :], ra[:, :], r0[:, :], ALU.mult).then_inc(s, 1)
            dve.wait_ge(*at(f"{p}.newton", i, 4))
            for t in range(NT):
                nc.vector.tensor_scalar(xg[:, t, :], y[:, t, :], mean[:, t:t + 1], rstd[:, t:t + 1], ALU.subtract, ALU.mult).then_inc(sem(f"{p}.x"), 1)

        def norm_act(act, p, i, dst):
            act.wait_ge(*at(f"{p}.mv", i, 6))
            nc.scalar.activation(root[:, :], var[:, :], ACT.Sqrt, bias=eps_ln[:, :]).then_inc(sem(f"{p}.root"), 1)
            if dst is not None:
                act.wait_ge(*at(f"{p}.xT_ps", i, 1))
                nc.scalar.copy(dst, bkA[:, 1, :].rearrange("c (b s) -> c b s", b=GB)).then_inc(sem(f"{p}.xT"), 1)

        def norm_pe(pe, p, i):
            for t in range(NT):
                pe.wait_ge(*at(f"{p}.x", i, t + 1))
                mm = nc.tensor.transpose(bkA[:, 1, t * P:(t + 1) * P], xg[:, t, :], ident)
            mm.then_inc(sem(f"{p}.xT_ps"), 1)

        MAGIC = 1.5 * 2.0 ** 23
        PER.update({"F.am": 1, "F.xs": 1, "F.rxs": 1, "F.div": NT, "F.clip": 1, "F.xq": 1, "F.xqT_ps": 1, "F.xqT": 1,
                    "F.acc": 1, "F.fo": NT, "F.xb": 1, "F.y": 1})

        def ffn_dve(dve, i):
            dve.wait_ge(*at("n1.x", i, NT))
            nc.vector.tensor_reduce(am[:, :], xg[:, :, :], AX.X, ALU.max, apply_absolute_value=True).then_inc(sem("F.am"), 1)
            dve.wait_ge(*at("F.am", i, 1))
            nc.vector.tensor_scalar(xs[:, :], am[:, :], 1e-6, 1.0 / 127.0, ALU.max, ALU.mult).then_inc(sem("F.xs"), 1)
            dve.wait_ge(*at("F.xs", i, 1))
            nc.vector.reciprocal(rxs[:, :], xs[:, :]).then_inc(sem("F.rxs"), 1)
            dve.wait_ge(*at("F.rxs", i, 1))
            for t in range(NT):
                nc.vector.tensor_scalar(xq[:, t, :], xg[:, t, :], rxs[:, t:t + 1], MAGIC, ALU.mult, ALU.add).then_inc(sem("F.div"), 1)
            dve.wait_ge(*at("F.div", i, NT))
            nc.vector.tensor_scalar(xq[:, :, :], xq[:, :, :], MAGIC + 127.0, MAGIC - 128.0, ALU.min, ALU.max).then_inc(sem("F.clip"), 1)
            dve.wait_ge(*at("F.clip", i, 1))
            nc.vector.tensor_scalar(xq16[:, :, :], xq[:, :, :], MAGIC, None, ALU.subtract).then_inc(sem("F.xq"), 1)
            dve.wait_ge(*at("F.acc", i, 1))
            for t in range(NT):
                nc.vector.scalar_tensor_tensor(out=fo[:, t, :], in0=bkA[:, 0, t * P:(t + 1) * P], scalar=xs[:, t:t + 1],
                                               in1=w("ffn_ws"), op0=ALU.mult, op1=ALU.mult).then_inc(sem("F.fo"), 1)
            dve.wait_ge(*at("F.xb", i, 1))
            dve.wait_ge(*at("F.fo", i, NT))
            nc.vector.tensor_tensor(y[:, :, :], fo[:, :, :], xq[:, :, :], ALU.add).then_inc(sem("F.y"), 1)

        def ffn_pool(pool, i):
            pool.wait_ge(*at("n1.x", i, NT))
            pool.wait_ge(*at("F.xq", i, 1))
            nc.gpsimd.tensor_tensor(xq[:, :, :], xg[:, :, :],
                                    w("ffn_b").rearrange("p (o c) -> p o c", o=1).to_broadcast([P, NT, P]),
                                    ALU.add).then_inc(sem("F.xb"), 1)

        def ffn_pe(pe, i):
            pe.wait_ge(*at("F.xq", i, 1))
            for t in range(NT):
                mm = nc.tensor.transpose(bkD16[:, t * P:(t + 1) * P], xq16[:, t, :], ident16[:, :])
            mm.then_inc(sem("F.xqT_ps"), 1)
            pe.wait_ge(*at("F.xqT", i, 1))
            for t in range(NT):
                mm = nc.tensor.matmul(bkA[:, 0, t * P:(t + 1) * P], xqT[:, t * P:(t + 1) * P], ffn_w16[:, :], start=True, stop=True)
            mm.then_inc(sem("F.acc"), 1)

        def ffn_act(act, i):
            act.wait_ge(*at("F.xqT_ps", i, 1))
            nc.scalar.copy(xqT[:, :], bkD16[:, 0:T]).then_inc(sem("F.xqT"), 1)

        TAPS, SHORT, LONG = 4, 5, 64
        NH, DV, BLK = 4, 32, 32
        LEVELS = 5
        NU = P // BLK
        first = ExitStack()
        xTp = sb("xTp", [P, GB, TAPS - 1 + S], life=first)
        conv_bc = sb("conv_bc", [P, TAPS, 3 * P], life=first)
        Wqkv = sb("Wqkv", [P, 3 * P], life=first)
        DW = sb("DW", [P, DCOLS], life=first)
        qkv = sb("qkv", [P, NT, 3 * P], life=first)
        sq = sb("sq", [P, NT, 2 * NH, DV], life=first)
        ez, eb, beta = (sb(n, [P, NT * NH], life=first) for n in ("ez", "eb", "beta"))
        ss, ssr, rs0, rsa, rsb, rn = (sb(n, [P, NT * 2 * NH], life=first) for n in ("ss", "ssr", "rs0", "rsa", "rsb", "rn"))
        qkn = sb("qkn", [P, NT, 2 * NH, DV], life=first)
        vkb = sb("vkb", [P, NT, 2, NH, DV], life=first)
        vb, kb = vkb[:, :, 0], vkb[:, :, 1]
        kT = sb("kT", [P, NT, 2 * P], life=first)
        kz = sb("kz", [P, 2, NH, P], life=first)
        MT = sb("MT", [P, NT, NH, 2 * P], life=first)
        Cm = sb("Cm", [P, 2, NT * NH, P], life=first)
        LT = sb("LT", [P, NT * NH, P], life=first)
        TTf = sb("TTf", [P, NT * NH, P], life=first)
        Tc, TcT, Xs = (sb(n, [P, NT * NH, BLK], life=first) for n in ("Tc", "TcT", "Xs"))
        zb = qkv[:, :, 0:2 * P].rearrange("p t (a h d) -> p t a h d", a=2, h=NH)
        uz = sq[:, :, :, :].rearrange("p t (a h) d -> p t a h d", a=2)
        u1 = sb("u1", [P, GB, NH, DV], life=first)
        wT = sb("wT", [P, GB, P], life=first)
        Sbd = sb("Sbd", [P, GB, P], life=first)
        vTp = sb("vTp", [P, GB, SHORT - 1 + S], life=first)
        d_tm = sb("d_tm", [P, GB, 2, P], life=first)
        sh_tm = sb("sh_tm", [P, NT, P], life=first)
        eps_l2 = sb("eps_l2", [P, 1], life=first)

        PER.update({"D.z": 1, "D.qkv": 1, "D.ez": 1, "D.silu": 1, "D.beta": 2, "D.sq": 1, "D.ss": 1,
                    "D.qkn": 1, "D.vkb": 2, "D.tr": NT + 1, "D.trc": NT, "D.kz": NT * NH,
                    "D.gram": NT, "D.msk": NT + 1, "D.cm": LEVELS - 1, "D.lt": 1, "D.mmX": 2 * LEVELS, "D.tc": 2 * LEVELS,
                    "D.tcT": 2 * LEVELS, "D.expA": 4 * LEVELS + 4, "D.expD": 4 * LEVELS + 4, "D.xs": 2 * (LEVELS - 1),
                    "D.mmY": 2 * (LEVELS - 1), "D.g": NT, "D.mmZ": 2 * NU, "D.zz": 2 * (NU - 1) + 1, "D.uz": 3,
                    "D.state": 3, "D.Sbd": 1, "D.o": 2, "D.oc": 2,
                    "D.vT": 1, "D.vTc": 1, "D.sh": 1, "D.shc": 1})
        half = lambda a: slice(NT * NH // 2 * a, NT * NH // 2 * (a + 1))
        X_bank = lambda a: (bkC, bkD)[a][:, 0:NT * NH // 2 * BLK].rearrange("p (m c) -> p m c", c=BLK)
        Y_bank = lambda a: bkB[:, 0, a, 0:NT * NH // 2 * BLK].rearrange("p (m c) -> p m c", c=BLK)
        Z_bank = bkA[:, :, :].rearrange("p b (s a h d) -> p (b s) a h d", s=2, a=2, h=NH)

        def dw(name):
            return DW[:, DAT[name][0]:DAT[name][1]]

        def delta_pe(pe, i):
            pe.wait_ge(*at("n2.xT", i, 1))
            start_in_pe(pe, i, 1)
            for t in range(NT):
                if t == 1:
                    start_qk_pe(pe, i, 1)
                for j in range(TAPS):
                    c = j + (t % 2) * P
                    mm = nc.tensor.matmul(bkB[:, t // 2, t % 2, 0:3 * P], xTp[:, t // 2, c:c + P], conv_bc[:, j, :],
                                          start=j == 0, stop=j == TAPS - 1)
            mm.then_inc(sem("D.qkv"), 1)
            pe.wait_ge(*at("P.rot", i, 6, 1))
            for t in range(NT):
                c = TAPS - 1 + (t % 2) * P
                mm = nc.tensor.matmul(bkD[:, t * NH:(t + 1) * NH], xTp[:, t // 2, c:c + P], dw("Wb"), start=True, stop=True)
            mm.then_inc(sem("D.z"), 1)
            pe.wait_ge(*at("D.silu", i, 1))
            for t in range(NT):
                mm = nc.tensor.transpose(bkC[:, t * P:(t + 1) * P], qkv[:, t, 2 * P:3 * P], ident)
            mm.then_inc(sem("D.vT"), 1)
            pe.wait_ge(*at("D.vTc", i, 1))
            for t in range(NT):
                for j in range(SHORT):
                    c = j + (t % 2) * P
                    mm = nc.tensor.matmul(bkD[:, t * P:(t + 1) * P], vTp[:, t // 2, c:c + P], dw("short")[:, j * P:(j + 1) * P],
                                          start=j == 0, stop=j == SHORT - 1)
            mm.then_inc(sem("D.sh"), 1)
            pe.wait_ge(*at("D.qkn", i, 1))
            pe.wait_ge(*at("D.vkb", i, 2))
            for t in range(NT):
                mm = nc.tensor.transpose(bkC[:, t * P:(t + 1) * P], qkn[:, t, NH:2 * NH, :].rearrange("q h d -> q (h d)"), ident)
            mm.then_inc(sem("D.tr"), 1)
            for t in range(NT):
                if t >= 2:
                    pe.wait_ge(*at("D.trc", i, t - 1))
                for n, a in enumerate((kb[:, t, :, :], qkn[:, t, 0:NH, :])):
                    mm = nc.tensor.transpose(bkA[:, t % 2, n * P:(n + 1) * P], a.rearrange("q h d -> q (h d)"), ident)
                mm.then_inc(sem("D.tr"), 1)
            for t in range(NT):
                pe.wait_ge(*at("D.trc", i, t + 1))
                pe.wait_ge(*at("D.kz", i, NH * (t + 1)))
                if t >= 2:
                    pe.wait_ge(*at("D.msk", i, t - 1))
                for h in range(NH):
                    mm = nc.tensor.matmul(bkB[:, t % 2, h // 2, h % 2 * 2 * P:(h % 2 + 1) * 2 * P], kz[:, t % 2, h, :], kT[:, t, :],
                                          start=True, stop=True)
                mm.then_inc(sem("D.gram"), 1)
            for l in range(LEVELS):
                for a in range(2):
                    if a == 0:
                        pe.wait_ge(*(at("D.cm", i, l) if l else at("D.msk", i, NT + 1)))
                    if l:
                        pe.wait_ge(*at("D.tc", i, 2 * (l - 1) + a + 1))
                    for m in range(8):
                        rhs = Tc[:, 8 * a + m, :] if l else dw("ident32")
                        mm = nc.tensor.matmul(X_bank(a)[:, m, :], Cm[:, l % 2, 8 * a + m, :], rhs, start=True, stop=True)
                    mm.then_inc(sem("D.mmX"), 1)
                for a in range(2 if l else 0):
                    pe.wait_ge(*at("D.xs", i, 2 * (l - 1) + a + 1))
                    pe.wait_ge(*at("D.expA", i, 4 * (l - 1) + 2 * a + 2))
                    pe.wait_ge(*at("D.expD", i, 4 * (l - 1) + 2 * a + 2))
                    for m in range(8):
                        mm = nc.tensor.matmul(Y_bank(a)[:, m, :], TTf[:, 8 * a + m, :], Xs[:, 8 * a + m, :], start=True, stop=True)
                    mm.then_inc(sem("D.mmY"), 1)
            pe.wait_ge(*at("D.expA", i, 4 * LEVELS + 2))
            pe.wait_ge(*at("D.expD", i, 4 * LEVELS + 2))
            pe.wait_ge(*at("D.lt", i, 1))
            for t in range(NT):
                for h in range(NH):
                    mm = nc.tensor.matmul(bkB[:, t // 2, t % 2, h * P:(h + 1) * P], Cm[:, 1, t * NH + h, :], LT[:, t * NH + h, :],
                                          start=True, stop=True)
                mm.then_inc(sem("D.g"), 1)
            for n in range(NU):
                for b in range(GB):
                    if n == 0:
                        pe.wait_ge(*at("D.expA" if b else "D.expD", i, 4 * LEVELS + 4))
                    else:
                        pe.wait_ge(*at("D.zz", i, 2 * (n - 1) + b + 1))
                    for t in (2 * b, 2 * b + 1):
                        for h in range(NH):
                            m = t * NH + h
                            mm = nc.tensor.matmul(Z_bank[:, t, :, h, :], (LT if n + 1 < NU else TTf)[:, m, :],
                                                  (zb if n else vkb)[:, t, :, h, :], start=True, stop=True)
                    mm.then_inc(sem("D.mmZ"), 1)
            pe.wait_ge(*at("D.uz", i, 2))
            for b in range(GB):
                mm = nc.tensor.matmul(bkD[:, b * P:(b + 1) * P], qkn[:, 2 * b, NH:2 * NH, :].rearrange("q h d -> q (h d)"),
                                      uz[:, 2 * b, 0, :, :].rearrange("q h d -> q (h d)"), start=True, stop=True)
            mm.then_inc(sem("D.state"), 1)
            for b in range(GB):
                mm = nc.tensor.transpose(bkC[:, b * P:(b + 1) * P], uz[:, 2 * b + 1, 1, :, :].rearrange("q h d -> q (h d)"), ident)
            mm.then_inc(sem("D.state"), 1)
            for b in range(GB):
                for h in range(NH):
                    mm = nc.tensor.matmul(bkB[:, 0, 0, b * P + h * DV:b * P + (h + 1) * DV], MT[:, 2 * b, h, P:2 * P], uz[:, 2 * b, 0, h, :],
                                          start=True, stop=True, skip_group_check=True)
            mm.then_inc(sem("D.o"), 1)
            pe.wait_ge(*at("D.Sbd", i, 1))
            pe.wait_ge(*at("D.uz", i, 3))
            for b in range(GB):
                mm = nc.tensor.matmul(bkD[:, b * P:(b + 1) * P], wT[:, b, :], Sbd[:, b, :], start=True, stop=True)
            mm.then_inc(sem("D.state"), 1)
            pe.wait_ge(*at("D.zz", i, 2 * (NU - 1) + 1))
            for b in range(GB):
                nc.tensor.matmul(bkC[:, b * P:(b + 1) * P], kT[:, 2 * b + 1, P:2 * P], Sbd[:, b, :],
                                 start=True, stop=False, skip_group_check=True)
                for h in range(NH):
                    mm = nc.tensor.matmul(bkC[:, b * P + h * DV:b * P + (h + 1) * DV], MT[:, 2 * b + 1, h, P:2 * P], u1[:, b, h, :],
                                          start=False, stop=True, skip_group_check=True)
            mm.then_inc(sem("D.o"), 1)

        def delta_sp(sp, k, i):
            tiles = bass.ds(k * NT, NT)
            start_sp(sp, i, 1)
            for src, dst, ready in ((qkv[:, :, 2 * P:3 * P], v_d, at("D.silu", i, 1)), (xg[:, :, :], x3_d, at("n2.x", i, NT)),
                                    (sh_tm[:, :, :], sh_d, at("D.shc", i, 1)),
                                    (d_tm[:, :, :, :].rearrange("p b s c -> p (b s) c"), dl_d, at("D.oc", i, 2))):
                sp.wait_ge(*ready)
                sp.dma_start(dst[:, tiles, :], src).then_inc(sem("free"), 16)

        def delta_act(act, i):
            start_act(act, i, 1)
            act.wait_ge(*at("D.z", i, 1))
            nc.scalar.activation(ez[:, :], bkD[:, 0:NT * NH], ACT.Exp, scale=-1.0).then_inc(sem("D.ez"), 1)
            act.wait_ge(*at("D.qkv", i, 1))
            nc.scalar.activation(qkv[:, :, :].rearrange("p (a b) c -> p a b c", a=2), bkB[:, :, :, 0:3 * P], ACT.Silu).then_inc(sem("D.silu"), 1)
            act.wait_ge(*at("D.vT", i, 1))
            nc.scalar.copy(vTp[:, :, SHORT - 1:], bkC[:, :].rearrange("c (b s) -> c b s", b=GB)).then_inc(sem("D.vTc"), 1)
            act.wait_ge(*at("D.ss", i, 1))
            nc.scalar.activation(ssr[:, :], ss[:, :], ACT.Sqrt, bias=eps_l2[:, :]).then_inc(sem("D.root"), 1)
            for t in range(NT):
                act.wait_ge(*at("D.tr", i, t + 2))
                nc.scalar.copy(kT[:, t, :], bkA[:, t % 2, 0:2 * P]).then_inc(sem("D.trc"), 1)
            for l in range(LEVELS):
                for a in range(2 if l else 0):
                    act.wait_ge(*at("D.mmX", i, 2 * l + a + 1))
                    nc.scalar.copy(Xs[:, half(a), :], X_bank(a)).then_inc(sem("D.xs"), 1)
                for a in range(2):
                    act.wait_ge(*at("D.tcT", i, 2 * l + a + 1))
                    for k in (0, 1):
                        r = slice(BLK * k, BLK * (k + 1))
                        nc.scalar.copy(TTf[r, half(a), r], TcT[r, half(a), :]).then_inc(sem("D.expA"), 1)
            for k in (0, 1):
                r = slice(BLK * k, BLK * (k + 1))
                nc.scalar.copy(Cm[r, 1, :, r], Tc[r, :, :]).then_inc(sem("D.expA"), 1)
            for t in (2, 3):
                act.wait_ge(*at("D.g", i, t + 1))
                nc.scalar.copy(LT[:, t * NH:(t + 1) * NH, :], bkB[:, t // 2, t % 2, :].rearrange("p (h c) -> p h c", h=NH)).then_inc(sem("D.expA"), 1)
            for b in range(GB):
                act.wait_ge(*at("D.mmZ", i, 2 * (NU - 1) + b + 1))
                nc.scalar.copy(uz[:, 2 * b:2 * b + 2, :, :, :], Z_bank[:, 2 * b:2 * b + 2]).then_inc(sem("D.uz"), 1)
            act.wait_ge(*at("D.state", i, 2))
            nc.scalar.copy(wT[:, :, :], bkC[:, 0:GB * P].rearrange("p (b c) -> p b c", b=GB)).then_inc(sem("D.uz"), 1)

        def delta_pool(pool, k, i):
            split_pool(pool, "P", i, 1)
            pool.wait_ge(*at("D.silu", i, 1))
            qk = qkv[:, :, 0:2 * P].rearrange("p t (h d) -> p t h d", d=DV)
            nc.gpsimd.tensor_tensor(sq[:, :, :, :], qk, qk, ALU.mult).then_inc(sem("D.sq"), 1)
            bb = beta[:, :].rearrange("p (t h o) -> p t h o", h=NH, o=1).to_broadcast([P, NT, NH, DV])
            pool.wait_ge(*at("D.beta", i, 2))
            nc.gpsimd.tensor_tensor(vb, qkv[:, :, 2 * P:3 * P].rearrange("p t (h d) -> p t h d", d=DV), bb, ALU.mult).then_inc(sem("D.vkb"), 1)
            pool.wait_ge(*at("D.qkn", i, 1))
            nc.gpsimd.tensor_tensor(kb, qkn[:, :, NH:2 * NH, :], bb, ALU.mult).then_inc(sem("D.vkb"), 1)
            A = MT[:, :, :, 0:P].rearrange("p t h c -> p (t h) c")

            def masked(out, name, done):
                nc.gpsimd.tensor_tensor(out, A, dw(name).rearrange("p (o c) -> p o c", o=1).to_broadcast([P, NT * NH, P]),
                                        ALU.mult).then_inc(done, 1)
            pool.wait_ge(*at("D.msk", i, NT))
            for l in range(1, LEVELS):
                if l >= 2:
                    pool.wait_ge(*at("D.mmX", i, 2 * (l - 1)))
                masked(Cm[:, l % 2, :, :], f"level{l}", sem("D.cm"))
            masked(LT[:, :, :], "off", sem("D.lt"))

        def delta_dve(dve, k, i):
            start_dve(dve, i, 1)
            dve.wait_ge(*at("D.ez", i, 1))
            nc.vector.tensor_scalar(eb[:, :], ez[:, :], 1.0, None, ALU.add).then_inc(sem("D.beta"), 1)
            dve.wait_ge(*at("D.beta", i, 1))
            nc.vector.reciprocal(beta[:, :], eb[:, :]).then_inc(sem("D.beta"), 1)
            dve.wait_ge(*at("D.sq", i, 1))
            nc.vector.tensor_reduce(ss[:, :].rearrange("p (t h) -> p t h", t=NT), sq[:, :, :, :], AX.X, ALU.add).then_inc(sem("D.ss"), 1)
            dve.wait_ge(*at("D.root", i, 1))
            nc.vector.reciprocal(rs0[:, :], ssr[:, :]).then_inc(sem("D.r0"), 1)
            dve.wait_ge(*at("D.r0", i, 1))
            s = sem("D.newton")
            nc.vector.scalar_tensor_tensor(out=rsa[:, :], in0=ss[:, :], scalar=1e-6, in1=rs0[:, :], op0=ALU.add, op1=ALU.mult).then_inc(s, 1)
            dve.wait_ge(*at("D.newton", i, 1))
            nc.vector.tensor_tensor(rsb[:, :], rsa[:, :], rs0[:, :], ALU.mult).then_inc(s, 1)
            dve.wait_ge(*at("D.newton", i, 2))
            nc.vector.tensor_scalar(rsa[:, :], rsb[:, :], -0.5, 1.5, ALU.mult, ALU.add).then_inc(s, 1)
            dve.wait_ge(*at("D.newton", i, 3))
            nc.vector.tensor_tensor(rn[:, :], rsa[:, :], rs0[:, :], ALU.mult).then_inc(s, 1)
            dve.wait_ge(*at("D.newton", i, 4))
            nc.vector.tensor_tensor(qkn[:, :, :, :], qkv[:, :, 0:2 * P].rearrange("p t (h d) -> p t h d", d=DV),
                                    rn[:, :].rearrange("p (t h o) -> p t h o", t=NT, o=1).to_broadcast([P, NT, 2 * NH, DV]),
                                    ALU.mult).then_inc(sem("D.qkn"), 1)
            dve.wait_ge(*at("D.sh", i, 1))
            nc.vector.tensor_copy(sh_tm[:, :, :], bkD[:, :].rearrange("p (t c) -> p t c", t=NT)).then_inc(sem("D.shc"), 1)
            for t in range(NT + 2):
                if t < NT:
                    if t == 0:
                        dve.wait_ge(*at("D.tr", i, 1))
                    if t >= 2:
                        dve.wait_ge(*at("D.gram", i, t - 1))
                    for h in range(NH):
                        r = slice(DV * h, DV * (h + 1))
                        nc.vector.tensor_copy(kz[r, t % 2, h, :], bkC[r, t * P:(t + 1) * P]).then_inc(sem("D.kz"), 1)
                if t >= 2:
                    dve.wait_ge(*at("D.gram", i, t - 1))
                    nc.vector.tensor_tensor(MT[:, t - 2, :, :], bkB[:, t % 2, :, :].rearrange("p a (b c) -> p (a b) c", b=2),
                                            dw("mask2").rearrange("p (o c) -> p o c", o=1).to_broadcast([P, NH, 2 * P]),
                                            ALU.mult).then_inc(sem("D.msk"), 1)
            dve.wait_ge(*at("D.msk", i, NT))
            nc.vector.tensor_tensor(Cm[:, 0, :, :], MT[:, :, :, 0:P].rearrange("p t h c -> p (t h) c"),
                                    dw("level0").rearrange("p (o c) -> p o c", o=1).to_broadcast([P, NT * NH, P]),
                                    ALU.mult).then_inc(sem("D.msk"), 1)
            for l in range(LEVELS):
                for a in range(2):
                    if l == 0:
                        dve.wait_ge(*at("D.mmX", i, a + 1))
                        prev, new = dw("ident32").rearrange("p (o c) -> p o c", o=1).to_broadcast([P, NT * NH // 2, BLK]), X_bank(a)
                    else:
                        dve.wait_ge(*at("D.mmY", i, 2 * (l - 1) + a + 1))
                        prev, new = Tc[:, half(a), :], Y_bank(a)
                    nc.vector.tensor_tensor(Tc[:, half(a), :], prev, new, ALU.subtract).then_inc(sem("D.tc"), 1)
                    dve.wait_ge(*at("D.tc", i, 2 * l + a + 1))
                    if l:
                        dve.wait_ge(*at("D.expA", i, 4 * (l - 1) + 2 * a + 2))
                    nc.vector.transpose(TcT[:, half(a), :].rearrange("p m c -> p (m c)"),
                                        Tc[:, half(a), :].rearrange("p m c -> p (m c)")).then_inc(sem("D.tcT"), 1)
                    dve.wait_ge(*at("D.tcT", i, 2 * l + a + 1))
                    for n in (2, 3):
                        r = slice(BLK * n, BLK * (n + 1))
                        nc.vector.tensor_copy(TTf[r, half(a), r], TcT[r, half(a), :]).then_inc(sem("D.expD"), 1)
            for n in (2, 3):
                r = slice(BLK * n, BLK * (n + 1))
                nc.vector.tensor_copy(Cm[r, 1, :, r], Tc[r, :, :]).then_inc(sem("D.expD"), 1)
            for t in (0, 1):
                dve.wait_ge(*at("D.g", i, t + 1))
                nc.vector.tensor_copy(LT[:, t * NH:(t + 1) * NH, :], bkB[:, t // 2, t % 2, :].rearrange("p (h c) -> p h c", h=NH)).then_inc(sem("D.expD"), 1)
            for n in range(NU - 1):
                for b in range(GB):
                    dve.wait_ge(*at("D.mmZ", i, 2 * n + b + 1))
                    nc.vector.tensor_tensor(qkv[:, 2 * b:2 * b + 2, 0:2 * P],
                                            vkb[:, 2 * b:2 * b + 2, :, :, :].rearrange("p t a h d -> p t (a h d)"),
                                            bkA[:, b, :].rearrange("p (t c) -> p t c", t=2), ALU.subtract).then_inc(sem("D.zz"), 1)
            dve.wait_ge(*at("D.state", i, 1))
            nc.vector.tensor_tensor(Sbd[:, :, :], bkD[:, 0:GB * P].rearrange("p (b c) -> p b c", b=GB),
                                    dw("heads").rearrange("p (o c) -> p o c", o=1).to_broadcast([P, GB, P]),
                                    ALU.mult).then_inc(sem("D.Sbd"), 1)
            dve.wait_ge(*at("D.o", i, 1))
            nc.vector.tensor_copy(d_tm[:, :, 0, :], bkB[:, 0, 0, 0:GB * P].rearrange("p (b c) -> p b c", b=GB)).then_inc(sem("D.oc"), 1)
            dve.wait_ge(*at("D.state", i, 3))
            nc.vector.tensor_tensor(u1[:, :, :, :], uz[:, :, 0, :, :].rearrange("p (b s) h d -> p s b h d", s=2)[:, 1],
                                    bkD[:, 0:GB * P].rearrange("p (b h d) -> p b h d", b=GB, h=NH), ALU.subtract).then_inc(sem("D.zz"), 1)
            dve.wait_ge(*at("D.o", i, 2))
            nc.vector.tensor_copy(d_tm[:, :, 1, :], bkC[:, 0:GB * P].rearrange("p (b c) -> p b c", b=GB)).then_inc(sem("D.oc"), 1)


        attention_counts("L0", True)
        attention_counts("X0", False)
        for n, transposed in (("n0", True), ("n1", False), ("n2", True)):
            norm_counts(n, transposed)
        stage("N", "D", {"root": 1, "r0": 1, "newton": 4})
        s_w, s_rows, s_lora, s_wi = (sem(n) for n in ("load_w", "load_rows", "load_lora", "load_wi"))
        s_const, s_lora_mm, s_lora_w, s_memset = (sem(n) for n in ("const", "lora_mm", "lora_w", "memset"))
        block = first.enter_context(nc.Block())
        x_view = A["x"].rearrange("(n p) c -> p n c", p=P)
        c_view = A["ctx"].rearrange("(n p) c -> p n c", p=P)
        out_view = out.rearrange("(n p) c -> p n c", p=P)

        @block.sync
        def _(sp):
            for n in range(4):
                sp.dma_start(DW[32 * n:32 * n + 32, :], A["DW"][32 * n:32 * n + 32, :]).then_inc(sem("free"), 16)
            sp.dma_start(lora[:, :], A["lora"]).then_inc(s_lora, 16)
            sp.dma_start(rows[:, :], A["rows"]).then_inc(s_rows, 16)
            sp.dma_start(W[:, :], A["W"]).then_inc(s_w, 16)
            sp.dma_start(conv_bc[:, :, :], A["conv"]).then_inc(sem("load_DW"), 16)
            sp.dma_start(Wqkv[:, :], A["Wqkv"]).then_inc(sem("load_DW"), 16)
            sp.dma_start(ffn_wi[:, :], A["ffn_w"]).then_inc(s_wi, 16)
            sp.dma_start(xn[:, :, :], x_view[:, 0:NT, :]).then_inc(sem("P.in"), 16)
            sp.dma_start(cg[:, :, :], c_view[:, 0:NT, :]).then_inc(sem("P.in"), 16)
            i = Turn(sp, "first")
            start_sp(sp, i, 0)
            with sp.Fori(0, G) as k:
                scratch_sp(sp, "X0", i, 1, 2, 2)
                sp.wait_ge(*at("L0.y", i, 1))
                sp.dma_start(xn[:, :, :], x_view[:, bass.ds(k * NT + NT, NT), :]).then_inc(sem("P.in"), 16)
                sp.dma_start(cg[:, :, :], c_view[:, bass.ds(k * NT + NT, NT), :]).then_inc(sem("P.in"), 16)
                stack_sp(sp, "X0", i, 1, unused="L0.s2")
                scratch_sp(sp, "X0", i, 0, 2, 4)
                stack_sp(sp, "X0", i, 0)
                delta_sp(sp, k, i)
                i.next()
            sp.wait_ge(sem("free"), 64 * (G + 1))
            sp.wait_ge(sem("P.stk"), PER["P.stk"] * (G + 1))

        @block.gpsimd
        def _(pool):
            nc.gpsimd.memset(vaug[:, :, :, 0:DH], 0.0).then_inc(s_memset, 1)
            nc.gpsimd.memset(vaug[:, :, :, DH:DH + 1], 1.0).then_inc(s_memset, 1)
            nc.gpsimd.memset(vaug[:, :, :, DH + 1:], 0.0).then_inc(s_memset, 1)
            nc.gpsimd.memset(mx16[:, :, :, :], 0.0).then_inc(s_memset, 1)
            nc.gpsimd.memset(eps_ln[:, :], LN_EPS).then_inc(s_memset, 1)
            nc.gpsimd.memset(xTp[:, :, :], 0.0).then_inc(s_memset, 1)
            nc.gpsimd.memset(vTp[:, :, :], 0.0).then_inc(s_memset, 1)
            nc.gpsimd.memset(TTf[:, :, :], 0.0).then_inc(s_memset, 1)
            nc.gpsimd.memset(eps_l2[:, :], 1e-6).then_inc(s_memset, 1)
            nc.gpsimd.memset(kz[:, :, :, :], 0.0).then_inc(s_memset, 1)
            pool.wait_ge(sem("free"), 64)
            i = Turn(pool, "first")
            split_pool(pool, "P", i, 0)
            with pool.Fori(0, G) as k:
                keys_pool(pool, "X0", i)
                ffn_pool(pool, i)
                delta_pool(pool, k, i)
                i.next()

        @block.vector
        def _(dve):
            dve.wait_ge(s_w, 16)
            nc.vector.tensor_copy(ident16[:, :], ident).then_inc(s_const, 1)
            for n, name in enumerate(("mask_qk", "mask_kq")):
                nc.vector.tensor_copy(mask16[:, n, :, :], w(name).rearrange("p (o c) -> p o c", o=1).to_broadcast([P, 2, P])).then_inc(s_const, 1)
            nc.vector.tensor_copy(sel16[:, :, :], w("sel").rearrange("p (g k) -> p g k", g=HG)).then_inc(s_const, 1)
            dve.wait_ge(s_wi, 16)
            nc.vector.tensor_copy(ffn_w16[:, :], ffn_wi[:, :]).then_inc(s_const, 1)
            dve.wait_ge(s_lora_mm, 1)
            for n, name in enumerate(("L0_q", "L0_qs", "L0_v")):
                nc.vector.scalar_tensor_tensor(out=w(name), in0=bkA[:, 0, n * P:(n + 1) * P], scalar=LORA_SCALE,
                                               in1=w(name), op0=ALU.mult, op1=ALU.add).then_inc(s_lora_w, 1)
            dve.wait_ge(sem("load_DW"), 32)
            for j in range(TAPS):
                nc.vector.tensor_tensor(conv_bc[:, j, :], conv_bc[:, j, :], Wqkv[:, :], ALU.mult).then_inc(s_const, 1)
            dve.wait_ge(s_memset, 10)
            dve.wait_ge(sem("free"), 64)
            i = Turn(dve, "first")
            start_dve(dve, i, 0)
            with dve.Fori(0, G) as k:
                attention_dve(dve, "L0", i, True, True, False, "X0")
                dve.wait_ge(*at("free", i, 64))
                norm_dve(dve, "n0", i, at("L0.y", i, 1))
                attention_dve(dve, "X0", i, False, False, True)
                norm_dve(dve, "n1", i, at("X0.y", i, 1))
                ffn_dve(dve, i)
                norm_dve(dve, "n2", i, at("F.y", i, 1))
                delta_dve(dve, k, i)
                i.next()

        @block.scalar
        def _(act):
            act.wait_ge(s_memset, 10)
            i = Turn(act, "first")
            start_act(act, i, 0)
            with act.Fori(0, G) as k:
                attention_act(act, "L0", i, True, True, "X0")
                norm_act(act, "n0", i, xT[:, :].rearrange("c (b s) -> c b s", b=GB))
                attention_act(act, "X0", i, False, False)
                norm_act(act, "n1", i, None)
                ffn_act(act, i)
                norm_act(act, "n2", i, xTp[:, :, TAPS - 1:])
                delta_act(act, i)
                i.next()

        @block.tensor
        def _(pe):
            pe.wait_ge(s_lora, 16)
            for n, a in enumerate((0, 0, 1)):
                mm = nc.tensor.matmul(bkA[:, 0, n * P:(n + 1) * P], lora[:, a * P:(a + 1) * P],
                                      lora[:, (2 + n) * P:(3 + n) * P], start=True, stop=True)
            mm.then_inc(s_lora_mm, 1)
            pe.wait_ge(s_lora_w, 3)
            pe.wait_ge(s_rows, 16)
            pe.wait_ge(s_memset, 10)
            pe.wait_ge(sem("free"), 64)
            pe.wait_ge(s_const, 5 + TAPS)
            i = Turn(pe, "first")
            start_in_pe(pe, i, 0)
            start_qk_pe(pe, i, 0)
            with pe.Fori(0, G) as k:
                attention_pe(pe, "L0", i, None, xT, True, True, False, "X0")
                norm_pe(pe, "n0", i)
                attention_pe(pe, "X0", i, at("n0.xT", i, 1), cT, False, False, True)
                ffn_pe(pe, i)
                norm_pe(pe, "n2", i)
                delta_pe(pe, i)
                i.next()
        first.close()

        FC, FH = 16, 8
        TW = P + LONG
        filt = ExitStack()
        Tz = sb("Tz", [P, 2, FC, TW], life=filt)
        V2 = sb("V2", [P, G * NT, P], life=filt)
        Vc = sb("Vc", [P, 2, G * NT, FH], life=filt)
        Vp = sb("Vp", [P, 2, G * NT, FH], life=filt)
        LL = sb("LL", [G * NT, P, P], life=filt)
        ll_d = nc.dram_tensor("long_scratch", [B * S, P], F32, kind="Internal").ap().rearrange("(n p) c -> p n c", p=P)
        ll_tiles = ll_d.rearrange("p n c -> n p c")
        BEFORE.update({n: G * PER[n] for n, _ in STEPS.values()})
        PER.clear()
        PER.update({"L.tz0": 16, "L.tz1": 16, "L.vc": 8, "L.fir": 4, "L.ll": 4})
        taps = A["taps"].rearrange("i (c j) -> i c j", j=TW)
        CHUNKS = P // FC
        block = filt.enter_context(nc.Block())

        @block.sync
        def _(sp):
            sp.dma_start(V2[:, :, :], v_d).then_inc(sem("load_v2"), 16)
            for n in range(2):
                sp.dma_start(Tz[:, n, :, :], taps[:, n * FC:(n + 1) * FC, :]).then_inc(sem(f"L.tz{n}"), 16)
            i = Turn(sp, "fir")
            with sp.Fori(0, CHUNKS // 2 - 1) as k:
                for n in range(2):
                    sp.wait_ge(*at("L.fir", i, 2 * n + 2))
                    sp.dma_start(Tz[:, n, :, :], taps[:, bass.ds(k * 2 * FC + (n + 2) * FC, FC), :]).then_inc(sem(f"L.tz{n}"), 16)
                i.next()
            sp.wait_ge(sem("L.ll"), 2 * CHUNKS)
            sp.dma_start(ll_tiles, LL[:, :, :]).then_inc(sem("free2"), 16)
            sp.wait_ge(sem("free2"), 16)

        @block.tensor
        def _(pe):
            i = Turn(pe, "fir")
            with pe.Fori(0, CHUNKS // 2) as k:
                for u in range(4):
                    n = u // 2
                    if u % 2 == 0:
                        pe.wait_ge(*at(f"L.tz{n}", i, 16))
                    pe.wait_ge(*at("L.vc", i, 2 * u + 2))
                    for c in range(FH):
                        o = bkB[0:G * NT, u % 2, c // 4, (c % 4) * P:(c % 4 + 1) * P]
                        z = (u % 2) * FH + c
                        nc.tensor.matmul(o, Vc[:, u % 2, :, c], Tz[:, n, z, 0:P], start=True, stop=False, skip_group_check=True)
                        mm = nc.tensor.matmul(o[:, 0:LONG], Vp[LONG:P, u % 2, :, c], Tz[LONG:P, n, z, P:TW],
                                              start=False, stop=True, skip_group_check=True)
                    mm.then_inc(sem("L.fir"), 1)
                i.next()

        @block.vector
        def _(dve):
            nc.vector.memset(Vp[:, :, :, :], 0.0).then_inc(sem("Vp_zero"), 1)
            dve.wait_ge(sem("load_v2"), 16)
            dve.wait_ge(sem("Vp_zero"), 1)
            i = Turn(dve, "fir")
            halves = lambda a: a.rearrange("p (b s) c -> p b s c", s=2)

            def gather(k, u):
                v = V2[:, :, bass.ds(k * 2 * FC + u * FH, FH)]
                nc.vector.tensor_scalar(halves(Vp[LONG:P, u % 2, :, :])[:, :, 1, :], halves(v[LONG:P])[:, :, 0, :], 1.0, None, ALU.mult).then_inc(sem("L.vc"), 1)
                nc.vector.tensor_scalar(Vc[:, u % 2, :, :], v, 1.0, None, ALU.mult).then_inc(sem("L.vc"), 1)

            def results(k, u):
                dve.wait_ge(*at("L.fir", i, u + 1))
                nc.vector.tensor_scalar(LL[:, :, bass.ds(k * 2 * FC + u * FH, FH)],
                                        bkB[0:G * NT, u % 2, :, :].rearrange("n a (c j) -> n j (a c)", j=P), 1.0, None, ALU.mult).then_inc(sem("L.ll"), 1)

            for u in range(2):
                gather(0, u)
            def step(k, u, more):
                results(k, u)
                if more:
                    dve.wait_ge(*at("L.ll", i, u + 1))
                    gather(k, u + 2)
            with dve.Fori(0, CHUNKS // 2 - 1) as k:
                for u in range(4):
                    step(k, u, True)
                i.next()
            for u in range(4):
                step(CHUNKS // 2 - 1, u, u < 2)

        filt.close()

        PER.clear()
        NE, HID = 16, 2
        stage("N", "O", {"root": 1, "r0": 1, "newton": 4})
        stage("A", "O", {"oT_ps": 1, "oT": 1, "oproj": 1, "y": 1})
        attention_counts("X1", False)
        stage("A", "M", {"oT_ps": 1, "oT": 1, "oproj": 1, "y": 1})
        for n, transposed in (("n3", True), ("n4", True), ("n5", False)):
            norm_counts(n, transposed)
        PER.update({"free2": 16, "src": 96, "G.T_ps": 2, "G.T": 2, "G.root": 1, "G.r0": 1, "G.newton": 4,
                    "G.sum": 1, "G.abs": 1, "G.mean": 1, "G.xc": 1, "G.xsq": 1, "G.ssq": 1, "G.st": 3, "G.q": 3, 
                    "G.l2": 1, "G.stT_ps": 1, "G.stT": 1, "G.h1": NH, "G.gelu": NH, "G.lg": 1,
                    "G.soft": 8, "G.pexp": 1, "G.mixD": 3, "G.mixP": 1, "G.sum2": 1, "G.o": 1, "G.osq": 1, "G.oss": 2, 
                    "G.on": 2, 
                    "M.lg": 1, "M.rt": 25, "M.ed": 1, "M.cwT_ps": 1, "M.cwT": 1, "M.cpT_ps": 1, "M.cpT": 1,
                    "M.up": 2 * NE, "M.relu": 2 * NE, "M.bc": NE, "M.h": NE, "M.dn": NE - 1})
        second = ExitStack()
        s2 = lambda name, shape, dt=F32: sb(name, shape, dt, life=second)
        MW = s2("MW", [P, MCOLS])
        X4 = s2("X4", [P, NT, 4, P])
        xc = s2("xc", [P, NT, 4, P])
        NS = NT * 4 * NH
        gs1, gsa, gmean, gss, gq, gqs, gqm, groot, gr0, gra, grb, gr = (s2(n, [P, NS]) for n in (
            "gs1", "gsa", "gmean", "gss", "gq", "gqs", "gqm", "groot", "gr0", "gra", "grb", "gr"))
        st = s2("st", [P, NT, NH, 32])
        stT = s2("stT", [P, T])
        xnT = s2("xnT", [P, T])
        h1T = s2("h1T", [P, NH, T])
        inv_temp = s2("inv_temp", [P, NH * 4])
        la, lb, lc, le, pr = (s2(n, [P, NT * NH, 4]) for n in ("la", "lb", "lc", "le", "pr"))
        lm, lsum, lrec = (s2(n, [P, NT * NH]) for n in ("lm", "lsum", "lrec"))
        xm = s2("xm", [P, NT, 4, P])
        x2s = s2("x2s", [P, NT, 2, P])
        og = s2("og", [P, NT, P])
        osq = s2("osq", [P, NT, P])
        oss, ovv, oroot, or0, ora, orb, orr = (s2(n, [P, NT * NH]) for n in ("oss", "ovv", "oroot", "or0", "ora", "orb", "orr"))
        on1 = s2("on1", [P, NT, P])
        on2 = s2("on2", [P, NT, P])
        rt0, rlg, rlc, oh1, oh2, ow1, ow2, cw = (s2(n, [P, NT, NE]) for n in ("rt0", "rlg", "rlc", "oh1", "oh2", "ow1", "ow2", "cw"))
        rmx = s2("rmx", [P, NT, 8])
        rix = s2("rix", [P, NT, 8], mybir.dt.uint32)
        rif = s2("rif", [P, NT, 2])
        rd, red, rsu, rw1, rw2 = (s2(n, [P, NT]) for n in ("rd", "red", "rsu", "rw1", "rw2"))
        cwT = s2("cwT", [NE, T])
        cres = s2("cres", [P, NT, NE])
        cp = s2("cp", [P, NT, 3, NE], BF16)
        cpT = s2("cpT", [3 * NE, T], BF16)
        pick16 = s2("pick16", [P, NE], BF16)
        hr = h1T[:, :, :].rearrange("p (a f) t -> p a f t", a=2)
        hT = s2("hT", [P, 2, HID, T])
        block = second.enter_context(nc.Block())

        def mw(name):
            return MW[:, MAT[name][0]:MAT[name][1]]

        heads = lambda a: a.rearrange("p t (h d) -> p (t h) d", d=DV)
        col = lambda a: a.rearrange("p (m o) -> p m o", o=1)

        def stat(n):
            return st[:, :, :, :].rearrange("p t h (s k) -> p t s h k", k=4)[:, :, 0:4, :, n]

        def tsh(a):
            return a[:, :].rearrange("p (t s h) -> p t s h", t=NT, s=4)

        def newton(dve, name, i, var, eps, r0_, a_, b_, out_, later=0):
            s = sem(name)
            nc.vector.scalar_tensor_tensor(out=a_[:, :], in0=var[:, :], scalar=eps, in1=r0_[:, :], op0=ALU.add, op1=ALU.mult).then_inc(s, 1)
            dve.wait_ge(*at(name, i, 1, later))
            nc.vector.tensor_tensor(b_[:, :], a_[:, :], r0_[:, :], ALU.mult).then_inc(s, 1)
            dve.wait_ge(*at(name, i, 2, later))
            nc.vector.tensor_scalar(a_[:, :], b_[:, :], -0.5, 1.5, ALU.mult, ALU.add).then_inc(s, 1)
            dve.wait_ge(*at(name, i, 3, later))
            nc.vector.tensor_tensor(out_[:, :], a_[:, :], r0_[:, :], ALU.mult).then_inc(s, 1)
            dve.wait_ge(*at(name, i, 4, later))

        def front_sp(sp, tiles):
            sp.dma_start(xn[:, :, :], x3_d[:, tiles, :]).then_inc(sem("src"), 16)
            for n, src in enumerate((sh_d, ll_d, dl_d, v_d)):
                sp.dma_start(X4[:, :, n, :], src[:, tiles, :]).then_inc(sem("src"), 16)
            sp.dma_start(cg[:, :, :], c_view[:, tiles, :]).then_inc(sem("src"), 16)

        def front_dve(dve, i, e, later):
            x4 = X4[:, :, :, :].rearrange("p t s (h d) -> p (t s h) d", d=DV)
            if e == 1:
                dve.wait_ge(*at("src", i, 96, later))
                nc.vector.tensor_reduce(gs1[:, :], x4, AX.X, ALU.add).then_inc(sem("G.sum"), 1)
                dve.wait_ge(*at("G.sum", i, 1, later))
                nc.vector.tensor_scalar(gmean[:, :], gs1[:, :], 1.0 / DV, None, ALU.mult).then_inc(sem("G.mean"), 1)
                nc.vector.tensor_scalar(stat(0), tsh(gs1), 1.0 / DV, None, ALU.mult).then_inc(sem("G.st"), 1)
            if e == 3:
                nc.vector.tensor_reduce(gsa[:, :], x4, AX.X, ALU.add, apply_absolute_value=True).then_inc(sem("G.abs"), 1)
                dve.wait_ge(*at("G.mean", i, 1, later))
                nc.vector.tensor_tensor(gq[:, :], gs1[:, :], gmean[:, :], ALU.mult).then_inc(sem("G.q"), 1)
                dve.wait_ge(*at("G.abs", i, 1, later))
                nc.vector.tensor_scalar(stat(2), tsh(gsa), 1.0 / DV, None, ALU.mult).then_inc(sem("G.st"), 1)
            if e == 7:
                dve.wait_ge(*at("G.xsq", i, 1, later))
                nc.vector.tensor_reduce(gss[:, :], xc[:, :, :, :].rearrange("p t s (h d) -> p (t s h) d", d=DV), AX.X, ALU.add).then_inc(sem("G.ssq"), 1)
                dve.wait_ge(*at("G.ssq", i, 1, later))
                dve.wait_ge(*at("G.q", i, 1, later))
                nc.vector.tensor_scalar(stat(1), tsh(gss), 1.0 / DV, None, ALU.mult).then_inc(sem("G.st"), 1)
                nc.vector.tensor_tensor(gqs[:, :], gss[:, :], gq[:, :], ALU.add).then_inc(sem("G.q"), 1)
                dve.wait_ge(*at("G.q", i, 2, later))
                nc.vector.tensor_scalar(gqm[:, :], gqs[:, :], 1e-18, None, ALU.max).then_inc(sem("G.q"), 1)
            if e == 10:
                keys_dve(dve, "X1", i, later)
            if e == 12:
                dve.wait_ge(*at("G.root", i, 1, later))
                nc.vector.reciprocal(gr0[:, :], groot[:, :]).then_inc(sem("G.r0"), 1)
                dve.wait_ge(*at("G.r0", i, 1, later))
                dve.wait_ge(*at("G.q", i, 3, later))
                newton(dve, "G.newton", i, gqm, 0.0, gr0, gra, grb, gr, later)
                nc.vector.tensor_tensor(stat(3), tsh(gqs), tsh(gr), ALU.mult).then_inc(sem("G.l2"), 1)

        def front_act(act, i, e, later):
            if e == 5:
                act.wait_ge(*at("G.T_ps", i, 1, later))
                nc.scalar.copy(xnT[:, :], bkD[:, :]).then_inc(sem("G.T"), 1)
            if e == 6:
                act.wait_ge(*at("G.xc", i, 1, later))
                nc.scalar.activation(xc[:, :, :, :], xc[:, :, :, :], ACT.Square).then_inc(sem("G.xsq"), 1)
            if e == 8:
                act.wait_ge(*at("G.T_ps", i, 2, later))
                nc.scalar.copy(cT[:, :], bkD[:, :]).then_inc(sem("G.T"), 1)
            if e == 9:
                act.wait_ge(*at("G.q", i, 3, later))
                nc.scalar.activation(groot[:, :], gqm[:, :], ACT.Sqrt).then_inc(sem("G.root"), 1)
            if e == 12:
                keys_act(act, "X1", i, 0, later)
            if e == 14:
                keys_act(act, "X1", i, 1, later)
            if e == 15:
                act.wait_ge(*at("G.stT_ps", i, 1, later))
                nc.scalar.copy(stT[:, :], bkD[:, :]).then_inc(sem("G.stT"), 1)

        def front_pool(pool, i, later):
            x4 = lambda a: a[:, :, :, :].rearrange("p t s (h d) -> p (t s h) d", d=DV)
            pool.wait_ge(*at("G.mean", i, 1, later))
            nc.gpsimd.tensor_tensor(x4(xc), x4(X4), col(gmean[:, :]).to_broadcast([P, NS, DV]), ALU.subtract).then_inc(sem("G.xc"), 1)
            keys_pool(pool, "X1", i, later)

        def front_pe(pe, i, e, later):
            if e == 3:
                pe.wait_ge(*at("src", i, 96, later))
                for t in range(NT):
                    mm = nc.tensor.transpose(bkD[:, t * P:(t + 1) * P], xn[:, t, :], ident)
                mm.then_inc(sem("G.T_ps"), 1)
            if e == 6:
                pe.wait_ge(*at("G.T", i, 1, later))
                for t in range(NT):
                    mm = nc.tensor.transpose(bkD[:, t * P:(t + 1) * P], cg[:, t, :], ident)
                mm.then_inc(sem("G.T_ps"), 1)
            if e == 9:
                pe.wait_ge(*at("G.T", i, 2, later))
                keys_pe(pe, "X1", i)
            if e == 13:
                pe.wait_ge(*at("X1.rot", i, 1, later))
                pe.wait_ge(*at("G.l2", i, 1, later))
                pe.wait_ge(*at("G.st", i, 3, later))
                for t in range(NT):
                    mm = nc.tensor.transpose(bkD[:, t * P:(t + 1) * P], st[:, t, :, :].rearrange("p h c -> p (h c)"), ident)
                mm.then_inc(sem("G.stT_ps"), 1)

        def gate_dve(dve, i):
            s = sem("G.soft")
            dve.wait_ge(*at("G.lg", i, 1))
            hb = lambda a: a.rearrange("p (o h s) -> p o (h s)", o=1, s=4).to_broadcast([P, NT, NH * 4])
            f3 = lambda a: a[:, :, :].rearrange("p (t h) s -> p t (h s)", t=NT)
            nc.vector.tensor_tensor(f3(la), bkC[:, 0:NS].rearrange("p (t m) -> p t m", t=NT), hb(mw("b2")), ALU.add).then_inc(s, 1)
            dve.wait_ge(*at("G.soft", i, 1))
            nc.vector.tensor_tensor(f3(lb), f3(la), hb(inv_temp[:, :]), ALU.mult).then_inc(s, 1)
            dve.wait_ge(*at("G.soft", i, 2))
            nc.vector.tensor_reduce(lm[:, :], lb[:, :, :], AX.X, ALU.max).then_inc(s, 1)
            dve.wait_ge(*at("G.soft", i, 3))
            nc.vector.tensor_tensor(lc[:, :, :], lb[:, :, :], col(lm[:, :]).to_broadcast([P, NT * NH, 4]), ALU.subtract).then_inc(s, 1)
            dve.wait_ge(*at("G.pexp", i, 1))
            nc.vector.tensor_reduce(lsum[:, :], le[:, :, :], AX.X, ALU.add).then_inc(s, 1)
            dve.wait_ge(*at("G.soft", i, 5))
            nc.vector.reciprocal(lrec[:, :], lsum[:, :]).then_inc(s, 1)
            dve.wait_ge(*at("G.soft", i, 6))
            nc.vector.tensor_tensor(la[:, :, :], le[:, :, :], col(lrec[:, :]).to_broadcast([P, NT * NH, 4]), ALU.mult).then_inc(s, 1)
            dve.wait_ge(*at("G.soft", i, 7))
            nc.vector.tensor_scalar(pr[:, :, :], la[:, :, :], 1.0 - 4 * FLOOR, FLOOR, ALU.mult, ALU.add).then_inc(s, 1)
            dve.wait_ge(*at("G.soft", i, 8))
            for t in (0, 1, 2):
                mix(nc.vector, t).then_inc(sem("G.mixD"), 1)
            dve.wait_ge(*at("G.mixD", i, 3))
            dve.wait_ge(*at("G.mixP", i, 1))
            nc.vector.tensor_tensor(x2s[:, :, :, :], xm[:, :, 0:2, :], xm[:, :, 2:4, :], ALU.add).then_inc(sem("G.sum2"), 1)
            dve.wait_ge(*at("G.sum2", i, 1))
            nc.vector.tensor_tensor(og[:, :, :], x2s[:, :, 0, :], x2s[:, :, 1, :], ALU.add).then_inc(sem("G.o"), 1)
            dve.wait_ge(*at("G.osq", i, 1))
            nc.vector.tensor_reduce(oss[:, :], heads(osq[:, :, :]), AX.X, ALU.add).then_inc(sem("G.oss"), 1)
            dve.wait_ge(*at("G.oss", i, 1))
            nc.vector.tensor_scalar(ovv[:, :], oss[:, :], 1.0 / DV, LN_EPS, ALU.mult, ALU.add).then_inc(sem("G.oss"), 1)
            dve.wait_ge(*at("O.root", i, 1))
            nc.vector.reciprocal(or0[:, :], oroot[:, :]).then_inc(sem("O.r0"), 1)
            dve.wait_ge(*at("O.r0", i, 1))
            dve.wait_ge(*at("G.oss", i, 2))
            newton(dve, "O.newton", i, ovv, 0.0, or0, ora, orb, orr)
            nc.vector.tensor_tensor(heads(on1[:, :, :]), heads(og[:, :, :]), col(orr[:, :]).to_broadcast([P, NT * NH, DV]), ALU.mult).then_inc(sem("G.on"), 1)
            dve.wait_ge(*at("G.on", i, 1))
            nc.vector.tensor_tensor(on2[:, :, :], on1[:, :, :], mw("onorm").rearrange("p (o c) -> p o c", o=1).to_broadcast([P, NT, P]), ALU.mult).then_inc(sem("G.on"), 1)
            dve.wait_ge(*at("O.oproj", i, 1))
            nc.vector.tensor_tensor(y[:, :, :], bkA[:, 0, :].rearrange("q (t c) -> q t c", t=NT), xn[:, :, :], ALU.add).then_inc(sem("O.y"), 1)

        def mix(eng, t):
            p = pr[:, t * NH:(t + 1) * NH, :].rearrange("p h (s o) -> p s h o", o=1).to_broadcast([P, 4, NH, DV])
            return eng.tensor_tensor(xm[:, t, :, :].rearrange("p s (h d) -> p s h d", d=DV),
                                     X4[:, t, :, :].rearrange("p s (h d) -> p s h d", d=DV), p, ALU.mult)

        def gate_pool(pool, i):
            pool.wait_ge(*at("G.soft", i, 8))
            mix(nc.gpsimd, 3).then_inc(sem("G.mixP"), 1)

        def gate_act(act, i):
            for h in range(NH):
                act.wait_ge(*at("G.h1", i, h + 1))
                nc.scalar.activation(h1T[:, h, :], bkB[:, h // 2, h % 2, :], ACT.Gelu, bias=mw("mlp_b1")).then_inc(sem("G.gelu"), 1)
            act.wait_ge(*at("G.soft", i, 4))
            nc.scalar.activation(le[:, :, :], lc[:, :, :], ACT.Exp).then_inc(sem("G.pexp"), 1)
            act.wait_ge(*at("G.o", i, 1))
            nc.scalar.activation(osq[:, :, :], og[:, :, :], ACT.Square).then_inc(sem("G.osq"), 1)
            act.wait_ge(*at("G.oss", i, 2))
            nc.scalar.activation(oroot[:, :], ovv[:, :], ACT.Sqrt).then_inc(sem("O.root"), 1)
            act.wait_ge(*at("O.oT_ps", i, 1))
            nc.scalar.copy(oT[:, :], bkD[:, :]).then_inc(sem("O.oT"), 1)

        def gate_pe(pe, i):
            pe.wait_ge(*at("G.T", i, 1))
            pe.wait_ge(*at("G.stT", i, 1))
            for h in range(NH):
                o = bkB[:, h // 2, h % 2, :]
                nc.tensor.matmul(o, mw("mlp_w1"), xnT[:, :], start=True, stop=False)
                r = slice(32 * h, 32 * h + 16)
                nc.tensor.matmul(o, MW[r, MAT["mlp_w1s"][0]:MAT["mlp_w1s"][1]], stT[r, :], start=False, stop=True).then_inc(sem("G.h1"), 1)
            for h in range(NH):
                pe.wait_ge(*at("G.gelu", i, h + 1))
                for t in range(NT):
                    m = (t * NH + h) * 4
                    mm = nc.tensor.matmul(bkC[:, m:m + 4], h1T[:, h, t * P:(t + 1) * P], mw("mlp_w2"), start=True, stop=True)
            mm.then_inc(sem("G.lg"), 1)
            pe.wait_ge(*at("G.on", i, 2))
            for t in range(NT):
                mm = nc.tensor.transpose(bkD[:, t * P:(t + 1) * P], on2[:, t, :], ident)
            mm.then_inc(sem("O.oT_ps"), 1)
            pe.wait_ge(*at("O.oT", i, 1))
            for t in range(NT):
                mm = nc.tensor.matmul(bkA[:, 0, t * P:(t + 1) * P], oT[:, t * P:(t + 1) * P], mw("Wo"), start=True, stop=True)
            mm.then_inc(sem("O.oproj"), 1)

        def experts_dve(dve, i, last):
            s = sem("M.rt")
            rb = lambda a: a.rearrange("p (o e) -> p o e", o=1).to_broadcast([P, NT, NE])
            tb = lambda a: a.rearrange("p (t o) -> p t o", o=1).to_broadcast([P, NT, NE])
            dve.wait_ge(*at("M.lg", i, 1))
            nc.vector.tensor_tensor(rt0[:, :, :], bkD[:, 0:NT * NE].rearrange("p (t e) -> p t e", t=NT), rb(mw("bg")), ALU.add).then_inc(s, 1)
            dve.wait_ge(*at("M.rt", i, 1))
            nc.vector.tensor_tensor(rlg[:, :, :], rt0[:, :, :], rb(mw("bias")), ALU.add).then_inc(s, 1)
            dve.wait_ge(*at("M.rt", i, 2))
            nc.vector.tensor_copy(rlc[:, :, :], rlg[:, :, :]).then_inc(s, 1)
            for t in range(NT):
                nc.vector.max(rmx[:, t, :], rlg[:, t, :]).then_inc(s, 1)
            dve.wait_ge(*at("M.rt", i, 3 + NT))
            nc.vector.tensor_tensor(rd[:, :], rmx[:, :, 1], rmx[:, :, 0], ALU.subtract).then_inc(s, 1)
            for t in range(NT):
                nc.vector.max_index(rix[:, t, :], rmx[:, t, :], rlc[:, t, :]).then_inc(s, 1)
            dve.wait_ge(*at("M.ed", i, 1))
            nc.vector.tensor_scalar(rsu[:, :], red[:, :], 1.0, None, ALU.add).then_inc(s, 1)
            dve.wait_ge(*at("M.rt", i, 5 + 2 * NT))
            nc.vector.reciprocal(rw1[:, :], rsu[:, :]).then_inc(s, 1)
            dve.wait_ge(*at("M.rt", i, 14))
            nc.vector.tensor_tensor(rw2[:, :], red[:, :], rw1[:, :], ALU.mult).then_inc(s, 1)
            nc.vector.tensor_copy(rif[:, :, :], rix[:, :, 0:2]).then_inc(s, 1)
            dve.wait_ge(*at("M.rt", i, 16))
            nc.vector.tensor_tensor(oh1[:, :, :], rb(mw("iota")), tb(rif[:, :, 0]), ALU.is_equal).then_inc(s, 1)
            nc.vector.tensor_tensor(oh2[:, :, :], rb(mw("iota")), tb(rif[:, :, 1]), ALU.is_equal).then_inc(s, 1)
            dve.wait_ge(*at("M.rt", i, 18))
            nc.vector.tensor_tensor(ow1[:, :, :], oh1[:, :, :], tb(rw1[:, :]), ALU.mult).then_inc(s, 1)
            nc.vector.tensor_tensor(ow2[:, :, :], oh2[:, :, :], tb(rw2[:, :]), ALU.mult).then_inc(s, 1)
            dve.wait_ge(*at("M.rt", i, 20))
            nc.vector.tensor_tensor(cw[:, :, :], ow1[:, :, :], ow2[:, :, :], ALU.add).then_inc(s, 1)
            dve.wait_ge(*at("M.rt", i, 21))
            nc.vector.tensor_copy(cp[:, :, 0, :], cw[:, :, :]).then_inc(s, 1)
            dve.wait_ge(*at("M.rt", i, 22))
            nc.vector.tensor_tensor(cres[:, :, :], cw[:, :, :], cp[:, :, 0, :], ALU.subtract).then_inc(s, 1)
            dve.wait_ge(*at("M.rt", i, 23))
            nc.vector.tensor_copy(cp[:, :, 1, :], cres[:, :, :]).then_inc(s, 1)
            dve.wait_ge(*at("M.rt", i, 24))
            nc.vector.tensor_tensor(cp[:, :, 2, :], cres[:, :, :], cp[:, :, 1, :], ALU.subtract).then_inc(s, 1)
            for e in range(NE):
                dve.wait_ge(*at("M.relu", i, 2 * e + 2))
                dve.wait_ge(*at("M.bc", i, e + 1))
                if e >= 2:
                    dve.wait_ge(*at("M.dn", i, e - 1))
                nc.vector.tensor_tensor(hT[:, e % 2, :, :], hr[:, e % 2, :, :],
                                        bkA[:, e % 2, :].rearrange("p (o t) -> p o t", o=1).to_broadcast([P, HID, T]),
                                        ALU.mult).then_inc(sem("M.h"), 1)
                if not last:
                    front_dve(dve, i, e, 1)
            dve.wait_ge(*at("M.oT_ps", i, 1))
            nc.vector.tensor_tensor(y[:, :, :], bkD[:, :].rearrange("q (t c) -> q t c", t=NT), xg[:, :, :], ALU.add).then_inc(sem("M.y"), 1)

        def experts_act(act, i, last):
            act.wait_ge(*at("M.rt", i, 4 + NT))
            nc.scalar.activation(red[:, :], rd[:, :], ACT.Exp).then_inc(sem("M.ed"), 1)

            def relu(e):
                for f in range(HID):
                    act.wait_ge(*at("M.up", i, 2 * e + f + 1))
                    if f == 0 and e >= 2:
                        act.wait_ge(*at("M.h", i, e - 1))
                    nc.scalar.activation(hr[:, e % 2, f, :], bkB[:, e % 2, f, :], ACT.Relu,
                                         bias=mw("eb1")[:, 2 * e + f:2 * e + f + 1]).then_inc(sem("M.relu"), 1)
            relu(0)
            relu(1)
            act.wait_ge(*at("M.cwT_ps", i, 1))
            nc.scalar.copy(cwT[:, :], bkD[0:NE, :]).then_inc(sem("M.cwT"), 1)
            act.wait_ge(*at("M.cpT_ps", i, 1))
            nc.scalar.copy(cpT[:, :], bkA16[0:3 * NE, 0:T]).then_inc(sem("M.cpT"), 1)
            for e in range(2, NE):
                relu(e)
                if not last:
                    front_act(act, i, e, 1)
            act.wait_ge(*at("M.oproj", i, 1))
            nc.scalar.copy(oT[:, :], bkC[:, :]).then_inc(sem("M.oT"), 1)

        def experts_pe(pe, i, last):
            pe.wait_ge(*at("n4.xT", i, 1))
            for t in range(NT):
                mm = nc.tensor.matmul(bkD[:, t * NE:(t + 1) * NE], xT[:, t * P:(t + 1) * P], mw("Wg"), start=True, stop=True)
            mm.then_inc(sem("M.lg"), 1)

            def up(e):
                for f in range(HID):
                    if e >= 2:
                        pe.wait_ge(*at("M.relu", i, 2 * (e - 2) + f + 1))
                    c = MAT["W1"][0] + (e * HID + f) * P
                    nc.tensor.matmul(bkB[:, e % 2, f, :], MW[:, c:c + P], xT[:, :], start=True, stop=True).then_inc(sem("M.up"), 1)

            def spread(e):
                if e >= 2:
                    pe.wait_ge(*at("M.h", i, e - 1))
                nc.tensor.matmul(bkA[:, e % 2, :], pick16[0:3 * NE, e:e + 1].to_broadcast([3 * NE, P]), cpT[:, :],
                                 start=True, stop=True).then_inc(sem("M.bc"), 1)

            def down(e):
                pe.wait_ge(*at("M.h", i, e + 1))
                for f in range(HID):
                    c = MAT["W2"][0] + (e * HID + f) * P
                    mm = nc.tensor.matmul(bkC[:, :], MW[:, c:c + P], hT[:, e % 2, f, :], start=False, stop=e == NE - 1 and f == HID - 1,
                                          skip_group_check=True)
                mm.then_inc(sem("M.dn") if e + 1 < NE else sem("M.oproj"), 1)
            up(0)
            up(1)
            pe.wait_ge(*at("M.rt", i, 21))
            for t in range(NT):
                mm = nc.tensor.transpose(bkD[0:NE, t * P:(t + 1) * P], cw[:, t, :], ident)
            mm.then_inc(sem("M.cwT_ps"), 1)
            pe.wait_ge(*at("M.rt", i, 25))
            pe.wait_ge(*at("M.cwT", i, 1))
            nc.tensor.matmul(bkC[:, :], MW[0:NE, MAT["eb2"][0]:MAT["eb2"][1]], cwT[:, :], start=True, stop=False, skip_group_check=True)
            for t in range(NT):
                mm = nc.tensor.transpose(bkA16[0:3 * NE, t * P:(t + 1) * P], cp[:, t, :, :].rearrange("q j e -> q (j e)"), ident16[:, :])
            mm.then_inc(sem("M.cpT_ps"), 1)
            pe.wait_ge(*at("M.cpT", i, 1))
            spread(0)
            spread(1)
            for e in range(NE):
                if e + 2 < NE:
                    up(e + 2)
                down(e)
                if e + 2 < NE:
                    spread(e + 2)
                if not last:
                    front_pe(pe, i, e, 1)
            if not last:
                pe.wait_ge(*at("G.stT", i, 1, 1))
            pe.wait_ge(*at("M.oT", i, 1))
            for t in range(NT):
                mm = nc.tensor.transpose(bkD[:, t * P:(t + 1) * P], oT[:, t * P:(t + 1) * P], ident)
            mm.then_inc(sem("M.oT_ps"), 1)

        @block.sync
        def _(sp):
            experts_from = MAT["W1"][0]
            sp.dma_start(MW[:, 0:experts_from], A["MW"][:, 0:experts_from]).then_inc(sem("load_MW"), 16)
            front_sp(sp, slice(0, NT))
            for n in range(4):
                r = slice(32 * n, 32 * n + 32)
                sp.dma_start(MW[r, experts_from:], A["MW"][r, experts_from:]).then_inc(sem("load_experts"), 16)
            i = Turn(sp, "second")
            scratch_sp(sp, "X1", i, 1, 2, 2)
            stack_sp(sp, "X1", i, 1)

            def turn(k, last):
                scratch_sp(sp, "X1", i, 0, 2, 4)
                stack_sp(sp, "X1", i, 0)
                if not last:
                    sp.wait_ge(*at("O.y", i, 1))
                    front_sp(sp, bass.ds(k * NT + NT, NT))
                    scratch_sp(sp, "X1", i, 1, 2, 2, 1)
                    stack_sp(sp, "X1", i, 1, 1, "X1.s2")
                sp.wait_ge(*at("n5.x", i, NT))
                sp.dma_start(out_view[:, bass.ds(k * NT, NT) if not last else slice(k * NT, k * NT + NT), :], xg[:, :, :]).then_inc(sem("free2"), 16)
            with sp.Fori(0, G - 1) as k:
                turn(k, False)
                i.next()
            turn(G - 1, True)
            sp.wait_ge(sem("free2"), 16 * (G + 1))

        @block.gpsimd
        def _(pool):
            nc.gpsimd.memset(st[:, :, :, :], 0.0).then_inc(sem("st_zero"), 1)
            i = Turn(pool, "second")
            front_pool(pool, i, 0)

            def turn(last):
                gate_pool(pool, i)
                if not last:
                    front_pool(pool, i, 1)
            with pool.Fori(0, G - 1) as k:
                turn(False)
                i.next()
            turn(True)

        @block.vector
        def _(dve):
            dve.wait_ge(sem("load_MW"), 16)
            dve.wait_ge(sem("st_zero"), 1)
            dve.wait_ge(sem("inv_temp"), 1)
            nc.vector.tensor_copy(pick16[:, :], mw("pick")).then_inc(sem("pick"), 1)
            i = Turn(dve, "second")
            for e in range(NE):
                front_dve(dve, i, e, 0)

            def turn(last):
                gate_dve(dve, i)
                dve.wait_ge(*at("free2", i, 16))
                norm_dve(dve, "n3", i, at("O.y", i, 1))
                attention_dve(dve, "X1", i, False, True, True)
                norm_dve(dve, "n4", i, at("X1.y", i, 1))
                experts_dve(dve, i, last)
                norm_dve(dve, "n5", i, at("M.y", i, 1))
            with dve.Fori(0, G - 1) as k:
                turn(False)
                i.next()
            turn(True)

        @block.scalar
        def _(act):
            act.wait_ge(sem("load_MW"), 16)
            nc.scalar.activation(inv_temp[:, :], mw("log_temp"), ACT.Exp, scale=-1.0).then_inc(sem("inv_temp"), 1)
            i = Turn(act, "second")
            for e in range(NE):
                front_act(act, i, e, 0)

            def turn(last):
                gate_act(act, i)
                norm_act(act, "n3", i, xT[:, :].rearrange("c (b s) -> c b s", b=GB))
                attention_act(act, "X1", i, False, True)
                norm_act(act, "n4", i, xT[:, :].rearrange("c (b s) -> c b s", b=GB))
                experts_act(act, i, last)
                norm_act(act, "n5", i, None)
            with act.Fori(0, G - 1) as k:
                turn(False)
                i.next()
            turn(True)

        @block.tensor
        def _(pe):
            pe.wait_ge(sem("load_MW"), 16)
            pe.wait_ge(sem("st_zero"), 1)
            pe.wait_ge(sem("pick"), 1)
            i = Turn(pe, "second")
            for e in range(NE):
                front_pe(pe, i, e, 0)

            def turn(last):
                gate_pe(pe, i)
                norm_pe(pe, "n3", i)
                attention_pe(pe, "X1", i, at("n3.xT", i, 1), cT, False, True, True)
                norm_pe(pe, "n4", i)
                pe.wait_ge(sem("load_experts"), 64)
                experts_pe(pe, i, last)
            with pe.Fori(0, G - 1) as k:
                turn(False)
                i.next()
            turn(True)

        second.close()


def _layout(inputs):
    f = lambda n: np.asarray(inputs[n], dtype=None)
    dh = np.array([h * DH + d for d in range(DH) for h in range(H)])
    dh_swap = np.array([h * DH + (d ^ 1) for d in range(DH) for h in range(H)])
    W = np.zeros((P, NCOLS), np.float32)

    def put(name, a):
        W[:, AT[name][0]:AT[name][1]] = a

    put("ident", np.eye(P, dtype=np.float32))
    theta = (np.arange(S, dtype=np.float32)[:, None]
             / np.float32(10000.0) ** (np.arange(0, DH, 2, dtype=np.float32) / np.float32(DH))[None, :]).astype(np.float32)
    sin, cos = np.sin(theta), np.cos(theta)
    for d in range(DH):
        r = slice(d * H, (d + 1) * H)
        W[r, AT["rope_c"][0]:AT["rope_c"][1]] = cos[:, d // 2]
        W[r, AT["rope_s"][0]:AT["rope_s"][1]] = sin[:, d // 2] if d % 2 else -sin[:, d // 2]
    put("mask_qk", np.triu(np.full((P, P), MASKED, np.float32), 1))
    put("mask_kq", np.tril(np.full((P, P), MASKED, np.float32), -1))
    sel = np.zeros((P, HG, P), np.float32)
    for a in range(HP):
        for j in range(3):
            for g in range(HG):
                sel[64 * a + HG * j + g, g, :] = 1.0
    put("sel", sel.reshape(P, -1))
    put("L0_q", f("L0_attn_wq")[:, dh]); put("L0_qs", f("L0_attn_wq")[:, dh_swap])
    put("L0_k", f("L0_attn_wk")[:, dh]); put("L0_ks", f("L0_attn_wk")[:, dh_swap])
    put("L0_v", f("L0_attn_wv")); put("L0_o", f("L0_attn_wo"))
    for n, names in (("X0", ("W_Q", "W_K", "W_V", "W_O", "b_Q", "b_K")), ("X1", ("Wq", "Wk", "Wv", "Wo", "bq", "bk"))):
        m = ("L0" if n == "X0" else "L1") + "_xattn_"
        put(n + "_q", f(m + names[0])[:, dh]); put(n + "_k", f(m + names[1])[:, dh])
        put(n + "_v", f(m + names[2])); put(n + "_o", f(m + names[3]))
        put(n + "_bq", f(m + names[4])[dh][:, None]); put(n + "_bk", f(m + names[5])[dh][:, None])
    put("ffn_ws", np.broadcast_to(f("L0_ffn_weight_scale"), (P, P))); put("ffn_b", np.broadcast_to(f("L0_ffn_bias"), (P, P)))
    rows = np.zeros((1, NROWS), np.float32)
    for n, m in (("X0_bv", "L0_xattn_b_V"), ("X0_bo", "L0_xattn_b_O"), ("X1_bv", "L1_xattn_bv"), ("X1_bo", "L1_xattn_bo")):
        rows[0, RAT[n][0]:RAT[n][1]] = f(m)
    rows[0, RAT["ones"][0]:RAT["ones"][1]] = 1.0
    lora = np.concatenate([f("L0_attn_Aq").T, f("L0_attn_Av").T, f("L0_attn_Bq")[:, dh], f("L0_attn_Bq")[:, dh_swap],
                           f("L0_attn_Bv")], axis=1)
    padded = lambda a: np.concatenate([a.reshape(B * S, P), np.zeros((T, P), np.float32)])
    return {"x": padded(f("x")), "ctx": padded(f("ctx_1024")), "W": W, "rows": rows,
            "lora": np.ascontiguousarray(lora), "ffn_w": np.ascontiguousarray(f("L0_ffn_weight_q").T.astype(np.int32)), **_layout2(inputs)}


def _layout2(inputs):
    f = lambda n: np.asarray(inputs[n])
    D = np.zeros((P, DCOLS), np.float32)

    def put(name, a):
        D[:, DAT[name][0]:DAT[name][1]] = a

    j, i = np.arange(P)[:, None], np.arange(P)[None, :]
    put("Wb", f("L1_attn_Wb"))
    put("ident32", (j % 32 == np.arange(32)[None, :]).astype(np.float32))
    put("mask2", np.concatenate([(i > j), (i >= j)], axis=1).astype(np.float32))
    put("off", ((i > j) & (i // 32 != j // 32)).astype(np.float32))
    put("heads", (i // 32 == j // 32).astype(np.float32))
    for l in range(5):
        n = 2 << l
        put(f"level{l}", ((i > j) & (i // n == j // n) & (i // (n // 2) != j // (n // 2))).astype(np.float32))
    short = np.zeros((P, 5, P), np.float32)
    for k in range(5):
        short[np.arange(P), k, np.arange(P)] = f("L1_attn_fir_short_w").reshape(P, 5)[:, k]
    put("short", short.reshape(P, -1))
    conv = np.concatenate([f("L1_attn_conv_q_w"), f("L1_attn_conv_k_w"), f("L1_attn_conv_v_w")]).T
    M = np.zeros((P, MCOLS), np.float32)

    def putm(name, a, r=slice(None)):
        M[r, MAT[name][0]:MAT[name][1]] = a

    w1 = f("L1_attn_mlp_w1")
    putm("mlp_w1", w1[:P])
    for h in range(4):
        putm("mlp_w1s", w1[P:], slice(32 * h, 32 * h + 16))
    putm("mlp_w2", f("L1_attn_mlp_w2"))
    putm("mlp_b1", f("L1_attn_mlp_b1")[:, None])
    putm("b2", np.tile(f("L1_attn_mlp_b2"), 4))
    putm("log_temp", np.repeat(f("L1_attn_log_temp").reshape(4), 4))
    putm("onorm", np.tile(f("L1_attn_o_norm_w"), 4))
    putm("Wo", f("L1_attn_Wo"))
    putm("Wg", f("L1_ffn_Wg")); putm("bg", f("L1_ffn_bg")); putm("bias", f("L1_ffn_bias"))
    putm("iota", np.arange(16, dtype=np.float32))
    putm("pick", np.tile(np.eye(16, dtype=np.float32), (3, 1)), slice(0, 48))
    putm("eb1", f("L1_ffn_b1").reshape(32, P).T)
    putm("eb2", f("L1_ffn_b2"), slice(0, 16))
    putm("W1", f("L1_ffn_W1").transpose(1, 0, 2).reshape(P, -1))
    putm("W2", f("L1_ffn_W2").reshape(16, 2, P, P).transpose(2, 0, 1, 3).reshape(P, -1))
    taps = np.zeros((P, P, P + 64), np.float32)
    for r in range(P):
        taps[r, :, r:r + 64] = f("L1_attn_fir_long_w").reshape(P, 64)[:, ::-1]
    return {"MW": M, "taps": taps.reshape(P, -1), "DW": D, "conv": np.ascontiguousarray(np.broadcast_to(conv[None], (P, 4, 3 * P))),
            "Wqkv": np.concatenate([f("L1_attn_Wq"), f("L1_attn_Wk"), f("L1_attn_Wv")], axis=1)}


def kernel(**inputs):
    import numpy as _np
    import concourse.bacc as _bacc
    from concourse import mybir as _mybir
    from concourse.bass_utils import run_bass_kernel_spmd as _run

    nc = _bacc.Bacc("TRN2", target_bir_lowering=False, num_devices=1)
    arrays = _layout(inputs)
    A = {n: nc.dram_tensor("in_" + n, a.shape, _mybir.dt.from_np(a.dtype), kind="ExternalInput").ap()
         for n, a in arrays.items()}
    out = nc.dram_tensor("out_x", (B * S, P), _mybir.dt.float32, kind="ExternalOutput").ap()
    decoder(nc, A, out)
    r = _run(nc, [{"in_" + n: a for n, a in arrays.items()}], core_ids=[0])
    return r.results[0]["out_x"].reshape(B, S, P)
```
